# Optimizing a Trainium2 kernel written in Bass

```python
import numpy as np
import jax
import jax.numpy as jnp

def _softmax(x, axis=-1):
    return jax.nn.softmax(x, axis=axis)

def _gelu(x):
    return jax.nn.gelu(x, approximate=True)

def _silu(x):
    return jax.nn.silu(x)

def _sigmoid(x):
    return jax.nn.sigmoid(x)

def _layernorm(x, axis=-1, eps=1e-05):
    m = jnp.mean(x, axis=axis, keepdims=True)
    v = jnp.var(x, axis=axis, keepdims=True)
    return (x - m) / jnp.sqrt(v + eps)

def _scatter_add(tgt, idx, src, axis=0):
    return tgt.at[idx].add(src)

def _segment_sum(src, seg, n):
    return jax.ops.segment_sum(src, seg, n)
kernel_name = 'mk_decoder_postln_d2_seqx_r8_120697'

def setup_inputs(seed: int=0):
    np.random.seed(seed)
    _w = jnp.asarray

    def _rec_inputs():
        import jax
        import jax.numpy as jnp
        _rk = jax.random.key(seed)
        x = -0.0002928 + 1 * jax.random.normal(jax.random.fold_in(_rk, 1), (32, 128, 128), jnp.float32)
        _lenS = 128 - jax.random.randint(jax.random.fold_in(_rk, 7), (32,), 0, max(1, 128 // 4) + 1, jnp.int32)
        _lenS2 = 77 - jax.random.randint(jax.random.fold_in(_rk, 8), (32,), 0, max(1, 77 // 4) + 1, jnp.int32)
        _ctx_1024P = jax.random.normal(jax.random.fold_in(_rk, 11), (32, 16, 128), jnp.float32)
        _ctx_1024c = jax.random.dirichlet(jax.random.fold_in(_rk, 511), 0.3 * jnp.ones((16,), jnp.float32), (32, 77))
        _ctx_1024t = jnp.einsum('bsk,bkd->bsd', _ctx_1024c, _ctx_1024P)
        _ctx_1024t = _ctx_1024t * jax.lax.rsqrt(jnp.mean(jnp.square(_ctx_1024t)) + 1e-12) * 0.953939
        ctx_1024 = -1.39393e-06 + 0.999914 * (_ctx_1024t + 0.3 * jax.random.normal(jax.random.fold_in(_rk, 611), (32, 77, 128), jnp.float32))
        _validS = jnp.arange(128)[None, :] < _lenS[:, None]
        _validS2 = jnp.arange(77)[None, :] < _lenS2[:, None]
        _causal = jnp.tril(jnp.ones((128, 128), dtype=bool))
        mask_Bx1xSxS2_ff1 = jnp.where(jnp.ones((32, 1, 128, 77), dtype=bool), 1.0, 0.0).astype(jnp.float32)
        return (x, ctx_1024, mask_Bx1xSxS2_ff1)
    x, ctx_1024, mask_Bx1xSxS2_ff1 = _rec_inputs()

    def _L0_attn_setup():
        import math
        import jax, jax.numpy as jnp
        import numpy as np
        N_HEADS = 8
        EPS = 1e-05
        key = jax.random.key(seed)
        ks = jax.random.split(key, 5)
        B, L, D = (4, 256, 128)
        w_scale = 0.02
        return {'x': jax.random.normal(ks[0], (B, L, D), dtype=jnp.float32), 'Wq': jax.random.normal(ks[1], (D, D), dtype=jnp.float32) * w_scale, 'Wk': jax.random.normal(ks[2], (D, D), dtype=jnp.float32) * w_scale, 'Wv': jax.random.normal(ks[3], (D, D), dtype=jnp.float32) * w_scale, 'Wo': jax.random.normal(ks[4], (D, D), dtype=jnp.float32) * w_scale, 'gn_weight': jnp.ones((D,), dtype=jnp.float32), 'gn_bias': jnp.zeros((D,), dtype=jnp.float32)}
    _L0_attn_all = _L0_attn_setup()
    _L0_attn_in = {k: v for k, v in _L0_attn_all.items() if k in ('Wq', 'Wk', 'Wv', 'Wo', 'gn_weight', 'gn_bias')}
    del _L0_attn_all

    def _L0_xattn_setup():
        import jax, jax.numpy as jnp
        import numpy as np
        MODEL_SIZE = 128
        H = 16
        KEY_SIZE = MODEL_SIZE // H
        B, LQ, LK = (2, 256, 256)
        NEG_INF = -1000000000.0
        key = jax.random.key(seed)
        ks = jax.random.split(key, 10)
        s = 0.02
        return {'decoder_output': jax.random.normal(ks[0], (B, LQ, MODEL_SIZE), dtype=jnp.float32), 'encoder_output': jax.random.normal(ks[1], (B, LK, MODEL_SIZE), dtype=jnp.float32), 'mask': jnp.ones((B, 1, LQ, LK), dtype=jnp.float32), 'wq_w': jax.random.normal(ks[2], (MODEL_SIZE, MODEL_SIZE), dtype=jnp.float32) * s, 'wq_b': jnp.zeros((MODEL_SIZE,), dtype=jnp.float32), 'wk_w': jax.random.normal(ks[3], (MODEL_SIZE, MODEL_SIZE), dtype=jnp.float32) * s, 'wk_b': jnp.zeros((MODEL_SIZE,), dtype=jnp.float32), 'wv_w': jax.random.normal(ks[4], (MODEL_SIZE, MODEL_SIZE), dtype=jnp.float32) * s, 'wv_b': jnp.zeros((MODEL_SIZE,), dtype=jnp.float32), 'wo_w': jax.random.normal(ks[5], (MODEL_SIZE, MODEL_SIZE), dtype=jnp.float32) * s, 'wo_b': jnp.zeros((MODEL_SIZE,), dtype=jnp.float32)}
    _L0_xattn_all = _L0_xattn_setup()
    _L0_xattn_in = {k: v for k, v in _L0_xattn_all.items() if k in ('wq_w', 'wq_b', 'wk_w', 'wk_b', 'wv_w', 'wv_b', 'wo_w', 'wo_b')}
    del _L0_xattn_all

    def _L0_ffn_setup():
        import jax, jax.numpy as jnp
        import numpy as np
        HIDDEN = 128
        INTER = 512
        NUM_EXPERTS = 8
        TOP_K = 2
        EPS = 1e-05

        def _layer_norm(x, g, b):
            m = jnp.mean(x, axis=-1, keepdims=True)
            v = jnp.mean(jnp.square(x - m), axis=-1, keepdims=True)
            return (x - m) * jax.lax.rsqrt(v + EPS) * g + b
        key = jax.random.key(seed)
        ks = jax.random.split(key, 8)
        s = 0.02
        return {'x': jax.random.normal(ks[0], (4, 256, HIDDEN), dtype=jnp.float32), 'ln1_g': jnp.ones((HIDDEN,), jnp.float32), 'ln1_b': jnp.zeros((HIDDEN,), jnp.float32), 'attn_w': jax.random.normal(ks[1], (HIDDEN, HIDDEN), jnp.float32) * s, 'ln2_g': jnp.ones((HIDDEN,), jnp.float32), 'ln2_b': jnp.zeros((HIDDEN,), jnp.float32), 'gate_w': jax.random.normal(ks[2], (NUM_EXPERTS, HIDDEN), jnp.float32) * s, 'gate_proj': jax.random.normal(ks[3], (NUM_EXPERTS, INTER, HIDDEN), jnp.float32) * s, 'up_proj': jax.random.normal(ks[4], (NUM_EXPERTS, INTER, HIDDEN), jnp.float32) * s, 'down_proj': jax.random.normal(ks[5], (NUM_EXPERTS, HIDDEN, INTER), jnp.float32) * s}
    _L0_ffn_all = _L0_ffn_setup()
    _L0_ffn_in = {k: v for k, v in _L0_ffn_all.items() if k in ('ln1_g', 'ln1_b', 'attn_w', 'ln2_g', 'ln2_b', 'gate_w', 'gate_proj', 'up_proj', 'down_proj')}
    del _L0_ffn_all

    def _L1_attn_setup():
        import jax, jax.numpy as jnp
        import numpy as np
        B, T, D, C = (4, 1024, 128, 64)
        key = jax.random.key(seed)
        k1, k2, k3 = jax.random.split(key, 3)
        out = jax.random.normal(k1, (B, T, D), jnp.float32)
        W_write = jax.random.normal(k2, (D, D), jnp.float32) / np.float32(np.sqrt(D))
        W_read = jax.random.normal(k3, (D, D), jnp.float32) / np.float32(np.sqrt(D))
        decay = jnp.float32(4.6)
        log_alpha = jnp.log(jnp.float32(0.03))
        return {'out': out, 'W_write': W_write, 'W_read': W_read, 'decay': decay, 'log_alpha': log_alpha}
    _L1_attn_all = _L1_attn_setup()
    _L1_attn_in = {k: v for k, v in _L1_attn_all.items() if k in ('W_write', 'W_read', 'decay', 'log_alpha')}
    del _L1_attn_all

    def _L1_xattn_setup():
        import jax, jax.numpy as jnp
        import numpy as np
        import math
        DIM = 128
        H = 16
        HD = DIM // H // 2
        DEPTH = 4
        LAMBDA_INIT = 0.8 - 0.6 * math.exp(-0.3 * DEPTH)
        SCALE = HD ** (-0.5)
        EPS = 1e-05

        def _sdpa(q, k, v):
            scores = jnp.einsum('bhqd,bhkd->bhqk', q * SCALE, k)
            p = jax.nn.softmax(scores, axis=-1)
            return jnp.einsum('bhqk,bhkd->bhqd', p, v)
        key = jax.random.key(seed)
        ks = jax.random.split(key, 12)
        B, Nq, Nk = (2, 256, 256)
        s = DIM ** (-0.5)
        return {'query': jax.random.normal(ks[0], (B, Nq, DIM), jnp.float32), 'key_': jax.random.normal(ks[1], (B, Nk, DIM), jnp.float32), 'value': jax.random.normal(ks[2], (B, Nk, DIM), jnp.float32), 'Wq': jax.random.normal(ks[3], (DIM, DIM), jnp.float32) * s, 'Wk': jax.random.normal(ks[4], (DIM, DIM), jnp.float32) * s, 'Wv': jax.random.normal(ks[5], (DIM, DIM), jnp.float32) * s, 'Wp': jax.random.normal(ks[6], (DIM, DIM), jnp.float32) * s, 'bp': jnp.zeros((DIM,), jnp.float32), 'lq1': jax.random.normal(ks[7], (HD,), jnp.float32) * 0.1, 'lk1': jax.random.normal(ks[8], (HD,), jnp.float32) * 0.1, 'lq2': jax.random.normal(ks[9], (HD,), jnp.float32) * 0.1, 'lk2': jax.random.normal(ks[10], (HD,), jnp.float32) * 0.1, 'subln_w': jnp.ones((2 * HD,), jnp.float32)}
    _L1_xattn_all = _L1_xattn_setup()
    _L1_xattn_in = {k: v for k, v in _L1_xattn_all.items() if k in ('Wq', 'Wk', 'Wv', 'Wp', 'bp', 'lq1', 'lk1', 'lq2', 'lk2', 'subln_w')}
    del _L1_xattn_all

    def _L1_ffn_setup():
        import jax, jax.numpy as jnp
        import numpy as np
        B, T, C, H, E = (4, 256, 128, 256, 8)
        CAPACITY_FACTOR = 1.0
        key = jax.random.key(seed)
        ks = jax.random.split(key, 5)
        scale = 0.02
        return {'x': jax.random.normal(ks[0], (B, T, C), dtype=jnp.float32), 'Wg': jax.random.normal(ks[1], (E, C), dtype=jnp.float32) * scale, 'W1': jax.random.normal(ks[2], (E, H, C), dtype=jnp.float32) * scale, 'W2': jax.random.normal(ks[3], (E, C, H), dtype=jnp.float32) * scale, 'W3': jax.random.normal(ks[4], (E, H, C), dtype=jnp.float32) * scale}
    _L1_ffn_all = _L1_ffn_setup()
    _L1_ffn_in = {k: v for k, v in _L1_ffn_all.items() if k in ('Wg', 'W1', 'W2', 'W3')}
    del _L1_ffn_all
    return {'x': x, 'ctx_1024': ctx_1024, 'mask_Bx1xSxS2_ff1': mask_Bx1xSxS2_ff1, 'L0_attn_Wq': _L0_attn_in['Wq'], 'L0_attn_Wk': _L0_attn_in['Wk'], 'L0_attn_Wv': _L0_attn_in['Wv'], 'L0_attn_Wo': _L0_attn_in['Wo'], 'L0_attn_gn_weight': _L0_attn_in['gn_weight'], 'L0_attn_gn_bias': _L0_attn_in['gn_bias'], 'L0_xattn_wq_w': _L0_xattn_in['wq_w'], 'L0_xattn_wq_b': _L0_xattn_in['wq_b'], 'L0_xattn_wk_w': _L0_xattn_in['wk_w'], 'L0_xattn_wk_b': _L0_xattn_in['wk_b'], 'L0_xattn_wv_w': _L0_xattn_in['wv_w'], 'L0_xattn_wv_b': _L0_xattn_in['wv_b'], 'L0_xattn_wo_w': _L0_xattn_in['wo_w'], 'L0_xattn_wo_b': _L0_xattn_in['wo_b'], 'L0_ffn_ln1_g': _L0_ffn_in['ln1_g'], 'L0_ffn_ln1_b': _L0_ffn_in['ln1_b'], 'L0_ffn_attn_w': _L0_ffn_in['attn_w'], 'L0_ffn_ln2_g': _L0_ffn_in['ln2_g'], 'L0_ffn_ln2_b': _L0_ffn_in['ln2_b'], 'L0_ffn_gate_w': _L0_ffn_in['gate_w'], 'L0_ffn_gate_proj': _L0_ffn_in['gate_proj'], 'L0_ffn_up_proj': _L0_ffn_in['up_proj'], 'L0_ffn_down_proj': _L0_ffn_in['down_proj'], 'L1_attn_W_write': _L1_attn_in['W_write'], 'L1_attn_W_read': _L1_attn_in['W_read'], 'L1_attn_decay': _L1_attn_in['decay'], 'L1_attn_log_alpha': _L1_attn_in['log_alpha'], 'L1_xattn_Wq': _L1_xattn_in['Wq'], 'L1_xattn_Wk': _L1_xattn_in['Wk'], 'L1_xattn_Wv': _L1_xattn_in['Wv'], 'L1_xattn_Wp': _L1_xattn_in['Wp'], 'L1_xattn_bp': _L1_xattn_in['bp'], 'L1_xattn_lq1': _L1_xattn_in['lq1'], 'L1_xattn_lk1': _L1_xattn_in['lk1'], 'L1_xattn_lq2': _L1_xattn_in['lq2'], 'L1_xattn_lk2': _L1_xattn_in['lk2'], 'L1_xattn_subln_w': _L1_xattn_in['subln_w'], 'L1_ffn_Wg': _L1_ffn_in['Wg'], 'L1_ffn_W1': _L1_ffn_in['W1'], 'L1_ffn_W2': _L1_ffn_in['W2'], 'L1_ffn_W3': _L1_ffn_in['W3']}

def reference(x, ctx_1024, mask_Bx1xSxS2_ff1, L0_attn_Wq, L0_attn_Wk, L0_attn_Wv, L0_attn_Wo, L0_attn_gn_weight, L0_attn_gn_bias, L0_xattn_wq_w, L0_xattn_wq_b, L0_xattn_wk_w, L0_xattn_wk_b, L0_xattn_wv_w, L0_xattn_wv_b, L0_xattn_wo_w, L0_xattn_wo_b, L0_ffn_ln1_g, L0_ffn_ln1_b, L0_ffn_attn_w, L0_ffn_ln2_g, L0_ffn_ln2_b, L0_ffn_gate_w, L0_ffn_gate_proj, L0_ffn_up_proj, L0_ffn_down_proj, L1_attn_W_write, L1_attn_W_read, L1_attn_decay, L1_attn_log_alpha, L1_xattn_Wq, L1_xattn_Wk, L1_xattn_Wv, L1_xattn_Wp, L1_xattn_bp, L1_xattn_lq1, L1_xattn_lk1, L1_xattn_lq2, L1_xattn_lk2, L1_xattn_subln_w, L1_ffn_Wg, L1_ffn_W1, L1_ffn_W2, L1_ffn_W3):
    import jax
    import jax.numpy as jnp

    def _L0_attn_ref(x, Wq, Wk, Wv, Wo, gn_weight, gn_bias):
        import math
        import jax, jax.numpy as jnp
        import numpy as np
        N_HEADS = 8
        EPS = 1e-05
        B, L, D = x.shape
        H = N_HEADS
        dh = D // H
        gammas = 1.0 - jnp.exp(jnp.linspace(math.log(1.0 / 32.0), math.log(1.0 / 512.0), H)).astype(x.dtype)

        def proj(W):
            return (x @ W.T).reshape(B, L, H, dh).transpose(1, 0, 2, 3)
        qT, kT, vT = (proj(Wq), proj(Wk), proj(Wv))
        g = gammas[None, :, None, None]

        def step(S, qkv_t):
            q_t, k_t, v_t = qkv_t
            S = g * S + k_t[..., :, None] * v_t[..., None, :]
            y_t = jnp.einsum('bhde,bhd->bhe', S, q_t)
            return (S, y_t)
        S0 = jnp.zeros((B, H, dh, dh), dtype=x.dtype)
        _, ys = jax.lax.scan(step, S0, (qT, kT, vT))
        out = ys.transpose(1, 0, 2, 3)
        mean = out.mean(axis=(1, 3), keepdims=True)
        var = out.var(axis=(1, 3), keepdims=True)
        out = (out - mean) * jax.lax.rsqrt(var + EPS)
        out = out.reshape(B, L, D) * gn_weight + gn_bias
        return out @ Wo.T

    def _L0_xattn_ref(decoder_output, encoder_output, mask, wq_w, wq_b, wk_w, wk_b, wv_w, wv_b, wo_w, wo_b):
        import jax, jax.numpy as jnp
        import numpy as np
        MODEL_SIZE = 128
        H = 16
        KEY_SIZE = MODEL_SIZE // H
        B, LQ, LK = (2, 256, 256)
        NEG_INF = -1000000000.0
        b = decoder_output.shape[0]
        q = decoder_output @ wq_w + wq_b
        k = encoder_output @ wk_w + wk_b
        v = encoder_output @ wv_w + wv_b
        q = q.reshape(b, -1, H, KEY_SIZE).transpose(0, 2, 1, 3)
        k = k.reshape(b, -1, H, KEY_SIZE).transpose(0, 2, 1, 3)
        v = v.reshape(b, -1, H, KEY_SIZE).transpose(0, 2, 1, 3)
        score = jnp.einsum('bhqd,bhkd->bhqk', q, k) / jnp.sqrt(jnp.asarray(KEY_SIZE, dtype=jnp.float32))
        score = score * mask
        score = jnp.where(score == 0, jnp.float32(NEG_INF), score)
        alignment = jax.nn.softmax(score, axis=-1)
        context = jnp.einsum('bhqk,bhkd->bhqd', alignment, v)
        context = context.transpose(0, 2, 1, 3).reshape(b, -1, H * KEY_SIZE)
        heads = context @ wo_w + wo_b
        return heads

    def _L0_ffn_ref(x, ln1_g, ln1_b, attn_w, ln2_g, ln2_b, gate_w, gate_proj, up_proj, down_proj):
        import jax, jax.numpy as jnp
        import numpy as np
        HIDDEN = 128
        INTER = 512
        NUM_EXPERTS = 8
        TOP_K = 2
        EPS = 1e-05

        def _layer_norm(x, g, b):
            m = jnp.mean(x, axis=-1, keepdims=True)
            v = jnp.mean(jnp.square(x - m), axis=-1, keepdims=True)
            return (x - m) * jax.lax.rsqrt(v + EPS) * g + b
        B, S, H = x.shape
        h = x + jnp.einsum('bsh,oh->bso', _layer_norm(x, ln1_g, ln1_b), attn_w)
        t = _layer_norm(h, ln2_g, ln2_b).reshape(-1, H)
        T = t.shape[0]
        logits = jnp.einsum('th,eh->te', t, gate_w)
        top_vals, top_idx = jax.lax.top_k(logits, TOP_K)
        rw = jax.nn.softmax(top_vals, axis=-1)
        comb = jnp.zeros((T, NUM_EXPERTS), dtype=t.dtype)
        comb = comb.at[jnp.arange(T)[:, None], top_idx].add(rw)
        out = jnp.zeros_like(t)
        for e in range(NUM_EXPERTS):
            g = jnp.einsum('th,ih->ti', t, gate_proj[e])
            u = jnp.einsum('th,ih->ti', t, up_proj[e])
            oe = jnp.einsum('ti,hi->th', jax.nn.silu(g) * u, down_proj[e])
            out = out + comb[:, e:e + 1] * oe
        return h + out.reshape(B, S, H)

    def _L1_attn_ref(out, W_write, W_read, decay, log_alpha):
        import jax, jax.numpy as jnp
        import numpy as np
        B, T, D, C = (4, 1024, 128, 64)
        Bd, Td, Dd = out.shape
        nC = Td // C
        out32 = out.astype(jnp.float32)
        gamma = jax.nn.sigmoid(decay)
        log_gamma = jnp.log(gamma)
        v = out32 @ W_write.T
        wk = jnp.pad(out32[:, :-1], ((0, 0), (1, 0), (0, 0)))
        rk = out32
        p = jnp.arange(C)
        diffs = jnp.maximum(p[:, None] - 1 - p[None, :], 0)
        causal = (p[:, None] > p[None, :]).astype(jnp.float32)
        M = jnp.exp(diffs * log_gamma) * causal
        dec_inter = gamma ** p
        gw = gamma ** (C - 1 - p)
        gC = gamma ** C

        def chunk(x):
            return x.reshape(Bd, nC, C, Dd).transpose(1, 0, 2, 3)
        rk_c, wk_c, v_c = (chunk(rk), chunk(wk), chunk(v))

        def body(W, xs):
            r, w, vv = xs
            inter = jnp.einsum('bde,bce->bcd', W, r) * dec_inter[None, :, None]
            S = jnp.einsum('bcd,bed->bce', r, w)
            intra = jnp.einsum('bce,bed->bcd', S * M, vv)
            W_new = gC * W + jnp.einsum('bcd,bce->bde', vv * gw[None, :, None], w)
            return (W_new, inter + intra)
        W0 = jnp.zeros((Bd, Dd, Dd), jnp.float32)
        _, reads = jax.lax.scan(body, W0, (rk_c, wk_c, v_c))
        reads = reads.transpose(1, 0, 2, 3).reshape(Bd, Td, Dd)
        alpha = jnp.exp(log_alpha)
        return out + alpha * (reads @ W_read.T).astype(out.dtype)

    def _L1_xattn_ref(query, key_, value, Wq, Wk, Wv, Wp, bp, lq1, lk1, lq2, lk2, subln_w):
        import jax, jax.numpy as jnp
        import numpy as np
        import math
        DIM = 128
        H = 16
        HD = DIM // H // 2
        DEPTH = 4
        LAMBDA_INIT = 0.8 - 0.6 * math.exp(-0.3 * DEPTH)
        SCALE = HD ** (-0.5)
        EPS = 1e-05

        def _sdpa(q, k, v):
            scores = jnp.einsum('bhqd,bhkd->bhqk', q * SCALE, k)
            p = jax.nn.softmax(scores, axis=-1)
            return jnp.einsum('bhqk,bhkd->bhqd', p, v)
        B, Nq, C = query.shape
        Nk = key_.shape[1]
        q = (query @ Wq.T).reshape(B, Nq, 2 * H, HD).transpose(0, 2, 1, 3)
        k = (key_ @ Wk.T).reshape(B, Nk, 2 * H, HD).transpose(0, 2, 1, 3)
        v = (value @ Wv.T).reshape(B, Nk, H, 2 * HD).transpose(0, 2, 1, 3)
        q1, q2 = (q[:, :H], q[:, H:])
        k1, k2 = (k[:, :H], k[:, H:])
        a1 = _sdpa(q1, k1, v)
        a2 = _sdpa(q2, k2, v)
        lam1 = jnp.exp(jnp.sum(lq1 * lk1))
        lam2 = jnp.exp(jnp.sum(lq2 * lk2))
        lam = lam1 - lam2 + LAMBDA_INIT
        attn = a1 - lam * a2
        attn = attn.transpose(0, 2, 1, 3)
        attn = attn * jax.lax.rsqrt(jnp.mean(attn * attn, axis=-1, keepdims=True) + EPS)
        attn = attn * subln_w
        attn = attn * (1.0 - LAMBDA_INIT)
        attn = attn.reshape(B, Nq, C)
        return attn @ Wp.T + bp

    def _L1_ffn_ref(x, Wg, W1, W2, W3):
        import jax, jax.numpy as jnp
        import numpy as np
        B, T, C, H, E = (4, 256, 128, 256, 8)
        CAPACITY_FACTOR = 1.0
        b, t, c = x.shape
        e = Wg.shape[0]
        n = b * t
        capacity = max(1, int(CAPACITY_FACTOR * n / e))
        x_flat = x.reshape(n, c)
        scores = (x_flat @ Wg.T).T
        top_vals, token_idx = jax.lax.top_k(scores, capacity)
        token_w = jax.nn.softmax(top_vals, axis=-1)
        xg = x_flat[token_idx]
        h = jax.nn.silu(jnp.einsum('eic,ehc->eih', xg, W1)) * jnp.einsum('eic,ehc->eih', xg, W3)
        y = jnp.einsum('eih,ech->eic', h, W2) * token_w[..., None]
        out = jnp.zeros_like(x_flat).at[token_idx.reshape(-1)].add(y.reshape(-1, c))
        return out.reshape(b, t, c)
    x = _layernorm(x + _L0_attn_ref(x, L0_attn_Wq, L0_attn_Wk, L0_attn_Wv, L0_attn_Wo, L0_attn_gn_weight, L0_attn_gn_bias), axis=-1)
    x = _layernorm(x + _L0_xattn_ref(x, ctx_1024, mask_Bx1xSxS2_ff1, L0_xattn_wq_w, L0_xattn_wq_b, L0_xattn_wk_w, L0_xattn_wk_b, L0_xattn_wv_w, L0_xattn_wv_b, L0_xattn_wo_w, L0_xattn_wo_b), axis=-1)
    x = _layernorm(x + _L0_ffn_ref(x, L0_ffn_ln1_g, L0_ffn_ln1_b, L0_ffn_attn_w, L0_ffn_ln2_g, L0_ffn_ln2_b, L0_ffn_gate_w, L0_ffn_gate_proj, L0_ffn_up_proj, L0_ffn_down_proj), axis=-1)
    x = _layernorm(x + _L1_attn_ref(x, L1_attn_W_write, L1_attn_W_read, L1_attn_decay, L1_attn_log_alpha), axis=-1)
    x = _layernorm(x + _L1_xattn_ref(x, ctx_1024, ctx_1024, L1_xattn_Wq, L1_xattn_Wk, L1_xattn_Wv, L1_xattn_Wp, L1_xattn_bp, L1_xattn_lq1, L1_xattn_lk1, L1_xattn_lq2, L1_xattn_lk2, L1_xattn_subln_w), axis=-1)
    x = _layernorm(x + _L1_ffn_ref(x, L1_ffn_Wg, L1_ffn_W1, L1_ffn_W2, L1_ffn_W3), axis=-1)
    return x

_drawn_inputs = setup_inputs


def setup_inputs(seed=0):
    import zlib

    import numpy as np

    out = dict(_drawn_inputs(seed))
    spreads = {'L0_attn_gn_weight': (1.0, 0.2),
     'L0_attn_gn_bias': (0.0, 0.1),
     'L0_xattn_wq_b': (0.0, 0.8),
     'L0_xattn_wk_b': (0.0, 0.8),
     'L0_xattn_wv_b': (0.0, 0.1),
     'L0_xattn_wo_b': (0.0, 0.1),
     'L0_ffn_ln1_g': (1.0, 0.2),
     'L0_ffn_ln1_b': (0.0, 0.393),
     'L0_ffn_ln2_g': (1.0, 0.6),
     'L0_ffn_ln2_b': (0.0, 0.8),
     'L1_xattn_bp': (0.0, 0.1),
     'L1_xattn_subln_w': (1.0, 0.2)}
    factors = {'L0_xattn_wq_w': 8.0,
     'L0_xattn_wk_w': 8.0,
     'L0_ffn_gate_w': 8.0,
     'L0_ffn_gate_proj': 8.0,
     'L0_ffn_up_proj': 8.0,
     'L0_ffn_down_proj': 8.0,
     'L1_xattn_lq1': 3.677,
     'L1_xattn_lk1': 3.677,
     'L1_xattn_lq2': 8.0,
     'L1_xattn_lk2': 8.0,
     'L1_ffn_Wg': 22.808,
     'L1_ffn_W1': 24.969,
     'L1_ffn_W2': 22.349,
     'L1_ffn_W3': 23.319}
    for name, (base, spread) in spreads.items():
        noise = np.random.default_rng([zlib.crc32(name.encode()), seed]).standard_normal(out[name].shape)
        drawn = base * np.exp(spread * noise) if base else spread * noise
        out[name] = jnp.asarray(drawn.astype(out[name].dtype))
    for name, factor in factors.items():
        out[name] = (out[name] * factor).astype(out[name].dtype)
    return out
```

```python
import math
from contextlib import ExitStack

import concourse.bass as bass
import numpy as np
from concourse import mybir

F32 = mybir.dt.float32
ALU = mybir.AluOpType
ACT = mybir.ActivationFunctionType
AX = mybir.AxisListType
RMAX = bass.bass_isa.ReduceOp.max

P = 128
STOP = 6


class Engines:

    ORDER = ("sync", "tensor", "vector", "scalar", "gpsimd")

    def __init__(self, nc, ctx):
        self.nc, self.ctx = nc, ctx
        self.queue = {e: [] for e in self.ORDER}
        self.progress, self.count, self.last = {}, {}, {}

    def sem(self, name):
        return self.ctx.enter_context(self.nc.semaphore(name))

    def stage(self, name):
        for e in self.ORDER[1:]:
            self.progress[e] = self.sem(f"{name}_{e}_done")
            self.count[e] = 0

    def do(self, engine, what, *waits, tell=True):
        step = [[w for w in waits if w is not None], what, None, 1]
        self.queue[engine].append(step)
        if not tell:
            return None
        self.count[engine] += 1
        step[2] = self.progress[engine]
        token = (self.progress[engine], self.count[engine])
        self.last[engine] = token
        return token

    def dma(self, engine, name, out, in_, *waits, **how):
        s = self.sem(f"{name}_landed")
        self.queue[engine].append([[w for w in waits if w is not None],
                                   lambda e: e.dma_start(out, in_, **how), s, 16])
        return (s, 16)

    def wait(self, engine, *waits):
        self.queue[engine].append([[w for w in waits if w is not None], None, None, 0])

    def join(self):
        ends = dict(self.last)
        for e in self.ORDER:
            self.wait(e, *[t for f, t in ends.items() if f != e])

    def emit(self, block):
        def body(name):
            def run(eng):
                seen = {}
                for waits, what, s, by in self.queue[name]:
                    for ws, value in waits:
                        if seen.get(id(ws), 0) < value:
                            eng.wait_ge(ws, value)
                            seen[id(ws)] = value
                    if what is not None:
                        ins = what(eng)
                        if s is not None:
                            ins.then_inc(s, by)
            return run
        for name in self.ORDER:
            blocks = {"sync": block.sync, "tensor": block.tensor, "vector": block.vector,
                            "scalar": block.scalar, "gpsimd": block.gpsimd}[name]
            blocks(body(name))


def build(nc, D, out):
    NB, S, C = D["x_tok"].shape[1], D["x_T"].shape[2], D["x_T"].shape[0]
    SK = D["ctx_T"].shape[2]
    GB = 4
    NG = NB // GB
    GN = GB * S
    EPS = 1e-5
    NE0, I0 = D["gate_T"].shape[1], D["gate_T"].shape[2]
    NE1, I1 = D["w1_T"].shape[1], D["w1_T"].shape[2]
    CAP = NB * S // NE1
    NEG = 1e9

    with ExitStack() as ctx:
        def sb(name, shape, dt=F32, scope=ctx):
            return scope.enter_context(nc.sbuf_tensor(name, shape, dt))

        E = Engines(nc, ctx)
        do = E.do
        ps = ctx.enter_context(nc.psum_tensor("ps", [P, 8, 512], F32))

        x_tok = sb("x_tok_sb", [P, NB, C])
        x_Tp = sb("x_T_sb", [P, NB * S + 8])
        x_T = x_Tp[:, 8:].rearrange("p (b t) -> p b t", b=NB)
        ctx_T = sb("ctx_T_sb", [P, NB, SK])
        n_proj = D["proj"].shape[1]
        proj = sb("proj_sb", [P, n_proj, P])
        n_cols = D["cols"].shape[1]
        cols = sb("cols_sb", [P, n_cols])
        rows = sb("rows_sb", [P, 3, P])
        gates = sb("gates_sb", [P, 2, 8])
        lams = sb("lams_sb", [P, 4, D["lams"].shape[2]])
        n_mats = D["mats"].shape[1]
        mats = sb("mats_sb", [P, n_mats, P])
        picks = sb("picks_sb", [P, D["picks"].shape[1]])
        stats = sb("stats", [P, NB, 6])
        mv = sb("mv", [P, NB, 2])
        veps = sb("veps", [P, NB])
        rstd = sb("rstd", [P, NB])
        minus_half = sb("minus_half", [P, P])
        EW = max(2 * NE0 * I0 + NE0 * I0, 2 * NE1 * I1 + NE1 * I1)
        expert_w = sb("expert_w", [P, EW])

        PJ = {n: i for i, n in enumerate(PROJ)}
        CO = {n: i for i, n in enumerate(COLS)}
        W = lambda n: proj[:, PJ[n], :]
        col = lambda n: cols[:, CO[n]:CO[n] + 1]
        ident, headavg, diffs, causal, below, ones = [mats[:, i, :] for i in range(6)]

        E.stage("start")
        l_proj = E.dma("sync", "proj", proj[:, :, :], D["proj"])
        l_xT = [E.dma("sync", f"x_T{h}", x_T[:, h * 16:h * 16 + 16, :], D["x_T"][:, h * 16:h * 16 + 16, :])
                for h in range(2)]
        l_picks = E.dma("sync", "picks", picks[:, :], D["picks"])
        l_cols = E.dma("sync", "cols", cols[:, :], D["cols"])
        l_mats = E.dma("sync", "mats", mats[:, :, :], D["mats"])
        a_scope = ExitStack()
        decay_T = sb("decay_T", [P, 8, S], scope=a_scope)
        l_decay = E.dma("sync", "decay", decay_T[:, :, :], D["decay"])
        l_xtok = E.dma("sync", "x_tok", x_tok[:, :, :], D["x_tok"])
        l_ctx = E.dma("sync", "ctx_T", ctx_T[:, :, :], D["ctx_T"])
        l_rows = E.dma("sync", "rows", rows[:, :, :], D["rows"])
        l_gates = E.dma("sync", "gates", gates[:, :, :], D["gates"])
        l_lams = E.dma("sync", "lams", lams[:, :, :], D["lams"])
        n0 = NE0 * I0
        gate_T = expert_w[:, 0:n0].rearrange("p (e i) -> p e i", e=NE0)
        up_T = expert_w[:, n0:2 * n0].rearrange("p (e i) -> p e i", e=NE0)
        down_T = expert_w[:, 2 * n0:3 * n0].rearrange("p (e k c) -> p e k c", e=NE0, c=C)
        l_moe0 = [E.dma("sync", "gate_T", gate_T, D["gate_T"]), E.dma("sync", "up_T", up_T, D["up_T"]),
                  E.dma("sync", "down_T", down_T, D["down_T"])]
        t_half = do("gpsimd", lambda e: e.memset(minus_half[:, :], -0.5))
        t_pad = do("gpsimd", lambda e: e.memset(x_Tp[:, 0:8], 0.0))

        def group(G):
            return slice(G * GB, (G + 1) * GB)

        def layer_stats(G, ready):
            t = ready
            for b in range(G * GB, (G + 1) * GB):
                t = do("vector", lambda e, b=b: e.bn_stats(stats[:, b, :], x_tok[:, b, :]), ready)
            for b in range(G * GB, (G + 1) * GB):
                t2 = do("vector", lambda e, b=b: e.bn_aggr(mv[:, b, :], stats[:, b, :]), t)
            g = group(G)
            t3 = do("gpsimd", lambda e: e.tensor_scalar(veps[:, g], mv[:, g, 1], EPS, None, ALU.add), t2)
            return do("gpsimd", lambda e: e.tensor_tensor(rstd[:, g], veps[:, g], minus_half[:, 0:GB], ALU.pow),
                      t3, t_half)

        def residual(G, summand, ready, times=1.0):
            g = group(G)
            t = do("vector", lambda e: e.scalar_tensor_tensor(x_tok[:, g, :], x_tok[:, g, :], times, summand,
                                                              ALU.mult, ALU.add), ready, l_xtok)
            return t, layer_stats(G, t)

        def normalize(G, ready, dst=None, *waits):
            dst = x_tok if dst is None else dst
            for i, b in enumerate(range(G * GB, (G + 1) * GB)):
                o = dst[:, b, :] if dst is x_tok else dst[:, i, :]
                t = do("vector", lambda e, b=b, o=o: e.tensor_scalar(
                    o, x_tok[:, b, :], mv[:, b, 0:1], rstd[:, b:b + 1], ALU.subtract, ALU.mult), ready, *waits)
            return t

        def turn(src, bank, *waits):
            for i in range(GB):
                t = do("tensor", lambda e, i=i: e.transpose(ps[:, bank, i * S:(i + 1) * S], src(i), ident),
                       *waits, l_mats, tell=i == GB - 1)
            return t

        def bank4(bank):
            return ps[:, bank, :].rearrange("p (b c) -> p b c", b=GB)

        def renew_xT(G, ready, bank, bank_free):
            t = turn(lambda i: x_tok[:, G * GB + i, :], bank, ready, bank_free)
            return do("scalar", lambda e: e.copy(x_T[:, group(G), :], bank4(bank)), t)

        def output():
            for G in range(NG):
                stores.append(E.dma("sync", f"out{G}", out[:, group(G), :], x_tok[:, group(G), :], x_done[G]))

        stores = []
        x_done = [l_xtok] * NG
        xT_done = [l_xT[G * GB // 16] for G in range(NG)]

        E.stage("retention")
        NH, HD = 8, C // 8
        kT = sb("ret_kT", [P, 2, GN], scope=a_scope)
        qB = sb("ret_qB", [P, 2, 2, GN], scope=a_scope)
        vS = sb("ret_v", [P, 2, GB, C], scope=a_scope)
        aT = sb("ret_aT", [P, 3, 2, 2, S], scope=a_scope)
        yS = sb("ret_y", [P, 2, GB, C], scope=a_scope)
        yT = sb("ret_yT", [P, NB, S], scope=a_scope)
        ystat = sb("ret_ystat", [P, NB, 6], scope=a_scope)
        ymv = sb("ret_ymv", [P, NB, 2], scope=a_scope)
        small = sb("ret_small", [P, 8, NB], scope=a_scope)

        free7 = None
        qkv_ready = [[None] * 3 for _ in range(NG)]
        qk_free = [None, None]
        y_free = [None, None]
        av_done = [None] * (2 * NB + 4)
        group_used = [None] * (NG + 1)
        ys_used = [None, None]

        def ret_project(G, which):
            nonlocal free7
            s = G % 2
            old = group_used[G - 2] if G >= 2 else None
            rhs = x_T[:, group(G), :]
            if which == 0:
                t = do("tensor", lambda e: e.matmul(ps[:, 7, :], W("ret_q"), rhs, start=True, stop=True),
                       free7, l_proj, xT_done[G])
                for j in range(2):
                    free7 = do("scalar", lambda e, j=j: e.activation(
                        qB[:, s, j, :], ps[:, 7, :], ACT.Copy, scale=picks[:, j:j + 1]), t, old, l_picks)
            elif which == 1:
                t = do("tensor", lambda e: e.matmul(ps[:, 7, :], W("ret_k"), rhs, start=True, stop=True), free7)
                free7 = do("scalar", lambda e: e.copy(kT[:, s, :], ps[:, 7, :]), t, old)
            else:
                for i in range(GB):
                    t = do("tensor", lambda e, i=i: e.matmul(ps[:, 7, i * S:(i + 1) * S], x_T[:, G * GB + i, :],
                                                             W("ret_v"), start=True, stop=True),
                           free7, tell=i == GB - 1)
                free7 = do("scalar", lambda e: e.copy(vS[:, s, :, :], bank4(7)), t, old)
            qkv_ready[G][which] = free7

        def ret_scores(u):
            b, h = divmod(u, 2)
            G, i = divmod(b, GB)
            s = G % 2
            for q in range(2):
                g = 2 * h + q
                t = do("tensor", lambda e, g=g: e.matmul(
                    ps[:, g, 0:2 * S].rearrange("p (j t) -> p j t", j=2),
                    kT[32 * g:32 * g + 32, s, i * S:(i + 1) * S],
                    qB[32 * g:32 * g + 32, s, :, i * S:(i + 1) * S], start=True, stop=True),
                    qk_free[h], *qkv_ready[G], tell=q == 1)
            a = aT[:, u % 3, :, :, :].rearrange("p g j t -> p g (j t)")
            m = decay_T[:, 4 * h:4 * h + 4, :].rearrange("p (g j) t -> p g (j t)", g=2)
            qk_free[h] = masked[u] = do("vector", lambda e: e.tensor_tensor(
                a, ps[:, 2 * h:2 * h + 2, 0:2 * S], m, ALU.mult), t, l_decay, av_done[u - 3] if u >= 3 else None)

        def ret_values(u):
            b, h = divmod(u, 2)
            G, i = divmod(b, GB)
            bank = 4 + G % 2
            for n in range(4):
                c = i * C + (4 * h + n) * HD
                t = do("tensor", lambda e, n=n, c=c: e.matmul(
                    ps[:, bank, c:c + HD], aT[:, u % 3, n // 2, n % 2, :],
                    vS[:, G % 2, i, (4 * h + n) * HD:(4 * h + n + 1) * HD], start=True, stop=True),
                    masked[u], y_free[G % 2], tell=n == 3)
            av_done[u] = t
            if u % 8 == 7:
                group_used[G] = t
                y_free[G % 2] = y_copied[G] = do("scalar", lambda e: e.copy(yS[:, G % 2, :, :], bank4(bank)),
                                                 t, ys_used[G % 2])

        masked = [None] * (2 * NB)
        y_copied = [None] * NG

        def ret_turn(G):
            nonlocal free7
            t = turn(lambda i: yS[:, G % 2, i, :], 7, y_copied[G], free7)
            ys_used[G % 2] = t
            free7 = t2 = do("scalar", lambda e: e.copy(yT[:, group(G), :], bank4(7)), t)
            for b in range(G * GB, (G + 1) * GB):
                t3 = do("vector", lambda e, b=b: e.bn_stats(ystat[:, b, :], yT[:, b, :]), t2)
            return t3

        for w in range(3):
            ret_project(0, w)
        n_u = 2 * NB
        for u in range(n_u + 2):
            if u < n_u:
                ret_scores(u)
            if u % 8 in (1, 2, 3) and u // 8 + 1 < NG:
                ret_project(u // 8 + 1, u % 8 - 1)
            if u >= 1 and u - 1 < n_u:
                ret_values(u - 1)
            if u % 8 == 4 and u >= 8:
                ret_turn(u // 8 - 1)
        t = ret_turn(NG - 1)
        for b in range(NB):
            t2 = do("vector", lambda e, b=b: e.bn_aggr(ymv[:, b, :], ystat[:, b, :]), t)
        mean_h, delta, dvar, v_h, y_scale, y_bias, tmp = [small[:, i, :] for i in range(7)]
        t3 = do("tensor", lambda e: e.matmul(ps[:, 6, 0:NB], headavg, ymv[:, :, 0], start=True, stop=True), t2)
        t4 = do("vector", lambda e: e.tensor_copy(mean_h, ps[:, 6, 0:NB]), t3)
        t5 = do("vector", lambda e: e.tensor_tensor(delta, ymv[:, :, 0], mean_h, ALU.subtract), t4)
        t6 = do("vector", lambda e: e.tensor_tensor(dvar, delta, delta, ALU.mult), t5)
        t7 = do("vector", lambda e: e.tensor_tensor(dvar, dvar, ymv[:, :, 1], ALU.add), t6)
        t8 = do("tensor", lambda e: e.matmul(ps[:, 6, 0:NB], headavg, dvar, start=True, stop=True), t7)
        t9 = do("vector", lambda e: e.tensor_scalar(v_h, ps[:, 6, 0:NB], EPS, None, ALU.add), t8)
        t10 = do("gpsimd", lambda e: e.tensor_tensor(tmp, v_h, minus_half[:, 0:NB], ALU.pow), t9, t_half)
        t11 = do("vector", lambda e: e.tensor_scalar(y_scale, tmp, col("gn_w"), None, ALU.mult), t10, l_cols)
        t12 = do("vector", lambda e: e.tensor_tensor(delta, mean_h, y_scale, ALU.mult), t11)
        t13 = do("vector", lambda e: e.tensor_scalar(y_bias, delta, -1.0, col("gn_b"), ALU.mult, ALU.add), t12)
        bank_free = [None] * 8
        pend = [None] * NG
        for G in range(NG + 2):
            if G < NG:
                for b in range(G * GB, (G + 1) * GB):
                    t = do("scalar", lambda e, b=b: e.activation(
                        yT[:, b, :], yT[:, b, :], ACT.Identity, scale=y_scale[:, b:b + 1],
                        bias=y_bias[:, b:b + 1]), t13)
                bank = G % 3
                for i in range(GB):
                    t2 = do("tensor", lambda e, i=i, G=G, bank=bank: e.matmul(
                        ps[:, bank, i * S:(i + 1) * S], yT[:, G * GB + i, :], W("ret_o"), start=True, stop=True),
                        t, bank_free[bank], tell=i == GB - 1)
                bank_free[bank], pend[G] = residual(G, bank4(bank), t2)
            if G >= 1 and G - 1 < NG:
                g = G - 1
                x_done[g] = normalize(g, pend[g])
                xT_done[g] = bank_free[4 + g % 2] = renew_xT(g, x_done[g], 4 + g % 2, bank_free[4 + g % 2])
        E.join()
        a_scope.close()

        def cross_attention(name, differential):
            scope = ExitStack()
            E.stage(name)
            do = E.do
            NU = 4 if differential else 2
            NK = 8 if differential else 4
            UH = 8
            VD = 8
            qT = sb(name + "_qT", [P, 2, GN], scope=scope)
            kB = sb(name + "_kB", [P, 2, NK, GB, SK], scope=scope)
            vX = sb(name + "_vX", [SK, 2, GB, 16, VD + 1], scope=scope)
            tS = sb(name + "_t", [P, 2, UH, SK], scope=scope)
            rS = sb(name + "_r", [P, 3, UH, SK], scope=scope)
            mS = sb(name + "_m", [P, 3, UH], scope=scope)
            dS = sb(name + "_d", [P, 3, UH, SK], scope=scope)
            pS = sb(name + "_p", [P, 3, UH, SK], scope=scope)
            pT = sb(name + "_pT", [SK, 2, UH, S], scope=scope)
            NA = 2 if differential else 1
            rec = sb(name + "_rec", [P, NA * 16], scope=scope)
            cS = sb(name + "_c", [P, 2, NA, GB, 16, VD], scope=scope)
            cT = sb(name + "_cT", [P, 2, GN], scope=scope)
            if differential:
                sq = sb(name + "_sq", [P, 2, GB * 16, VD], scope=scope)
                ms = sb(name + "_ms", [P, 2, 3, GB * 16], scope=scope)
            else:
                mask = sb(name + "_mask", [P, NB, SK], scope=scope)
                l_mask = E.dma("sync", "mask", mask[:, :, :], D["mask"])
            t_ones = do("gpsimd", lambda e: e.memset(vX[:, :, :, :, VD:VD + 1], 1.0))

            free7 = None
            ready = [[None] * 3 for _ in range(NG)]
            qk_free = [None, None]
            pt_free = None
            av_free = None
            qk_last = [None] * NG
            av_last = [None] * NG
            n_u = NU * NB
            soft, exp_done, turned, pt_ready, av_done, d_done = [[None] * n_u for _ in range(6)]
            c_ready = [None] * NG
            c_used = [None, None]
            cT_used = [None, None]
            pend = [None] * NG
            rms_tok = [None] * NG

            def project(G, which):
                nonlocal free7
                s = G % 2
                if which == 0:
                    t = do("tensor", lambda e: e.matmul(ps[:, 7, :], W(name + "_q"), x_T[:, group(G), :],
                                                        start=True, stop=True), free7)
                    old = qk_last[G - 2] if G >= 2 else None
                    if differential:
                        free7 = do("scalar", lambda e: e.mul(qT[:, s, :], ps[:, 7, :], 0.5), t, old)
                    else:
                        free7 = do("vector", lambda e: e.tensor_scalar(
                            qT[:, s, :], ps[:, 7, :], col("xq_b"), 1.0 / (NEG * math.sqrt(8.0)),
                            ALU.add, ALU.mult), t, old)
                elif which == 1:
                    kin = ctx_T[:, group(G), :]
                    kp = ps[:, 7, 0:GB * SK]
                    t = do("tensor", lambda e: e.matmul(kp, W(name + "_k"), kin, start=True, stop=True),
                           free7, l_ctx)
                    old = qk_last[G - 2] if G >= 2 else None
                    for j in range(NK):
                        dst = kB[:, s, j, :, :]
                        src = kp.rearrange("p (b k) -> p b k", b=GB)
                        if differential:
                            pick = picks[:, 6 + j:7 + j]
                            free7 = do("scalar", lambda e, dst=dst, pick=pick: e.activation(
                                dst, src, ACT.Copy, scale=pick), t, old)
                        else:
                            pick = picks[:, 2 + j:3 + j]
                            free7 = do("vector", lambda e, dst=dst, pick=pick: e.tensor_scalar(
                                dst, src, col("xk_b"), pick, ALU.add, ALU.mult), t, old)
                else:
                    for i in range(GB):
                        t = do("tensor", lambda e, i=i: e.matmul(
                            ps[0:SK, 7, i * C:(i + 1) * C], ctx_T[:, G * GB + i, :], W(name + "_v"),
                            start=True, stop=True), free7, l_ctx, tell=i == GB - 1)
                    old = av_last[G - 2] if G >= 2 else None
                    dst = vX[:, s, :, :, 0:VD].rearrange("p b h d -> p (b h) d")
                    src = ps[0:SK, 7, :].rearrange("p (b h d) -> p (b h) d", b=GB, d=VD)
                    if differential:
                        free7 = do("scalar", lambda e: e.copy(dst, src), t, old, t_ones)
                    else:
                        bias = rows[0:SK, 0:1, :].broadcast_to([SK, GB, C])
                        free7 = do("vector", lambda e: e.tensor_tensor(
                            vX[:, s, :, :, 0:VD].rearrange("p b h d -> p b h d"),
                            ps[0:SK, 7, :].rearrange("p (b h d) -> p b h d", b=GB, d=VD),
                            bias.rearrange("p b (h d) -> p b h d", d=VD), ALU.add), t, old, t_ones, l_rows)
                ready[G][which] = free7

            def scores(u):
                b, r = divmod(u, NU)
                G, i = divmod(b, GB)
                half, att = r % 2, r // 2
                s = G % 2
                for q in range(2):
                    g = 2 * half + q
                    t = do("tensor", lambda e, g=g: e.matmul(
                        ps[:, g, 0:4 * SK].rearrange("p (j k) -> p j k", j=4),
                        qT[32 * g:32 * g + 32, s, i * S:(i + 1) * S],
                        kB[32 * g:32 * g + 32, s, 4 * att:4 * att + 4, i, :], start=True, stop=True),
                        qk_free[half], *ready[G], tell=q == 1)
                if r == NU - 1 and i == GB - 1:
                    qk_last[G] = t
                sc = ps[:, 2 * half:2 * half + 2, 0:4 * SK].rearrange("p g (j k) -> p g j k", j=4)
                v3 = u % 3
                if differential:
                    t2 = do("vector", lambda e: e.tensor_reduce(mS[:, v3, :], sc, AX.X, ALU.max), t,
                            soft[u - 3] if u >= 3 else None)
                    m = mS[:, v3, :].rearrange("p (g j k) -> p g j k", g=2, k=1).broadcast_to([P, 2, 4, SK])
                    soft[u] = qk_free[half] = do("vector", lambda e: e.tensor_tensor(
                        dS[:, v3, :, :].rearrange("p (g j) k -> p g j k", g=2), sc, m, ALU.subtract),
                        t2, exp_done[u - 3] if u >= 3 else None)
                else:
                    mk = mask[:, b:b + 1, :].unsqueeze(1).broadcast_to([P, 2, 4, SK])
                    qk_free[half] = t2 = do("vector", lambda e: e.tensor_tensor(
                        tS[:, u % 2, :, :].rearrange("p (g j) k -> p g j k", g=2), sc, mk, ALU.mult), t, l_mask)
                    flat = tS[:, u % 2, :, :].rearrange("p h k -> p (h k)")
                    t3 = do("vector", lambda e: e.scalar_tensor_tensor(
                        rS[:, v3, :, :].rearrange("p h k -> p (h k)"), flat, 0.0, flat,
                        ALU.is_equal, ALU.subtract), t2, soft[u - 3] if u >= 3 else None)
                    t4 = do("vector", lambda e: e.tensor_reduce(mS[:, v3, :], rS[:, v3, :, :], AX.X, ALU.min), t3)
                    m = mS[:, v3, :].unsqueeze(2).broadcast_to([P, UH, SK])
                    soft[u] = do("gpsimd", lambda e: e.tensor_tensor(dS[:, v3, :, :], rS[:, v3, :, :], m,
                                                                     ALU.subtract),
                                 t4, exp_done[u - 3] if u >= 3 else None)

            def exponentials(u):
                exp_done[u] = do("scalar", lambda e: e.activation(
                    pS[:, u % 3, :, :], dS[:, u % 3, :, :], ACT.Exp, scale=1.0 if differential else -NEG),
                    soft[u], turned[u - 3] if u >= 3 else None)

            def turn_p(u):
                nonlocal pt_free
                for h in range(UH):
                    t = do("tensor", lambda e, h=h: e.transpose(
                        ps[0:SK, 4 + h // 4, (h % 4) * S:(h % 4 + 1) * S], pS[:, u % 3, h, :], ident),
                        exp_done[u], pt_free, tell=h == UH - 1)
                turned[u] = t
                pt_free = pt_ready[u] = do("scalar", lambda e: e.copy(
                    pT[:, u % 2, :, :].rearrange("p (g h) q -> p g (h q)", g=2), ps[0:SK, 4:6, :]),
                    t, av_done[u - 2] if u >= 2 else None)

            def values(u):
                nonlocal av_free
                b, r = divmod(u, NU)
                G, i = divmod(b, GB)
                half, att = r % 2, r // 2
                for n in range(UH):
                    h = 8 * half + n
                    c = (att * 16 + h) * (VD + 1)
                    t = do("tensor", lambda e, n=n, h=h, c=c: e.matmul(
                        ps[:, 6, c:c + VD + 1], pT[:, u % 2, n, :], vX[:, G % 2, i, h, :], start=True, stop=True),
                        pt_ready[u], av_free, tell=n == UH - 1)
                av_done[u] = t
                if r < NU - 1:
                    return
                if i == GB - 1:
                    av_last[G] = t
                o = ps[:, 6, 0:NA * 16 * (VD + 1)].rearrange("p (a h d) -> p a h d", a=NA, d=VD + 1)
                t1 = do("vector", lambda e: e.reciprocal(
                    rec[:, :].rearrange("p (a h) -> p a h", a=NA), o[:, :, :, VD]), t, c_ready[G - 1] if G else None)
                rb = rec[:, :].rearrange("p (a h d) -> p a h d", a=NA, d=1).broadcast_to([P, NA, 16, VD])
                av_free = t2 = do("vector", lambda e: e.tensor_tensor(
                    cS[:, G % 2, :, i, :, :], o[:, :, :, 0:VD], rb, ALU.mult), t1, c_used[G % 2])
                c_ready[G] = t2
                if i == GB - 1 and differential:
                    rms(G)

            def rms(G):
                s = G % 2
                a1 = cS[:, s, 0, :, :, :].rearrange("p b h d -> p (b h d)")
                a2 = cS[:, s, 1, :, :, :].rearrange("p b h d -> p (b h d)")
                t = do("vector", lambda e: e.scalar_tensor_tensor(a1, a2, neg_lam[:, 0:1], a1,
                                                                  ALU.mult, ALU.add), c_ready[G], t_lam)
                t2 = do("vector", lambda e: e.tensor_tensor(
                    sq[:, s, :, :].rearrange("p h d -> p (h d)"), a1, a1, ALU.mult), t)
                t3 = do("vector", lambda e: e.tensor_reduce(ms[:, s, 0, :], sq[:, s, :, :], AX.X, ALU.add), t2)
                t4 = do("vector", lambda e: e.tensor_scalar(ms[:, s, 1, :], ms[:, s, 0, :], 1.0 / VD, EPS,
                                                            ALU.mult, ALU.add), t3)
                rms_tok[G] = do("gpsimd", lambda e: e.tensor_tensor(ms[:, s, 2, :], ms[:, s, 1, :],
                                                                    minus_half[:, 0:GB * 16], ALU.pow), t4)

            def scale_rms(G):
                s = G % 2
                a1 = cS[:, s, 0, :, :, :].rearrange("p b h d -> p (b h) d")
                rb = ms[:, s, 2, :].unsqueeze(2).broadcast_to([P, GB * 16, VD])
                c_ready[G] = do("vector", lambda e: e.tensor_tensor(a1, a1, rb, ALU.mult), rms_tok[G])

            def context_turn(G):
                nonlocal free7
                if differential:
                    scale_rms(G)
                s = G % 2
                src = cS[:, s, 0, :, :, :].rearrange("p b h d -> p b (h d)")
                t = turn(lambda i: src[:, i, :], 7, c_ready[G], free7)
                c_used[s] = t
                if differential:
                    free7 = do("scalar", lambda e: e.activation(cT[:, s, :], ps[:, 7, :], ACT.Copy,
                                                                scale=sub_w[:, 0:1]), t, t_sub, cT_used[s])
                else:
                    free7 = do("scalar", lambda e: e.copy(cT[:, s, :], ps[:, 7, :]), t, cT_used[s])
                return free7

            def context_out(G, ready):
                nonlocal free7
                s = G % 2
                for i in range(GB):
                    t = do("tensor", lambda e, i=i: e.matmul(
                        ps[:, 7, i * C:(i + 1) * C], cT[:, s, i * S:(i + 1) * S], W(name + "_o"),
                        start=True, stop=True), ready, free7, tell=i == GB - 1)
                cT_used[s] = t
                b = rows[:, (2 if differential else 1):(3 if differential else 2), :].broadcast_to([P, GB, C])
                g = group(G)
                t2 = do("gpsimd", lambda e: e.tensor_tensor(x_tok[:, g, :], x_tok[:, g, :], b, ALU.add),
                        x_done[G], l_rows)
                E.wait("vector", t2)
                free7, pend[G] = residual(G, bank4(7), t)

            def finish(G):
                nonlocal free7
                x_done[G] = normalize(G, pend[G])
                free7 = xT_done[G] = renew_xT(G, x_done[G], 7, free7)

            if differential:
                lam_init = 0.8 - 0.6 * math.exp(-0.3 * 4)
                lw = sb(name + "_lw", [P, 12], scope=scope)
                neg_lam = sb(name + "_neg_lam", [P, 1], scope=scope)
                sub_w = sb(name + "_sub_w", [P, 1], scope=scope)
                for a in range(2):
                    ta = do("vector", lambda e, a=a: e.tensor_tensor(
                        lw[:, 4 * a:4 * a + 4], lams[:, 2 * a, :], lams[:, 2 * a + 1, :], ALU.mult), l_lams)
                for a in range(2):
                    tb = do("vector", lambda e, a=a: e.tensor_reduce(
                        lw[:, 8 + a:9 + a], lw[:, 4 * a:4 * a + 4], AX.X, ALU.add), ta)
                tc = do("scalar", lambda e: e.activation(lw[:, 10:12], lw[:, 8:10], ACT.Exp), tb)
                td = do("vector", lambda e: e.tensor_scalar(lw[:, 8:9], lw[:, 10:11], lam_init, -1.0,
                                                            ALU.add, ALU.mult), tc)
                t_lam = do("vector", lambda e: e.tensor_tensor(neg_lam[:, :], lw[:, 8:9], lw[:, 11:12], ALU.add), td)
                t_sub = do("vector", lambda e: e.tensor_scalar(sub_w[:, :], col("subln_w"), 1.0 - lam_init, None,
                                                               ALU.mult))

            for w in range(3):
                project(0, w)
            per = NU * GB
            LP, LV = 2, 3
            ct = {}
            for u in range(n_u + per):
                if u < n_u:
                    scores(u)
                if 1 <= u <= n_u:
                    exponentials(u - 1)
                j, G = u % per, u // per
                if j in (1, 2, 3) and G + 1 < NG and u < n_u:
                    project(G + 1, j - 1)
                if LP <= u < n_u + LP:
                    turn_p(u - LP)
                if LV <= u < n_u + LV:
                    values(u - LV)
                if G >= 1 and j == 5 and G - 1 < NG:
                    ct[G - 1] = context_turn(G - 1)
                if G >= 1 and j == 6 and G - 1 < NG:
                    context_out(G - 1, ct[G - 1])
                if G >= 1 and j == 7:
                    finish(G - 1)
            E.join()
            scope.close()

        def experts(name, G, src_T, ready, gate, up, down, NE, NI, weight, hS, sG, acc, acc_ready, w_ready, st):
            NC = NI // P
            for ex in range(NE):
                for c in range(NC):
                    k = st["k"]
                    st["k"] += 1
                    bg, bu = (k % 3) * 2, (k % 3) * 2 + 1
                    tg = do("tensor", lambda e, c=c, ex=ex, bg=bg: e.matmul(
                        ps[:, bg, :], gate[:, ex, c * P:(c + 1) * P], src_T, start=True, stop=True),
                        ready, st["free"][bg])
                    tu = do("tensor", lambda e, c=c, ex=ex, bu=bu: e.matmul(
                        ps[:, bu, :], up[:, ex, c * P:(c + 1) * P], src_T, start=True, stop=True),
                        st["free"][bu])
                    sl = k % 3
                    st["free"][bg] = ts = do("scalar", lambda e, bg=bg, sl=sl: e.activation(
                        sG[:, sl, :], ps[:, bg, :], ACT.Silu), tg, st["sg"][sl])
                    hp = (ex % 2) * NC + c
                    st["free"][bu] = st["sg"][sl] = th = do("vector", lambda e, bu=bu, sl=sl, hp=hp:
                        e.tensor_tensor(hS[:, hp, :], sG[:, sl, :], ps[:, bu, :], ALU.mult),
                        ts, tu, st["h"][ex % 2])
                if st["todo"]:
                    st["todo"].pop()()

                def down_product(ex=ex, th=th):
                    bank = 6 + st["y"] % 2
                    st["y"] += 1
                    for i in range(GB):
                        for c in range(NC):
                            t = do("tensor", lambda e, i=i, c=c: e.matmul(
                                ps[:, bank, i * C:(i + 1) * C], hS[:, (ex % 2) * NC + c, i * S:(i + 1) * S],
                                down[:, ex, c, :], start=c == 0, stop=c == NC - 1),
                                th, st["free"][bank], tell=(i == GB - 1 and c == NC - 1))
                    st["h"][ex % 2] = t
                    for i in range(GB):
                        t2 = do("vector", lambda e, i=i: e.scalar_tensor_tensor(
                            acc[:, i, :], ps[:, bank, i * C:(i + 1) * C], weight(G * GB + i, ex), acc[:, i, :],
                            ALU.mult, ALU.add), t, acc_ready, w_ready, st["acc"])
                    st["acc"] = st["free"][bank] = t2
                st["todo"].append(down_product)

        def new_state():
            return {"k": 0, "y": 0, "free": [None] * 8, "sg": [None] * 3, "h": [None] * 2, "todo": [], "acc": None}

        def moe_top2():
            scope = ExitStack()
            E.stage("moe")
            n1 = sb("moe_n", [P, GB, C], scope=scope)
            nT = sb("moe_nT", [P, GB, S], scope=scope)
            tT = sb("moe_tT", [P, NG, GN], scope=scope)
            lg = sb("moe_logits", [P, NB, NE0], scope=scope)
            wk = sb("moe_work", [P, 6, NB, NE0], scope=scope)
            sc = sb("moe_scalars", [P, 6, NB], scope=scope)
            comb = sb("moe_comb", [P, NB, NE0], scope=scope)
            hS = sb("moe_h", [P, 8, GN], scope=scope)
            sG = sb("moe_s", [P, 3, GN], scope=scope)
            free = [None] * 8
            used_n = used_nT = None
            for G in range(NG):
                t = layer_stats(G, x_done[G])
                t = normalize(G, t, n1, used_n)
                used_n = t2 = turn(lambda i: n1[:, i, :], 0, t, free[0])
                free[0] = t3 = do("scalar", lambda e: e.activation(nT[:, :, :], bank4(0), ACT.Identity,
                                                                   scale=col("ln1_g"), bias=col("ln1_b")),
                                  t2, used_nT)
                for i in range(GB):
                    t4 = do("tensor", lambda e, i=i: e.matmul(ps[:, 1, i * C:(i + 1) * C], nT[:, i, :],
                                                              W("attn_w"), start=True, stop=True),
                            t3, free[1], tell=i == GB - 1)
                used_nT = t4
                free[1], t5 = residual(G, bank4(1), t4)
                t6 = normalize(G, t5, n1, used_n)
                used_n = t7 = turn(lambda i: n1[:, i, :], 2, t6, free[2])
                free[2] = t8 = do("scalar", lambda e, G=G: e.activation(
                    tT[:, G, :], ps[:, 2, :], ACT.Identity, scale=col("ln2_g"), bias=col("ln2_b")), t7)
                for i in range(GB):
                    t9 = do("tensor", lambda e, i=i, G=G: e.matmul(
                        ps[:, 3, (G * GB + i) * 8:(G * GB + i) * 8 + 8], tT[:, G, i * S:(i + 1) * S],
                        gates[:, 0, :], start=True, stop=True), t8, l_gates, tell=i == GB - 1)
                x_done[G] = t5
            t = do("vector", lambda e: e.tensor_copy(lg[:, :, :], ps[:, 3, 0:NB * 8].rearrange(
                "p (b e) -> p b e", b=NB)), t9)
            iota = picks[:, 14:22].unsqueeze(1).broadcast_to([P, NB, NE0])

            def first_max(src, onehot, top, ready):
                a = do("vector", lambda e: e.tensor_reduce(top, src, AX.X, ALU.max), ready)
                a = do("vector", lambda e: e.tensor_tensor(wk[:, 0, :, :], src, top.unsqueeze(2).broadcast_to(
                    [P, NB, NE0]), ALU.is_lt), a)
                a = do("vector", lambda e: e.tensor_scalar(wk[:, 1, :, :], wk[:, 0, :, :], 100.0, None,
                                                           ALU.mult), a)
                a = do("vector", lambda e: e.tensor_tensor(wk[:, 0, :, :], wk[:, 1, :, :], iota, ALU.add), a)
                a = do("vector", lambda e: e.tensor_reduce(sc[:, 2, :], wk[:, 0, :, :], AX.X, ALU.min), a)
                return do("vector", lambda e: e.tensor_tensor(onehot, iota, sc[:, 2, :].unsqueeze(2).broadcast_to(
                    [P, NB, NE0]), ALU.is_equal), a)
            a = first_max(lg[:, :, :], wk[:, 2, :, :], sc[:, 0, :], t)
            a = do("vector", lambda e: e.scalar_tensor_tensor(
                wk[:, 3, :, :].rearrange("p b e -> p (b e)"), wk[:, 2, :, :].rearrange("p b e -> p (b e)"), -3.0e38,
                lg[:, :, :].rearrange("p b e -> p (b e)"), ALU.mult, ALU.add), a)
            a = first_max(wk[:, 3, :, :], wk[:, 4, :, :], sc[:, 1, :], a)
            a = do("vector", lambda e: e.tensor_tensor(sc[:, 3, :], sc[:, 1, :], sc[:, 0, :], ALU.subtract), a)
            a = do("scalar", lambda e: e.activation(sc[:, 4, :], sc[:, 3, :], ACT.Exp), a)
            a = do("vector", lambda e: e.tensor_scalar(sc[:, 3, :], sc[:, 4, :], 1.0, None, ALU.add), a)
            a = do("vector", lambda e: e.reciprocal(sc[:, 5, :], sc[:, 3, :]), a)
            a = do("vector", lambda e: e.tensor_tensor(sc[:, 3, :], sc[:, 5, :], sc[:, 4, :], ALU.mult), a)
            a = do("vector", lambda e: e.tensor_tensor(wk[:, 2, :, :], wk[:, 2, :, :], sc[:, 5, :].unsqueeze(2)
                                                       .broadcast_to([P, NB, NE0]), ALU.mult), a)
            a = do("vector", lambda e: e.tensor_tensor(wk[:, 4, :, :], wk[:, 4, :, :], sc[:, 3, :].unsqueeze(2)
                                                       .broadcast_to([P, NB, NE0]), ALU.mult), a)
            a = do("vector", lambda e: e.tensor_tensor(comb[:, :, :], wk[:, 2, :, :], wk[:, 4, :, :], ALU.add), a)
            E.join()
            st = new_state()
            fin = [None] * NG
            for G in range(NG + 1):
                if G < NG:
                    t = None
                    bank = 6 + st["y"] % 2
                    st["y"] += 1
                    for i in range(GB):
                        t = do("tensor", lambda e, i=i, G=G: e.transpose(
                            ps[:, bank, i * C:(i + 1) * C], x_T[:, G * GB + i, :], ident), st["free"][bank],
                            tell=i == GB - 1)
                    st["free"][bank] = t2 = do("vector", lambda e, G=G: e.tensor_tensor(
                        x_tok[:, group(G), :], x_tok[:, group(G), :], bank4(bank), ALU.add), t, x_done[G])
                    st["acc"] = t2
                    experts("moe", G, tT[:, G, :], None, gate_T, up_T, down_T, NE0, I0,
                            lambda b, ex: comb[:, b, ex:ex + 1], hS, sG, x_tok[:, group(G), :], t2, a, st)
                    st["todo"].pop()()
                    fin[G] = layer_stats(G, st["acc"])
                if G >= 1:
                    g = G - 1
                    x_done[g] = normalize(g, fin[g])
                    bank = 6 + st["y"] % 2
                    st["y"] += 1
                    xT_done[g] = st["free"][bank] = renew_xT(g, x_done[g], bank, st["free"][bank])
            E.join()
            scope.close()

        def memory():
            scope = ExitStack()
            E.stage("memory")
            n1 = NE1 * I1
            w1 = expert_w[:, 0:n1].rearrange("p (e i) -> p e i", e=NE1)
            w3 = expert_w[:, n1:2 * n1].rearrange("p (e i) -> p e i", e=NE1)
            w2 = expert_w[:, 2 * n1:3 * n1].rearrange("p (e k c) -> p e k c", e=NE1, c=C)
            l_moe1 = [E.dma("sync", "w1_T", w1, D["w1_T"]), E.dma("sync", "w3_T", w3, D["w3_T"]),
                      E.dma("sync", "w2_T", w2, D["w2_T"])]
            wc = sb("mem_wc", [P, P], scope=scope)
            sm = sb("mem_scalars", [P, 6], scope=scope)
            mT = sb("mem_mask", [P, P], scope=scope)
            mT0 = sb("mem_exp", [P, P], scope=scope)
            vC = sb("mem_v", [P, 2, GB, C], scope=scope)
            sM = sb("mem_s", [P, 2, GB, S], scope=scope)
            a = do("scalar", lambda e: e.activation(sm[:, 0:1], col("decay"), ACT.Exp, scale=-1.0))
            b_ = do("scalar", lambda e: e.activation(sm[:, 4:5], col("log_alpha"), ACT.Exp))
            a = do("vector", lambda e: e.tensor_scalar(sm[:, 1:2], sm[:, 0:1], 1.0, None, ALU.add), a)
            a = do("vector", lambda e: e.reciprocal(sm[:, 2:3], sm[:, 1:2]), a)
            a = do("scalar", lambda e: e.activation(sm[:, 3:4], sm[:, 2:3], ACT.Ln), a)
            a = do("scalar", lambda e: e.activation(mT0[:, :], diffs, ACT.Exp, scale=sm[:, 3:4]), a)
            t_mask = do("vector", lambda e: e.tensor_tensor(mT[:, :], mT0[:, :], causal, ALU.mult), a)
            t = do("tensor", lambda e: e.matmul(ps[:, 7, 0:P], W("w_write"), W("w_read"), start=True, stop=True))
            t_wc = do("vector", lambda e: e.tensor_scalar(wc[:, :], ps[:, 7, 0:P], sm[:, 4:5], None, ALU.mult),
                      t, b_)
            free = [None] * 8
            s_used, pend = [None] * 2, [None] * NG
            s_ready, v_ready = [None] * NG, [None] * NG
            for G in range(NG + 2):
                if G < NG:
                    s = G % 2
                    for i in range(GB):
                        t = do("tensor", lambda e, i=i, G=G, s=s: e.matmul(
                            ps[:, s, i * C:(i + 1) * C], x_T[:, G * GB + i, :], wc[:, :], start=True, stop=True),
                            t_wc, free[s], tell=i == GB - 1)
                    v_ready[G] = free[s] = do("scalar", lambda e, s=s: e.copy(vC[:, s, :, :], bank4(s)), t, s_used[s])
                    for i in range(GB):
                        c0 = 8 + (G * GB + i) * S
                        t = do("tensor", lambda e, i=i, G=G, s=s, c0=c0: e.matmul(
                            ps[:, 2 + s, i * S:(i + 1) * S], x_Tp[:, c0 - 1:c0 - 1 + S],
                            x_T[:, G * GB + i, :], start=True, stop=True), free[2 + s], t_pad, tell=i == GB - 1)
                    mb = mT[:, :].unsqueeze(1).broadcast_to([P, GB, S])
                    s_ready[G] = free[2 + s] = do("vector", lambda e, s=s: e.tensor_tensor(
                        sM[:, s, :, :], bank4(2 + s), mb, ALU.mult), t, t_mask, s_used[s])
                if G >= 1 and G - 1 < NG:
                    g = G - 1
                    s = g % 2
                    for i in range(GB):
                        t = do("tensor", lambda e, i=i, s=s: e.matmul(
                            ps[:, 4 + s, i * C:(i + 1) * C], sM[:, s, i, :], vC[:, s, i, :], start=True, stop=True),
                            s_ready[g], v_ready[g], free[4 + s], tell=i == GB - 1)
                    s_used[s] = t
                    free[4 + s], pend[g] = residual(g, bank4(4 + s), t, 2.0)
                if G >= 2:
                    g = G - 2
                    x_done[g] = normalize(g, pend[g])
            for g in range(NG):
                xT_done[g] = free[6 + g % 2] = renew_xT(g, x_done[g], 6 + g % 2, free[6 + g % 2])
            E.join()
            scope.close()
            return w1, w3, w2, l_moe1

        def expert_choice(w1, w3, w2, l_moe1):
            scope = ExitStack()
            E.stage("choice")
            NS = NB * NE1
            K = 26
            scS = sb("ch_scores", [P, NE1, NB], scope=scope)
            wk = sb("ch_work", [P, 6, NE1, NB], scope=scope)
            sm = sb("ch_small", [P, 16, NE1], scope=scope)
            half = sb("ch_halves", [P, K + 1], scope=scope)
            wgt = sb("ch_weights", [P, NE1, NB], scope=scope)
            hS = sb("ch_h", [P, 4, GN], scope=scope)
            sG = sb("ch_s", [P, 3, GN], scope=scope)
            for b in range(NB):
                t = do("tensor", lambda e, b=b: e.matmul(ps[:, 0, b * 8:b * 8 + 8], x_T[:, b, :], gates[:, 1, :],
                                                         start=True, stop=True), tell=b == NB - 1)
            v = lambda f, *w: do("vector", f, *w)
            p = lambda f, *w: do("gpsimd", f, *w)
            a = v(lambda e: e.tensor_copy(scS[:, :, :].rearrange("p e b -> p b e"),
                                          ps[:, 0, 0:NS].rearrange("p (b e) -> p b e", b=NB)), t)
            S_ = scS[:, :, :]
            r_ = lambda i: sm[:, i, :]
            bc = lambda x: x.unsqueeze(2).broadcast_to([P, NE1, NB])
            a1 = v(lambda e: e.tensor_reduce(r_(0), S_, AX.X, ALU.max), a)
            a2 = v(lambda e: e.tensor_reduce(r_(1), S_, AX.X, ALU.max, apply_absolute_value=True), a)
            m1 = p(lambda e: e.partition_all_reduce(r_(2), r_(0), P, RMAX), a1)
            m2 = p(lambda e: e.partition_all_reduce(r_(3), r_(1), P, RMAX), a2)
            lo, hi, mid, mx, big = r_(4), r_(5), r_(6), r_(2), r_(3)
            a3 = v(lambda e: e.tensor_reduce(sm[:, 7, 0:1], big, AX.X, ALU.max), m2)
            a4 = v(lambda e: e.tensor_scalar(lo, big, 0.0, sm[:, 7, 0:1], ALU.mult, ALU.subtract), a3)
            a5 = v(lambda e: e.tensor_scalar(hi, lo, -1.001, 1e-30, ALU.mult, ALU.add), a4)
            a6 = v(lambda e: e.tensor_scalar(half[:, 0:1], sm[:, 7, 0:1], 1.0, None, ALU.mult), a5)
            for k in range(K):
                a6 = v(lambda e, k=k: e.tensor_scalar(half[:, k + 1:k + 2], half[:, k:k + 1], 0.5, None, ALU.mult), a6)
            cur = v(lambda e: e.tensor_scalar(mid, lo, half[:, 0:1], None, ALU.add), a6)
            hdone = None
            for k in range(K):
                g = v(lambda e: e.tensor_tensor(wk[:, 0, :, :], S_, bc(mid), ALU.is_ge), cur)
                g = v(lambda e: e.tensor_reduce(r_(8), wk[:, 0, :, :], AX.X, ALU.add), g)
                g = do("tensor", lambda e: e.matmul(ps[:, 1, 0:NE1], ones, r_(8), start=True, stop=True), g)
                g1 = v(lambda e: e.tensor_scalar(r_(9), ps[:, 1, 0:NE1], float(CAP), 1e30, ALU.is_ge, ALU.mult), g, hdone)
                g2 = v(lambda e, k=k: e.tensor_scalar(r_(10), ps[:, 1, 0:NE1], float(CAP), half[:, k:k + 1],
                                                      ALU.is_ge, ALU.mult), g)
                h1 = v(lambda e: e.tensor_tensor(r_(11), mid, r_(9), ALU.add), g1)
                g3 = v(lambda e: e.tensor_tensor(lo, lo, r_(10), ALU.add), g2)
                h2 = v(lambda e: e.tensor_tensor(hi, hi, r_(11), ALU.min), h1)
                cur = v(lambda e, k=k: e.tensor_scalar(mid, lo, half[:, k + 1:k + 2], None, ALU.add), g3, h1)
            a = h2
            sure, tied = wk[:, 1, :, :], wk[:, 2, :, :]
            a = v(lambda e: e.tensor_tensor(sure, S_, bc(hi), ALU.is_ge), a, cur)
            a = v(lambda e: e.tensor_tensor(tied, S_, bc(lo), ALU.is_ge), a)
            a = v(lambda e: e.tensor_tensor(tied, tied, sure, ALU.subtract), a)
            a = v(lambda e: e.tensor_reduce(r_(8), sure, AX.X, ALU.add), a)
            t1 = do("tensor", lambda e: e.matmul(ps[:, 2, 0:NE1], ones, r_(8), start=True, stop=True), a)
            t2 = do("tensor", lambda e: e.matmul(ps[:, 3, 0:NS], below, tied, start=True, stop=True), a)
            t3 = do("tensor", lambda e: e.matmul(ps[:, 4, 0:NS], ones, tied, start=True, stop=True), a)
            a = v(lambda e: e.tensor_scalar(r_(12), ps[:, 2, 0:NE1], -1.0, float(CAP), ALU.mult, ALU.add), t1)
            v3 = lambda ap: ap.rearrange("p (e b) -> p e b", e=NE1)
            z = v(lambda e: e.memset(wk[:, 3:5, :, :], 0.0), a)
            a = v(lambda e: e.tensor_copy(wk[:, 3, :, 1:NB], v3(ps[:, 4, 0:NS])[:, :, 0:NB - 1]), t3, z)
            src, dst, sh = 3, 4, 1
            while sh < NB:
                a = v(lambda e, s=src, d=dst, sh=sh: e.tensor_tensor(
                    wk[:, d, :, sh:NB], wk[:, s, :, sh:NB], wk[:, s, :, 0:NB - sh], ALU.add), a)
                a = v(lambda e, s=src, d=dst, sh=sh: e.tensor_copy(wk[:, d, :, 0:sh], wk[:, s, :, 0:sh]), a)
                src, dst, sh = dst, src, sh * 2
            a = v(lambda e, s=src: e.tensor_tensor(wk[:, 5, :, :], wk[:, s, :, :], v3(ps[:, 3, 0:NS]), ALU.add), a, t2)
            a = v(lambda e: e.tensor_tensor(wk[:, 0, :, :], wk[:, 5, :, :], bc(r_(12)), ALU.is_lt), a)
            a = v(lambda e: e.tensor_tensor(wk[:, 5, :, :], wk[:, 0, :, :], tied, ALU.mult), a)
            a = v(lambda e: e.tensor_tensor(wk[:, 1, :, :], wk[:, 5, :, :], sure, ALU.add), a)
            c = v(lambda e: e.tensor_tensor(wk[:, 0, :, :], S_, bc(mx), ALU.subtract), a, m1)
            c = do("scalar", lambda e: e.activation(wk[:, 2, :, :], wk[:, 0, :, :], ACT.Exp), c)
            c = v(lambda e: e.tensor_tensor(wk[:, 5, :, :], wk[:, 2, :, :], wk[:, 1, :, :], ALU.mult), c)
            c = v(lambda e: e.tensor_reduce(r_(8), wk[:, 5, :, :], AX.X, ALU.add), c)
            c = do("tensor", lambda e: e.matmul(ps[:, 5, 0:NE1], ones, r_(8), start=True, stop=True), c)
            c = v(lambda e: e.reciprocal(r_(9), ps[:, 5, 0:NE1]), c)
            c = v(lambda e: e.tensor_tensor(wgt[:, :, :], wk[:, 5, :, :], bc(r_(9)), ALU.mult), c)
            E.join()
            st = new_state()
            fin = [None] * NG
            for G in range(NG + 1):
                if G < NG:
                    st["acc"] = x_done[G]
                    for l in l_moe1:
                        E.wait("tensor", l)
                    experts("choice", G, x_T[:, group(G), :], None, w1, w3, w2, NE1, I1,
                            lambda b, ex: wgt[:, ex, b:b + 1], hS, sG, x_tok[:, group(G), :], x_done[G], c, st)
                    st["todo"].pop()()
                    fin[G] = layer_stats(G, st["acc"])
                if G >= 1:
                    g = G - 1
                    x_done[g] = normalize(g, fin[g])
            scope.close()

        if STOP >= 2:
            cross_attention("x0", False)
        if STOP >= 3:
            for l in l_moe0:
                E.wait("tensor", l)
            moe_top2()
        if STOP >= 4:
            got = memory()
        if STOP >= 5:
            cross_attention("x1", True)
        if STOP >= 6:
            expert_choice(*got)
        output()
        E.wait("sync", *stores)
        with nc.Block() as block:
            E.emit(block)


PROJ = ["ret_q", "ret_k", "ret_v", "ret_o", "x0_q", "x0_k", "x0_v", "x0_o", "attn_w",
        "w_write", "w_read", "x1_q", "x1_k", "x1_v", "x1_o"]
COLS = ["gn_w", "gn_b", "xq_b", "xk_b", "ln1_g", "ln1_b", "ln2_g", "ln2_b", "subln_w", "decay", "log_alpha"]


def constants(S, C):
    f = np.float32
    gam = (f(1.0) - np.exp(np.linspace(math.log(1 / 32), math.log(1 / 512), 8, dtype=f))).astype(np.float64)
    s, t = np.arange(S)[:, None], np.arange(S)[None, :]
    decay = np.stack([np.where(t >= s, g ** np.maximum(t - s, 0), 0.0) for g in gam], 1).astype(f)
    p = np.arange(P)
    headavg = (p[:, None] // 16 == p[None, :] // 16) / 16.0
    mats = np.stack([np.eye(P), headavg, np.maximum(t - 1 - s, 0), (t > s) & (s > 0), s < t, np.ones((P, P))],
                    1).astype(f)
    picks = np.concatenate([(p[:, None] % 32) // 16 == np.arange(2), (p[:, None] % 32) // 8 == np.arange(4),
                            (p[:, None] % 32) // 4 == np.arange(8), np.broadcast_to(np.arange(8), (P, 8))],
                           1).astype(f)
    return decay, mats, picks


def kernel(**inputs):
    import concourse.bacc as bacc
    from concourse.bass_utils import run_bass_kernel_spmd

    i = {k: np.asarray(v) for k, v in inputs.items()}
    B, S, C = i["x"].shape
    order = np.array([(a * 16 + 4 * g + j) * 4 + d for g in range(4) for a in range(2) for j in range(4)
                      for d in range(4)])
    decay, mats, picks = constants(S, C)
    proj = [i["L0_attn_Wq"].T, i["L0_attn_Wk"].T, i["L0_attn_Wv"].T, i["L0_attn_Wo"].T,
            i["L0_xattn_wq_w"], i["L0_xattn_wk_w"], i["L0_xattn_wv_w"], i["L0_xattn_wo_w"],
            i["L0_ffn_attn_w"].T, i["L1_attn_W_write"], i["L1_attn_W_read"].T,
            i["L1_xattn_Wq"][order].T, i["L1_xattn_Wk"][order].T, i["L1_xattn_Wv"].T, i["L1_xattn_Wp"].T]
    rep = lambda v: np.broadcast_to(np.asarray(v).reshape(1, -1), (P, np.asarray(v).size))
    cols = [i["L0_attn_gn_weight"], i["L0_attn_gn_bias"], i["L0_xattn_wq_b"], i["L0_xattn_wk_b"],
            i["L0_ffn_ln1_g"], i["L0_ffn_ln1_b"], i["L0_ffn_ln2_g"], i["L0_ffn_ln2_b"],
            np.tile(i["L1_xattn_subln_w"], 16), rep(i["L1_attn_decay"])[:, 0], rep(i["L1_attn_log_alpha"])[:, 0]]
    chunked = lambda w: w.reshape(w.shape[0], C, -1, P).transpose(3, 0, 2, 1)
    data = {
        "x_tok": i["x"].transpose(1, 0, 2), "x_T": i["x"].transpose(2, 0, 1),
        "ctx_T": i["ctx_1024"].transpose(2, 0, 1), "mask": i["mask_Bx1xSxS2_ff1"][:, 0].transpose(1, 0, 2),
        "proj": np.stack(proj, 1), "cols": np.stack(cols, 1),
        "rows": np.stack([rep(i["L0_xattn_wv_b"]), rep(i["L0_xattn_wo_b"]), rep(i["L1_xattn_bp"])], 1),
        "gates": np.stack([i["L0_ffn_gate_w"].T, i["L1_ffn_Wg"].T], 1),
        "lams": np.stack([rep(i["L1_xattn_" + n]) for n in ("lq1", "lk1", "lq2", "lk2")], 1),
        "gate_T": i["L0_ffn_gate_proj"].transpose(2, 0, 1), "up_T": i["L0_ffn_up_proj"].transpose(2, 0, 1),
        "down_T": chunked(i["L0_ffn_down_proj"]),
        "w1_T": i["L1_ffn_W1"].transpose(2, 0, 1), "w3_T": i["L1_ffn_W3"].transpose(2, 0, 1),
        "w2_T": chunked(i["L1_ffn_W2"]),
        "decay": decay, "mats": mats, "picks": picks,
    }
    nc = bacc.Bacc("TRN2", target_bir_lowering=False, num_devices=1)
    arrays, D = {}, {}
    for name, a in data.items():
        a = np.ascontiguousarray(a)
        arrays[name] = a
        D[name] = nc.dram_tensor(name, a.shape, mybir.dt.from_np(a.dtype), kind="ExternalInput").ap()
    out = nc.dram_tensor("out", (S, B, C), F32, kind="ExternalOutput").ap()
    build(nc, D, out)
    r = run_bass_kernel_spmd(nc, [arrays], core_ids=[0])
    return np.ascontiguousarray(r.results[0]["out"].transpose(1, 0, 2))
```

```python
import math
from contextlib import ExitStack

import concourse.bass as bass
import numpy as np
from concourse import mybir

F32 = mybir.dt.float32
ALU = mybir.AluOpType
ACT = mybir.ActivationFunctionType
AX = mybir.AxisListType
RMAX = bass.bass_isa.ReduceOp.max

P = 128
STOP = 6


class Engines:

    ORDER = ("sync", "tensor", "vector", "scalar", "gpsimd")

    def __init__(self, nc, ctx):
        self.nc, self.ctx = nc, ctx
        self.queue = {e: [] for e in self.ORDER}
        self.progress, self.count, self.last = {}, {}, {}

    def sem(self, name):
        return self.ctx.enter_context(self.nc.semaphore(name))

    def stage(self, name):
        for e in self.ORDER[1:]:
            self.progress[e] = self.sem(f"{name}_{e}_done")
            self.count[e] = 0

    def do(self, engine, what, *waits, tell=True):
        step = [[w for w in waits if w is not None], what, None, 1]
        self.queue[engine].append(step)
        if not tell:
            return None
        self.count[engine] += 1
        step[2] = self.progress[engine]
        token = (self.progress[engine], self.count[engine])
        self.last[engine] = token
        return token

    def dma(self, engine, name, out, in_, *waits, **how):
        s = self.sem(f"{name}_landed")
        self.queue[engine].append([[w for w in waits if w is not None],
                                   lambda e: e.dma_start(out, in_, **how), s, 16])
        return (s, 16)

    def wait(self, engine, *waits):
        self.queue[engine].append([[w for w in waits if w is not None], None, None, 0])

    def join(self):
        ends = dict(self.last)
        for e in self.ORDER:
            self.wait(e, *[t for f, t in ends.items() if f != e])

    def emit(self, block):
        def body(name):
            def run(eng):
                seen = {}
                for waits, what, s, by in self.queue[name]:
                    for ws, value in waits:
                        if seen.get(id(ws), 0) < value:
                            eng.wait_ge(ws, value)
                            seen[id(ws)] = value
                    if what is not None:
                        ins = what(eng)
                        if s is not None:
                            ins.then_inc(s, by)
            return run
        for name in self.ORDER:
            blocks = {"sync": block.sync, "tensor": block.tensor, "vector": block.vector,
                            "scalar": block.scalar, "gpsimd": block.gpsimd}[name]
            blocks(body(name))


def build(nc, D, out):
    NB, S, C = D["x_tok"].shape[1], D["x_T"].shape[2], D["x_T"].shape[0]
    SK = D["ctx_T"].shape[2]
    GB = 4
    NG = NB // GB
    GN = GB * S
    EPS = 1e-5
    NE0, I0 = D["gate_T"].shape[1], D["gate_T"].shape[2]
    NE1, I1 = D["w1_T"].shape[1], D["w1_T"].shape[2]
    CAP = NB * S // NE1
    NEG = 1e9

    with ExitStack() as ctx:
        def sb(name, shape, dt=F32, scope=ctx):
            return scope.enter_context(nc.sbuf_tensor(name, shape, dt))

        E = Engines(nc, ctx)
        do = E.do
        ps = ctx.enter_context(nc.psum_tensor("ps", [P, 8, 512], F32))

        x_tok = sb("x_tok_sb", [P, NB, C])
        x_Tp = sb("x_T_sb", [P, NB * S + 8])
        x_T = x_Tp[:, 8:].rearrange("p (b t) -> p b t", b=NB)
        ctx_T = sb("ctx_T_sb", [P, NB, SK])
        n_proj = D["proj"].shape[1]
        proj = sb("proj_sb", [P, n_proj, P])
        n_cols = D["cols"].shape[1]
        cols = sb("cols_sb", [P, n_cols])
        rows = sb("rows_sb", [P, 3, P])
        gates = sb("gates_sb", [P, 2, 8])
        lams = sb("lams_sb", [P, 4, D["lams"].shape[2]])
        n_mats = D["mats"].shape[1]
        mats = sb("mats_sb", [P, n_mats, P])
        picks = sb("picks_sb", [P, D["picks"].shape[1]])
        stats = sb("stats", [P, NB, 6])
        mv = sb("mv", [P, NB, 2])
        veps = sb("veps", [P, NB])
        rstd = sb("rstd", [P, NB])
        minus_half = sb("minus_half", [P, P])
        EW = max(2 * NE0 * I0 + NE0 * I0, 2 * NE1 * I1 + NE1 * I1)
        expert_w = sb("expert_w", [P, EW])

        PJ = {n: i for i, n in enumerate(PROJ)}
        CO = {n: i for i, n in enumerate(COLS)}
        W = lambda n: proj[:, PJ[n], :]
        col = lambda n: cols[:, CO[n]:CO[n] + 1]
        ident, headavg, diffs, causal, below, ones, mean8 = [mats[:, i, :] for i in range(7)]

        E.stage("start")
        l_proj = E.dma("sync", "proj", proj[:, :, :], D["proj"])
        l_xT = [E.dma("sync", f"x_T{h}", x_T[:, h * 16:h * 16 + 16, :], D["x_T"][:, h * 16:h * 16 + 16, :])
                for h in range(2)]
        l_picks = E.dma("sync", "picks", picks[:, :], D["picks"])
        l_cols = E.dma("sync", "cols", cols[:, :], D["cols"])
        l_mats = E.dma("sync", "mats", mats[:, :, :], D["mats"])
        iota16 = sb("iota16", [P, P], mybir.dt.float16)
        a_scope = ExitStack()
        decay_T = sb("decay_T", [P, 8, S], scope=a_scope)
        l_decay = E.dma("sync", "decay", decay_T[:, :, :], D["decay"])
        l_xtok = E.dma("sync", "x_tok", x_tok[:, :, :], D["x_tok"])
        l_ctx = E.dma("sync", "ctx_T", ctx_T[:, :, :], D["ctx_T"])
        l_rows = E.dma("sync", "rows", rows[:, :, :], D["rows"])
        l_gates = E.dma("sync", "gates", gates[:, :, :], D["gates"])
        l_lams = E.dma("sync", "lams", lams[:, :, :], D["lams"])
        n0 = NE0 * I0
        gate_T = expert_w[:, 0:n0].rearrange("p (e i) -> p e i", e=NE0)
        up_T = expert_w[:, n0:2 * n0].rearrange("p (e i) -> p e i", e=NE0)
        down_T = expert_w[:, 2 * n0:3 * n0].rearrange("p (e k c) -> p e k c", e=NE0, c=C)
        l_moe0 = [E.dma("sync", "gate_T", gate_T, D["gate_T"]), E.dma("sync", "up_T", up_T, D["up_T"]),
                  E.dma("sync", "down_T", down_T, D["down_T"])]
        iotas = picks[:, 14:14 + P]
        tokens = picks[:, 14 + P:14 + P + NB // 2]
        t_i16 = do("gpsimd", lambda e: e.tensor_copy(iota16[:, :], iotas), l_picks)
        t_half = do("gpsimd", lambda e: e.memset(minus_half[:, :], -0.5))
        t_pad = do("gpsimd", lambda e: e.memset(x_Tp[:, 0:8], 0.0))

        def group(G):
            return slice(G * GB, (G + 1) * GB)

        def layer_stats(G, ready):
            t = ready
            for b in range(G * GB, (G + 1) * GB):
                t = do("vector", lambda e, b=b: e.bn_stats(stats[:, b, :], x_tok[:, b, :]), ready)
            for b in range(G * GB, (G + 1) * GB):
                t2 = do("vector", lambda e, b=b: e.bn_aggr(mv[:, b, :], stats[:, b, :]), t)
            g = group(G)
            t3 = do("gpsimd", lambda e: e.tensor_scalar(veps[:, g], mv[:, g, 1], EPS, None, ALU.add), t2)
            return do("gpsimd", lambda e: e.tensor_tensor(rstd[:, g], veps[:, g], minus_half[:, 0:GB], ALU.pow),
                      t3, t_half)

        def residual(G, summand, ready, times=1.0):
            g = group(G)
            t = do("vector", lambda e: e.scalar_tensor_tensor(x_tok[:, g, :], x_tok[:, g, :], times, summand,
                                                              ALU.mult, ALU.add), ready, l_xtok)
            return t, layer_stats(G, t)

        def normalize(G, ready, dst=None, *waits):
            dst = x_tok if dst is None else dst
            for i, b in enumerate(range(G * GB, (G + 1) * GB)):
                o = dst[:, b, :] if dst is x_tok else dst[:, i, :]
                t = do("vector", lambda e, b=b, o=o: e.tensor_scalar(
                    o, x_tok[:, b, :], mv[:, b, 0:1], rstd[:, b:b + 1], ALU.subtract, ALU.mult), ready, *waits)
            return t

        def turn(src, bank, *waits):
            for i in range(GB):
                t = do("tensor", lambda e, i=i, tile=src(i): e.transpose(ps[:, bank, i * S:(i + 1) * S], tile, ident),
                       *waits, l_mats, tell=i == GB - 1)
            return t

        def bank4(bank):
            return ps[:, bank, :].rearrange("p (b c) -> p b c", b=GB)

        def renew_xT(G, ready, bank, bank_free):
            t = turn(lambda i: x_tok[:, G * GB + i, :], bank, ready, bank_free)
            return do("scalar", lambda e: e.copy(x_T[:, group(G), :], bank4(bank)), t)

        def output():
            for G in range(NG):
                stores.append(E.dma("sync", f"out{G}", out[:, group(G), :], x_tok[:, group(G), :], x_done[G]))

        stores = []
        x_done = [l_xtok] * NG
        xT_done = [l_xT[G * GB // 16] for G in range(NG)]

        E.stage("retention")
        NH, HD = 8, C // 8
        kT = sb("ret_kT", [P, 2, GN], scope=a_scope)
        qB = sb("ret_qB", [P, 2, 2, GN], scope=a_scope)
        vB = sb("ret_v", [P, 2, GB, 4, 2, 32], scope=a_scope)
        t_zero = do("gpsimd", lambda e: e.memset(vB[:, :, :, :, :, :], 0.0))
        aT = sb("ret_aT", [P, 3, 2, 2, S], scope=a_scope)
        yT = sb("ret_yT", [P, NB, S], scope=a_scope)
        ystat = sb("ret_ystat", [P, NB, 6], scope=a_scope)
        ymv = sb("ret_ymv", [P, NB, 2], scope=a_scope)
        small = sb("ret_small", [P, 8, NB], scope=a_scope)

        free7 = None
        qkv_ready = [[None] * 3 for _ in range(NG)]
        qk_free = [None, None]
        y_free = [None, None]
        av_done = [None] * (2 * NB + 4)
        group_used = [None] * (NG + 1)

        def ret_project(G, which):
            nonlocal free7
            s = G % 2
            old = group_used[G - 2] if G >= 2 else None
            rhs = x_T[:, group(G), :]
            if which == 0:
                t = do("tensor", lambda e: e.matmul(ps[:, 7, :], W("ret_q"), rhs, start=True, stop=True),
                       free7, l_proj, xT_done[G])
                for j in range(2):
                    free7 = do("scalar", lambda e, j=j: e.activation(
                        qB[:, s, j, :], ps[:, 7, :], ACT.Copy, scale=picks[:, j:j + 1]), t, old, l_picks)
            elif which == 1:
                t = do("tensor", lambda e: e.matmul(ps[:, 7, :], W("ret_k"), rhs, start=True, stop=True), free7)
                free7 = do("scalar", lambda e: e.copy(kT[:, s, :], ps[:, 7, :]), t, old)
            else:
                for i in range(GB):
                    t = do("tensor", lambda e, i=i: e.matmul(ps[:, 7, i * S:(i + 1) * S], x_T[:, G * GB + i, :],
                                                             W("ret_v"), start=True, stop=True),
                           free7, tell=i == GB - 1)
                for i in range(GB):
                    flat = vB[:, s, i, :, :, :].rearrange("p g j c -> p g (j c)")
                    dst = bass.AP(tensor=flat.tensor, offset=flat.offset,
                                  ap=[list(flat.ap[0]), [64, 4], [48, 2], [1, HD]])
                    src = ps[:, 7, i * C:(i + 1) * C].rearrange("p (g j d) -> p g j d", g=4, d=HD)
                    free7 = do("scalar", lambda e, dst=dst, src=src: e.copy(dst, src), t, old, t_zero)
            qkv_ready[G][which] = free7

        def ret_scores(u):
            b, h = divmod(u, 2)
            G, i = divmod(b, GB)
            s = G % 2
            for q in range(2):
                g = 2 * h + q
                t = do("tensor", lambda e, g=g: e.matmul(
                    ps[:, g, 0:2 * S].rearrange("p (j t) -> p j t", j=2),
                    kT[32 * g:32 * g + 32, s, i * S:(i + 1) * S],
                    qB[32 * g:32 * g + 32, s, :, i * S:(i + 1) * S], start=True, stop=True),
                    qk_free[h], *qkv_ready[G], tell=q == 1)
            a = aT[:, u % 3, :, :, :].rearrange("p g j t -> p g (j t)")
            m = decay_T[:, 4 * h:4 * h + 4, :].rearrange("p (g j) t -> p g (j t)", g=2)
            qk_free[h] = masked[u] = do("vector", lambda e: e.tensor_tensor(
                a, ps[:, 2 * h:2 * h + 2, 0:2 * S], m, ALU.mult), t, l_decay, av_done[u - 3] if u >= 3 else None)

        def ret_values(u):
            b, h = divmod(u, 2)
            G, i = divmod(b, GB)
            bank = 4 + G % 2
            for n in range(4):
                g, j = 2 * h + n // 2, n % 2
                t = do("tensor", lambda e, n=n, g=g, j=j: e.matmul(
                    ps[32 * g:32 * g + 32, bank, i * S:(i + 1) * S], vB[:, G % 2, i, g, j, :],
                    aT[:, u % 3, n // 2, j, :], start=j == 0, stop=j == 1),
                    masked[u], y_free[G % 2], tell=n == 3)
            av_done[u] = t
            if u % 8 == 7:
                group_used[G] = t
                y_free[G % 2] = y_copied[G] = do("scalar", lambda e: e.copy(yT[:, group(G), :], bank4(bank)), t)

        masked = [None] * (2 * NB)
        y_copied = [None] * NG

        def ret_turn(G):
            for b in range(G * GB, (G + 1) * GB):
                t3 = do("vector", lambda e, b=b: e.bn_stats(ystat[:, b, :], yT[:, b, :]), y_copied[G])
            return t3

        for w in range(3):
            ret_project(0, w)
        n_u = 2 * NB
        for u in range(n_u + 2):
            if u < n_u:
                ret_scores(u)
            if u % 8 in (1, 2, 3) and u // 8 + 1 < NG:
                ret_project(u // 8 + 1, u % 8 - 1)
            if u >= 1 and u - 1 < n_u:
                ret_values(u - 1)
            if u % 8 == 4 and u >= 8:
                ret_turn(u // 8 - 1)
        t = ret_turn(NG - 1)
        for b in range(NB):
            t2 = do("vector", lambda e, b=b: e.bn_aggr(ymv[:, b, :], ystat[:, b, :]), t)
        mean_h, delta, dvar, v_h, y_scale, y_bias, tmp = [small[:, i, :] for i in range(7)]
        t3 = do("tensor", lambda e: e.matmul(ps[:, 6, 0:NB], headavg, ymv[:, :, 0], start=True, stop=True), t2)
        t4 = do("vector", lambda e: e.tensor_copy(mean_h, ps[:, 6, 0:NB]), t3)
        t5 = do("vector", lambda e: e.tensor_tensor(delta, ymv[:, :, 0], mean_h, ALU.subtract), t4)
        t6 = do("vector", lambda e: e.tensor_tensor(dvar, delta, delta, ALU.mult), t5)
        t7 = do("vector", lambda e: e.tensor_tensor(dvar, dvar, ymv[:, :, 1], ALU.add), t6)
        t8 = do("tensor", lambda e: e.matmul(ps[:, 6, 0:NB], headavg, dvar, start=True, stop=True), t7)
        t9 = do("vector", lambda e: e.tensor_scalar(v_h, ps[:, 6, 0:NB], EPS, None, ALU.add), t8)
        t10 = do("gpsimd", lambda e: e.tensor_tensor(tmp, v_h, minus_half[:, 0:NB], ALU.pow), t9, t_half)
        t11 = do("vector", lambda e: e.tensor_scalar(y_scale, tmp, col("gn_w"), None, ALU.mult), t10, l_cols)
        t12 = do("vector", lambda e: e.tensor_tensor(delta, mean_h, y_scale, ALU.mult), t11)
        t13 = do("vector", lambda e: e.tensor_scalar(y_bias, delta, -1.0, col("gn_b"), ALU.mult, ALU.add), t12)
        bank_free = [None] * 8
        pend = [None] * NG
        for G in range(NG + 2):
            if G < NG:
                for b in range(G * GB, (G + 1) * GB):
                    t = do("scalar", lambda e, b=b: e.activation(
                        yT[:, b, :], yT[:, b, :], ACT.Identity, scale=y_scale[:, b:b + 1],
                        bias=y_bias[:, b:b + 1]), t13)
                bank = G % 3
                for i in range(GB):
                    t2 = do("tensor", lambda e, i=i, G=G, bank=bank: e.matmul(
                        ps[:, bank, i * S:(i + 1) * S], yT[:, G * GB + i, :], W("ret_o"), start=True, stop=True),
                        t, bank_free[bank], tell=i == GB - 1)
                bank_free[bank], pend[G] = residual(G, bank4(bank), t2)
            if G >= 1 and G - 1 < NG:
                g = G - 1
                x_done[g] = normalize(g, pend[g])
                xT_done[g] = bank_free[4 + g % 2] = renew_xT(g, x_done[g], 4 + g % 2, bank_free[4 + g % 2])
        E.join()
        a_scope.close()

        def cross_attention(name, differential):
            scope = ExitStack()
            E.stage(name)
            NA = 2 if differential else 1
            NK = 4 * NA
            UH = 8
            VD = 8
            ND, NPB = 4, 6
            qT = sb(name + "_qT", [P, 2, GN], scope=scope)
            kB = sb(name + "_kB", [P, 2, NK, GB, SK], scope=scope)
            vX = sb(name + "_vX", [SK, 2, GB, 4, 4, 32], scope=scope)
            mS = sb(name + "_m", [P, ND, UH], scope=scope)
            dS = sb(name + "_d", [P, ND, UH, SK], scope=scope)
            pS = sb(name + "_p", [P, NPB, UH, SK], scope=scope)
            sums = sb(name + "_sums", [P, 2, NA, GB, 16], scope=scope)
            coef = sb(name + "_coef", [P, 4, UH], scope=scope)
            nS = sb(name + "_n", [P, 3, UH, SK], scope=scope)
            pT = sb(name + "_pT", [SK, 2, UH, S], scope=scope)
            cT = sb(name + "_cT", [P, 2, GN], scope=scope)
            if differential:
                cN = sb(name + "_cN", [P, 2, GN], scope=scope)
                sq = sb(name + "_sq", [P, 2, GN], scope=scope)
                rr = sb(name + "_rr", [P, 2, GN], scope=scope)
                lsq = sb(name + "_lsq", [P, 2, GB, C], scope=scope)
            else:
                tS = sb(name + "_t", [P, 2, UH, SK], scope=scope)
                rS = sb(name + "_r", [P, 3, UH, SK], scope=scope)
                mask = sb(name + "_mask", [P, NB, SK], scope=scope)
                l_mask = E.dma("sync", "mask", mask[:, :, :], D["mask"])
            t_zero = do("gpsimd", lambda e: e.memset(vX[:, :, :, :, :, :], 0.0))

            free7 = free6 = None
            ready = [[None] * 3 for _ in range(NG)]
            qk_free = [None, None]
            pt_free = None
            qk_last, av_last, c_done = [None] * NG, [None] * NG, [None] * NG
            NW = 2 * NB
            n_u = NA * NW
            soft, exp_done, sum_done, p_used = [[None] * n_u for _ in range(4)]
            n_done, turned, pt_ready, av_done = [[None] * NW for _ in range(4)]
            cT_used, cN_used = [None, None], [None, None]
            pend = [None] * NG

            def before(tokens, i):
                return tokens[i] if i >= 0 else None

            def project(G, which):
                nonlocal free7
                s = G % 2
                old = before(qk_last, G - 2)
                if which == 0:
                    t = do("tensor", lambda e: e.matmul(ps[:, 7, :], W(name + "_q"), x_T[:, group(G), :],
                                                        start=True, stop=True), free7)
                    if differential:
                        free7 = do("scalar", lambda e: e.mul(qT[:, s, :], ps[:, 7, :], 0.5), t, old)
                    else:
                        free7 = do("vector", lambda e: e.tensor_scalar(
                            qT[:, s, :], ps[:, 7, :], col("xq_b"), 1.0 / (NEG * math.sqrt(8.0)),
                            ALU.add, ALU.mult), t, old)
                elif which == 1:
                    kin = ctx_T[:, group(G), :]
                    kp = ps[:, 7, 0:GB * SK]
                    t = do("tensor", lambda e: e.matmul(kp, W(name + "_k"), kin, start=True, stop=True),
                           free7, l_ctx)
                    src = kp.rearrange("p (b k) -> p b k", b=GB)
                    for j in range(NK):
                        dst = kB[:, s, j, :, :]
                        pick = picks[:, (6 if differential else 2) + j:(7 if differential else 3) + j]
                        if differential:
                            free7 = do("scalar", lambda e, dst=dst, pick=pick: e.activation(
                                dst, src, ACT.Copy, scale=pick), t, old)
                        else:
                            bias = kbias[:, j:j + 1]
                            free7 = do("scalar", lambda e, dst=dst, pick=pick, bias=bias: e.activation(
                                dst, src, ACT.Identity, scale=pick, bias=bias), t, old, t_kbias)
                else:
                    for i in range(GB):
                        t = do("tensor", lambda e, i=i: e.matmul(
                            ps[0:SK, 7, i * C:(i + 1) * C], ctx_T[:, G * GB + i, :], W(name + "_v"),
                            start=True, stop=True), free7, l_ctx, tell=i == GB - 1)
                    old = before(av_last, G - 2)
                    for i in range(GB):
                        flat = vX[:, s, i, :, :, :].rearrange("p g j c -> p g (j c)")
                        dst = bass.AP(tensor=flat.tensor, offset=flat.offset,
                                      ap=[list(flat.ap[0]), [128, 4], [40, 4], [1, VD]])
                        src = ps[0:SK, 7, i * C:(i + 1) * C].rearrange("p (g j d) -> p g j d", g=4, d=VD)
                        if differential:
                            free7 = do("scalar", lambda e, dst=dst, src=src: e.copy(dst, src), t, old, t_zero)
                        else:
                            bias = rows[0:SK, 0, :].rearrange("p (g j d) -> p g j d", g=4, d=VD)
                            free7 = do("vector", lambda e, dst=dst, src=src, bias=bias: e.tensor_tensor(
                                dst, src, bias, ALU.add), t, old, t_zero, l_rows)
                ready[G][which] = free7

            def scores(w):
                b, half = divmod(w, 2)
                G, i = divmod(b, GB)
                s = G % 2
                for att in range(NA):
                    u = w * NA + att
                    bp = 2 * (u % 2)
                    for q in range(2):
                        g = 2 * half + q
                        t = do("tensor", lambda e, g=g, q=q, bp=bp, att=att: e.matmul(
                            ps[:, bp + q, 0:4 * SK].rearrange("p (j k) -> p j k", j=4),
                            qT[32 * g:32 * g + 32, s, i * S:(i + 1) * S],
                            kB[32 * g:32 * g + 32, s, 4 * att:4 * att + 4, i, :], start=True, stop=True),
                            qk_free[u % 2], *ready[G], tell=q == 1)
                    if half == 1 and i == GB - 1:
                        qk_last[G] = t
                    sc = ps[:, bp:bp + 2, 0:4 * SK].rearrange("p g (j k) -> p g j k", j=4)
                    v = u % ND
                    m = mS[:, v, :]
                    if differential:
                        t2 = do("vector", lambda e, m=m, sc=sc: e.tensor_reduce(m, sc, AX.X, ALU.max), t)
                        mb = m.rearrange("p (g j k) -> p g j k", g=2, k=1).broadcast_to([P, 2, 4, SK])
                        soft[u] = qk_free[u % 2] = do("vector", lambda e, v=v, sc=sc, mb=mb: e.tensor_tensor(
                            dS[:, v, :, :].rearrange("p (g j) k -> p g j k", g=2), sc, mb, ALU.subtract),
                            t2, before(exp_done, u - ND))
                    else:
                        mk = mask[:, b:b + 1, :].unsqueeze(1).broadcast_to([P, 2, 4, SK])
                        qk_free[u % 2] = t2 = do("vector", lambda e, sc=sc: e.tensor_tensor(
                            tS[:, u % 2, :, :].rearrange("p (g j) k -> p g j k", g=2), sc, mk, ALU.mult),
                            t, l_mask)
                        flat = tS[:, u % 2, :, :].rearrange("p h k -> p (h k)")
                        t3 = do("vector", lambda e: e.scalar_tensor_tensor(
                            rS[:, u % 3, :, :].rearrange("p h k -> p (h k)"), flat, 0.0, flat,
                            ALU.is_equal, ALU.subtract), t2, before(soft, u - 3))
                        t4 = do("vector", lambda e: e.tensor_reduce(m, rS[:, u % 3, :, :], AX.X, ALU.min), t3)
                        soft[u] = do("gpsimd", lambda e: e.tensor_tensor(
                            dS[:, v, :, :], rS[:, u % 3, :, :], m.unsqueeze(2).broadcast_to([P, UH, SK]),
                            ALU.subtract), t4, before(exp_done, u - ND))

            def exponentials(w):
                for u in range(w * NA, (w + 1) * NA):
                    exp_done[u] = do("scalar", lambda e, u=u: e.activation(
                        pS[:, u % NPB, :, :], dS[:, u % ND, :, :], ACT.Exp, scale=1.0 if differential else -NEG),
                        soft[u], before(p_used, u - NPB))

            def normalizers(w):
                b, half = divmod(w, 2)
                G, i = divmod(b, GB)
                n = w % 3
                for att in range(NA):
                    u = w * NA + att
                    l = sums[:, G % 2, att, i, 8 * half:8 * half + 8]
                    ts = do("vector", lambda e, u=u, l=l: e.tensor_reduce(l, pS[:, u % NPB, :, :], AX.X, ALU.add),
                            exp_done[u], before(c_done, G - 2))
                c0, c1 = coef[:, w % 2, :], coef[:, 2 + w % 2, :]
                old = before(turned, w - 3)
                tr = do("vector", lambda e: e.reciprocal(c0, l), ts, before(n_done, w - 2))
                if not differential:
                    p0 = pS[:, w % NPB, :, :]
                    p_used[w] = n_done[w] = do("gpsimd", lambda e: e.tensor_tensor(
                        nS[:, n, :, :], p0, c0.unsqueeze(2).broadcast_to([P, UH, SK]), ALU.mult), tr, old)
                else:
                    p1, p2 = pS[:, (2 * w) % NPB, :, :], pS[:, (2 * w + 1) % NPB, :, :]
                    l1 = sums[:, G % 2, 0, i, 8 * half:8 * half + 8]
                    tc = do("vector", lambda e: e.scalar_tensor_tensor(c1, l1, neg_lam[:, 0:1], c0,
                                                                       ALU.mult, ALU.mult), tr, t_lam)
                    t = do("gpsimd", lambda e: e.tensor_tensor(
                        nS[:, n, :, :], p2, c1.unsqueeze(2).broadcast_to([P, UH, SK]), ALU.mult), tc, old)
                    t = do("gpsimd", lambda e: e.tensor_tensor(nS[:, n, :, :], nS[:, n, :, :], p1, ALU.add), t)
                    p_used[2 * w] = p_used[2 * w + 1] = n_done[w] = t

            def turn_p(w):
                nonlocal pt_free
                for h in range(UH):
                    t = do("tensor", lambda e, h=h: e.transpose(
                        ps[0:SK, 4 + h // 4, (h % 4) * S:(h % 4 + 1) * S], nS[:, w % 3, h, :], ident),
                        n_done[w], pt_free, tell=h == UH - 1)
                turned[w] = t
                pt_free = pt_ready[w] = do("scalar", lambda e: e.copy(
                    pT[:, w % 2, :, :].rearrange("p (g h) q -> p g (h q)", g=2), ps[0:SK, 4:6, :]),
                    t, before(av_done, w - 2))

            def values(w):
                nonlocal free6
                b, half = divmod(w, 2)
                G, i = divmod(b, GB)
                for n in range(UH):
                    g, j = 2 * half + n // 4, n % 4
                    t = do("tensor", lambda e, n=n, g=g, j=j: e.matmul(
                        ps[32 * g:32 * g + 32, 6, i * S:(i + 1) * S], vX[:, G % 2, i, g, j, :],
                        pT[:, w % 2, n, :], start=j == 0, stop=j == 3), pt_ready[w], free6, tell=n == UH - 1)
                av_done[w] = t
                if half == 1 and i == GB - 1:
                    av_last[G] = t
                    free6 = c_done[G] = do("scalar", lambda e: e.copy(cT[:, G % 2, :], ps[:, 6, :]),
                                           t, cT_used[G % 2])
                    if not differential:
                        return
                    s = G % 2
                    l1 = sums[:, s, 0, :, :].rearrange("p b h -> p (b h)").unsqueeze(2).broadcast_to(
                        [P, GB * 16, VD])
                    tl = do("vector", lambda e: e.scalar_tensor_tensor(
                        lsq[:, s, :, :].rearrange("p b (h d) -> p (b h) d", d=VD), l1, EPS, l1,
                        ALU.mult, ALU.mult), cN_used[s])
                    tq = do("gpsimd", lambda e: e.tensor_tensor(sq[:, s, :], cT[:, s, :], cT[:, s, :], ALU.mult),
                            c_done[G], cN_used[s])
                    c_done[G] = tq
                    lsq_done[G] = tl

            lsq_done = [None] * NG

            def rms(G):
                nonlocal free7
                s = G % 2
                t = do("tensor", lambda e: e.matmul(ps[:, 7, :], mean8, sq[:, s, :], start=True, stop=False),
                       c_done[G], free7, tell=False)
                for i in range(GB):
                    t = do("tensor", lambda e, i=i: e.matmul(
                        ps[:, 7, i * S:(i + 1) * S], lsq[:, s, i, :], ident, start=False, stop=i == GB - 1),
                        lsq_done[G], tell=i == GB - 1)
                free7 = t = do("scalar", lambda e: e.activation(rr[:, s, :], ps[:, 7, :], ACT.Ln), t, cN_used[s])
                t = do("scalar", lambda e: e.activation(rr[:, s, :], rr[:, s, :], ACT.Exp, scale=-0.5), t)
                c_done[G] = do("vector", lambda e: e.scalar_tensor_tensor(
                    cN[:, s, :], cT[:, s, :], sub_w[:, 0:1], rr[:, s, :], ALU.mult, ALU.mult), t, t_sub, cN_used[s])

            def context_out(G):
                nonlocal free7
                s = G % 2
                src = cN if differential else cT
                for i in range(GB):
                    t = do("tensor", lambda e, i=i: e.matmul(
                        ps[:, 7, i * C:(i + 1) * C], src[:, s, i * S:(i + 1) * S], W(name + "_o"),
                        start=True, stop=True), c_done[G], free7, tell=i == GB - 1)
                cT_used[s] = cN_used[s] = t
                b = rows[:, (2 if differential else 1):(3 if differential else 2), :].broadcast_to([P, GB, C])
                g = group(G)
                t2 = do("gpsimd", lambda e: e.tensor_tensor(x_tok[:, g, :], x_tok[:, g, :], b, ALU.add),
                        x_done[G], l_rows)
                E.wait("vector", t2)
                free7, pend[G] = residual(G, bank4(7), t)

            def finish(G):
                nonlocal free7
                x_done[G] = normalize(G, pend[G])
                free7 = xT_done[G] = renew_xT(G, x_done[G], 7, free7)

            if differential:
                lam_init = 0.8 - 0.6 * math.exp(-0.3 * 4)
                lw = sb(name + "_lw", [P, 12], scope=scope)
                neg_lam = sb(name + "_neg_lam", [P, 1], scope=scope)
                sub_w = sb(name + "_sub_w", [P, 1], scope=scope)
                for a in range(2):
                    ta = do("vector", lambda e, a=a: e.tensor_tensor(
                        lw[:, 4 * a:4 * a + 4], lams[:, 2 * a, :], lams[:, 2 * a + 1, :], ALU.mult), l_lams)
                for a in range(2):
                    tb = do("vector", lambda e, a=a: e.tensor_reduce(
                        lw[:, 8 + a:9 + a], lw[:, 4 * a:4 * a + 4], AX.X, ALU.add), ta)
                tc = do("scalar", lambda e: e.activation(lw[:, 10:12], lw[:, 8:10], ACT.Exp), tb)
                td = do("vector", lambda e: e.tensor_scalar(lw[:, 8:9], lw[:, 10:11], lam_init, -1.0,
                                                            ALU.add, ALU.mult), tc)
                t_lam = do("vector", lambda e: e.tensor_tensor(neg_lam[:, :], lw[:, 8:9], lw[:, 11:12], ALU.add), td)
                t_sub = do("vector", lambda e: e.tensor_scalar(sub_w[:, :], col("subln_w"), 1.0 - lam_init, None,
                                                               ALU.mult))
            else:
                kbias = sb(name + "_kbias", [P, 4], scope=scope)
                t_kbias = do("vector", lambda e: e.tensor_scalar(kbias[:, :], picks[:, 2:6], col("xk_b"), None,
                                                                 ALU.mult))

            for k in range(3):
                project(0, k)
            per = 2 * GB
            LT, LV = 2, 3
            for w in range(NW + per + LV):
                j, G = w % per, w // per
                if w < NW:
                    scores(w)
                if LT <= w < NW + LT:
                    turn_p(w - LT)
                if w < NW:
                    exponentials(w)
                if j in (1, 2, 3) and G + 1 < NG and w < NW:
                    project(G + 1, j - 1)
                if 1 <= w <= NW:
                    normalizers(w - 1)
                if LV <= w < NW + LV:
                    values(w - LV)
                if differential and G >= 1 and j == 4 and G - 1 < NG:
                    rms(G - 1)
                if G >= 1 and j == 6 and G - 1 < NG:
                    context_out(G - 1)
                if (G >= 1 and j == 7) and G - 1 < NG:
                    finish(G - 1)
            E.join()
            scope.close()

        def experts(name, G, src_T, ready, gate, up, down, NE, NI, weight, hS, sG, acc, acc_ready, w_ready, st):
            NC = NI // P
            for ex in range(NE):
                for c in range(NC):
                    k = st["k"]
                    st["k"] += 1
                    bg, bu = (k % 3) * 2, (k % 3) * 2 + 1
                    tg = do("tensor", lambda e, c=c, ex=ex, bg=bg: e.matmul(
                        ps[:, bg, :], gate[:, ex, c * P:(c + 1) * P], src_T, start=True, stop=True),
                        ready, st["free"][bg])
                    tu = do("tensor", lambda e, c=c, ex=ex, bu=bu: e.matmul(
                        ps[:, bu, :], up[:, ex, c * P:(c + 1) * P], src_T, start=True, stop=True),
                        st["free"][bu])
                    sl = k % 3
                    st["free"][bg] = ts = do("scalar", lambda e, bg=bg, sl=sl: e.activation(
                        sG[:, sl, :], ps[:, bg, :], ACT.Silu), tg, st["sg"][sl])
                    hp = (ex % 2) * NC + c
                    st["free"][bu] = st["sg"][sl] = th = do("vector", lambda e, bu=bu, sl=sl, hp=hp:
                        e.tensor_tensor(hS[:, hp, :], sG[:, sl, :], ps[:, bu, :], ALU.mult),
                        ts, tu, st["h"][ex % 2])
                if st["todo"]:
                    st["todo"].pop()()

                def down_product(ex=ex, th=th):
                    bank = 6 + st["y"] % 2
                    st["y"] += 1
                    for i in range(GB):
                        for c in range(NC):
                            t = do("tensor", lambda e, i=i, c=c: e.matmul(
                                ps[:, bank, i * C:(i + 1) * C], hS[:, (ex % 2) * NC + c, i * S:(i + 1) * S],
                                down[:, ex, c, :], start=c == 0, stop=c == NC - 1),
                                th, st["free"][bank], tell=(i == GB - 1 and c == NC - 1))
                    st["h"][ex % 2] = t
                    for i in range(GB):
                        t2 = do("vector", lambda e, i=i: e.scalar_tensor_tensor(
                            acc[:, i, :], ps[:, bank, i * C:(i + 1) * C], weight(G * GB + i, ex), acc[:, i, :],
                            ALU.mult, ALU.add), t, acc_ready, w_ready, st["acc"])
                    st["acc"] = st["free"][bank] = t2
                st["todo"].append(down_product)

        def new_state():
            return {"k": 0, "y": 0, "free": [None] * 8, "sg": [None] * 3, "h": [None] * 2, "todo": [], "acc": None}

        def moe_top2():
            scope = ExitStack()
            E.stage("moe")
            NT = 2 * NB + NE0
            NX = 4
            rows_d = nc.dram_tensor("moe_rows", (NB * S, C), F32, kind="Internal").ap()
            y_d = nc.dram_tensor("moe_y", (2 * NB * S, C), F32, kind="Internal").ap()
            hB = sb("moe_hB", [P, 3, GB, C], scope=scope)
            n1 = sb("moe_n", [P, 2, GB, C], scope=scope)
            n2 = sb("moe_n2", [P, 3, GB, C], scope=scope)
            nT = sb("moe_nT", [P, 2, GB, S], scope=scope)
            tT = sb("moe_tT", [P, 2, GN], scope=scope)
            lg = sb("moe_logits", [P, NB, NE0], scope=scope)
            free = [None] * 8
            xh_done, row_store = [None] * NG, [None] * NG
            l1_done, l2_done, n1_used, nT_used = [None] * NG, [None] * NG, [None] * 2, [None] * 2
            h_done, tT_used, n2_used = [None] * NG, [None] * 2, [None] * 3

            def stats_of(src, G, ready, *waits):
                for i in range(GB):
                    t = do("vector", lambda e, i=i, tile=src(i): e.bn_stats(stats[:, G * GB + i, :], tile), ready, *waits)
                for i in range(GB):
                    t2 = do("vector", lambda e, i=i: e.bn_aggr(mv[:, G * GB + i, :], stats[:, G * GB + i, :]), t)
                g = group(G)
                t3 = do("gpsimd", lambda e: e.tensor_scalar(veps[:, g], mv[:, g, 1], EPS, None, ALU.add), t2)
                return do("gpsimd", lambda e: e.tensor_tensor(rstd[:, g], veps[:, g], minus_half[:, 0:GB],
                                                              ALU.pow), t3, t_half)

            def normal(dst, src, G, ready, *waits):
                for i in range(GB):
                    b = G * GB + i
                    t = do("vector", lambda e, b=b, to=dst(i), tile=src(i): e.tensor_scalar(
                        to, tile, mv[:, b, 0:1], rstd[:, b:b + 1], ALU.subtract, ALU.mult), ready, *waits)
                return t

            def first_norm(G):
                s = G % 2
                t = normal(lambda i: n1[:, s, i, :], lambda i: x_tok[:, G * GB + i, :], G, l1_done[G], n1_used[s])
                n1_used[s] = t = turn(lambda i: n1[:, s, i, :], s, t, free[s])
                free[s] = t = do("scalar", lambda e: e.activation(
                    nT[:, s, :, :], bank4(s), ACT.Identity, scale=col("ln1_g"), bias=col("ln1_b")), t, nT_used[s])
                for i in range(GB):
                    t4 = do("tensor", lambda e, i=i: e.matmul(ps[:, 2 + s, i * C:(i + 1) * C], nT[:, s, i, :],
                                                              W("attn_w"), start=True, stop=True),
                            t, free[2 + s], tell=i == GB - 1)
                nT_used[s] = t4
                g = group(G)
                h_done[G] = t5 = do("vector", lambda e: e.tensor_tensor(
                    hB[:, G % 3, :, :], bank4(2 + s), x_tok[:, g, :], ALU.add), t4)
                free[2 + s] = xh_done[G] = do("vector", lambda e: e.scalar_tensor_tensor(
                    x_tok[:, g, :], x_tok[:, g, :], 2.0, bank4(2 + s), ALU.mult, ALU.add), t5)
                l2_done[G] = stats_of(lambda i: hB[:, G % 3, i, :], G, h_done[G])

            def second_norm(G):
                s = G % 2
                t = normal(lambda i: n2[:, G % 3, i, :], lambda i: hB[:, G % 3, i, :], G, l2_done[G], row_store[G - 3] if G >= 3 else None)
                row_store[G] = E.dma("sync", f"rows{G}", rows_d[G * GN:(G + 1) * GN, :].rearrange(
                    "(b t) c -> t b c", b=GB), n2[:, G % 3, :, :], t)
                t = turn(lambda i: n2[:, G % 3, i, :], 4 + s, t, free[4 + s])
                free[4 + s] = t = do("scalar", lambda e: e.activation(
                    tT[:, s, :], ps[:, 4 + s, :], ACT.Identity, scale=col("ln2_g"), bias=col("ln2_b")), t, tT_used[s])
                for i in range(GB):
                    t = do("tensor", lambda e, i=i: e.matmul(
                        ps[:, 6, (G * GB + i) * 8:(G * GB + i) * 8 + 8], tT[:, s, i * S:(i + 1) * S],
                        gates[:, 0, :], start=True, stop=True), t, l_gates, tell=i == GB - 1)
                tT_used[s] = t
                return t

            for G in range(NG + 2):
                if G < NG:
                    l1_done[G] = stats_of(lambda i: x_tok[:, G * GB + i, :], G, x_done[G])
                if 1 <= G <= NG:
                    first_norm(G - 1)
                if G >= 2:
                    t_logits = second_norm(G - 2)

            weight = sb("rt_weight", [P, 2, NB], scope=scope)
            exp_i = sb("rt_exp_i", [1, NT], mybir.dt.int32, scope=scope)
            src_i = sb("rt_src", [P, NT], mybir.dt.int32, scope=scope)
            dst_i = sb("rt_dst", [P, NT], mybir.dt.int32, scope=scope)
            r_scope = ExitStack()
            wk = sb("rt_work", [P, 8, NB, NE0], scope=r_scope)
            sc = sb("rt_scalars", [P, 2, NB], scope=r_scope)
            slot = sb("rt_slot", [P, 2, NB], scope=r_scope)
            slot_i = sb("rt_slot_i", [P, 2, NB], mybir.dt.int32, scope=r_scope)
            hi = sb("rt_hi", [P, 2, NB], scope=r_scope)
            lo = sb("rt_lo", [P, 2, NB], scope=r_scope)
            tl = sb("rt_tiles", [P, 6, NE0], scope=r_scope)
            cmp32 = sb("rt_cmp", [P, NE0, NB], scope=r_scope)
            cmpT = sb("rt_cmpT", [1, NT, NE0], scope=r_scope)
            exp_f = sb("rt_exp_f", [1, NT], scope=r_scope)
            hotL = sb("rt_hotL", [P, 8, P], mybir.dt.float16, scope=r_scope)
            hotH = sb("rt_hotH", [P, 8, NT], mybir.dt.float16, scope=r_scope)
            inv = sb("rt_inv", [P, 6, NT], scope=r_scope)
            v = lambda f, *w: do("vector", f, *w)
            B3 = [P, NB, NE0]
            eio = iotas[:, 0:NE0].unsqueeze(1).broadcast_to(B3)
            over_e = lambda x: x.unsqueeze(2).broadcast_to(B3)
            over_b = lambda x: x.unsqueeze(1).broadcast_to(B3)
            flat = lambda x: x.rearrange("p b e -> p (b e)")
            logits, oh1, oh2, rest = lg[:, :, :], wk[:, 0, :, :], wk[:, 1, :, :], wk[:, 2, :, :]
            tmp0, tmp1, scanA, scanB = wk[:, 3, :, :], wk[:, 4, :, :], wk[:, 5, :, :], wk[:, 6, :, :]
            a = v(lambda e: e.tensor_copy(lg[:, :, :], ps[:, 6, 0:NB * 8].rearrange("p (b e) -> p b e", b=NB)), t_logits)

            def first_max(src, onehot, top, a):
                a = v(lambda e: e.tensor_reduce(top, src, AX.X, ALU.max), a)
                a = v(lambda e: e.tensor_tensor(tmp0, src, over_e(top), ALU.is_lt), a)
                a = v(lambda e: e.scalar_tensor_tensor(tmp1, tmp0, 100.0, eio, ALU.mult, ALU.add), a, l_picks)
                a = v(lambda e: e.tensor_reduce(hi[:, 0, :], tmp1, AX.X, ALU.min), a)
                return v(lambda e: e.tensor_tensor(onehot, eio, over_e(hi[:, 0, :]), ALU.is_equal), a)
            a = first_max(logits, oh1, sc[:, 0, :], a)
            a = v(lambda e: e.scalar_tensor_tensor(flat(rest), flat(oh1), -3.0e38, flat(logits), ALU.mult, ALU.add), a)
            a = first_max(rest, oh2, sc[:, 1, :], a)
            a = v(lambda e: e.tensor_tensor(tmp0, oh1, oh2, ALU.add), a)
            tb = do("tensor", lambda e: e.matmul(ps[:, 0, 0:NB * 8], below, flat(tmp0), start=True, stop=True), a)
            tt = do("tensor", lambda e: e.matmul(ps[:, 1, 0:NB * 8], ones, flat(tmp0), start=True, stop=True), a)
            totals = ps[:, 1, 0:NB * 8].rearrange("p (b e) -> p b e", b=NB)
            within = ps[:, 0, 0:NB * 8].rearrange("p (b e) -> p b e", b=NB)
            a = v(lambda e: e.tensor_tensor(lo[:, 0, :], sc[:, 1, :], sc[:, 0, :], ALU.subtract), a)
            ex = do("scalar", lambda e: e.activation(lo[:, 1, :], lo[:, 0, :], ACT.Exp), a)
            a = v(lambda e: e.tensor_copy(scanA, totals), tt)
            src, dst, sh = scanA, scanB, 1
            while sh < NB:
                v(lambda e, s=src, d=dst, sh=sh: e.tensor_copy(d[:, 0:sh, :], s[:, 0:sh, :]), a)
                a = v(lambda e, s=src, d=dst, sh=sh: e.tensor_tensor(
                    d[:, sh:NB, :], s[:, sh:NB, :], s[:, 0:NB - sh, :], ALU.add), a)
                src, dst, sh = dst, src, 2 * sh
            incl = src
            count, ntile, base, base2 = [tl[:, i, :] for i in range(4)]
            a = v(lambda e: e.tensor_scalar(count, incl[:, NB - 1, :], 1.0 / P, None, ALU.mult), a)
            a = v(lambda e: e.tensor_tensor(cmp32[:, :, :], iotas[:, 0:NB].unsqueeze(1).broadcast_to([P, NE0, NB]),
                                            count.unsqueeze(2).broadcast_to([P, NE0, NB]), ALU.is_lt), a)
            a = v(lambda e: e.tensor_reduce(ntile, cmp32[:, :, :], AX.X, ALU.add), a)
            z, y = ntile, base
            bufs, sh = [base, base2], 1
            while sh < NE0:
                d = bufs[0]
                v(lambda e, z=z, d=d, sh=sh: e.tensor_copy(d[:, 0:sh], z[:, 0:sh]), a)
                a = v(lambda e, z=z, d=d, sh=sh: e.tensor_tensor(d[:, sh:NE0], z[:, sh:NE0], z[:, 0:NE0 - sh],
                                                                 ALU.add), a)
                z, bufs, sh = d, bufs[::-1], 2 * sh
            end = z
            a = v(lambda e: e.tensor_tensor(
                cmpT[:, :, :], iotas[0:1, 0:NT].unsqueeze(2).broadcast_to([1, NT, NE0]),
                end[0:1, :].unsqueeze(1).broadcast_to([1, NT, NE0]), ALU.is_ge), a)
            a = v(lambda e: e.tensor_reduce(exp_f[:, :], cmpT[:, :, :], AX.X, ALU.add), a)
            a = v(lambda e: e.tensor_scalar(exp_f[:, :], exp_f[:, :], float(NE0 - 1), float(I0), ALU.min, ALU.mult), a)
            t_exp = v(lambda e: e.tensor_copy(exp_i[:, :], exp_f[:, :]), a)
            start = tl[:, 4, :]
            a = v(lambda e: e.tensor_tensor(tl[:, 5, :], end, ntile, ALU.subtract), t_exp)
            a = v(lambda e: e.tensor_scalar(start, tl[:, 5, :], float(P), None, ALU.mult), a)
            a = v(lambda e: e.tensor_tensor(tmp0, incl, totals, ALU.subtract), a)
            a = v(lambda e: e.tensor_tensor(tmp1, tmp0, within, ALU.add), a, tb)
            a = v(lambda e: e.tensor_tensor(tmp0, tmp1, over_b(start), ALU.add), a)
            a1 = v(lambda e: e.tensor_tensor(tmp1, tmp0, oh1, ALU.mult), a)
            a2 = v(lambda e: e.tensor_tensor(rest, tmp0, oh2, ALU.mult), a)
            a = v(lambda e: e.tensor_reduce(slot[:, 0, :], tmp1, AX.X, ALU.add), a1)
            a = v(lambda e: e.tensor_reduce(slot[:, 1, :], rest, AX.X, ALU.add), a2, a)
            a = v(lambda e: e.tensor_copy(slot_i[:, :, :], slot[:, :, :]), a)
            a = v(lambda e: e.tensor_single_scalar(slot_i[:, :, :], slot_i[:, :, :], 7, ALU.arith_shift_right), a)
            a = v(lambda e: e.tensor_scalar(weight[:, 0, :], lo[:, 1, :], 1.0, None, ALU.add), a, ex)
            a = v(lambda e: e.reciprocal(weight[:, 0, :], weight[:, 0, :]), a)
            t_w = v(lambda e: e.tensor_tensor(weight[:, 1, :], weight[:, 0, :], lo[:, 1, :], ALU.mult), a)
            a = v(lambda e: e.tensor_copy(hi[:, :, :], slot_i[:, :, :]), t_w)
            a = v(lambda e: e.scalar_tensor_tensor(
                lo[:, :, :].rearrange("p k b -> p (k b)"), hi[:, :, :].rearrange("p k b -> p (k b)"), -float(P),
                slot[:, :, :].rearrange("p k b -> p (k b)"), ALU.mult, ALU.add), a)
            HB = NB // 2
            hot_used = [None] * 8
            n = 0
            for k in range(2):
                for b in range(NB):
                    i = n % 8
                    tl_ = v(lambda e, i=i, k=k, b=b: e.tensor_scalar(
                        hotL[:, i, :], iota16[:, 0:P], lo[:, k, b:b + 1], None, ALU.is_equal), a, hot_used[i], t_i16)
                    th_ = v(lambda e, i=i, k=k, b=b: e.tensor_scalar(
                        hotH[:, i, :], iota16[:, 0:NT], hi[:, k, b:b + 1], tokens[:, b % HB:b % HB + 1],
                        ALU.is_equal, ALU.mult), a, hot_used[i])
                    r = 2 * k + b // HB
                    hot_used[i] = t = do("tensor", lambda e, i=i, r=r, b=b: e.matmul(
                        ps[:, 2, r * NT:(r + 1) * NT], hotL[:, i, :], hotH[:, i, :],
                        start=b % HB == 0, stop=b % HB == HB - 1), th_)
                    n += 1
            q = lambda i: inv[:, i, :]
            part = lambda r: ps[:, 2, r * NT:(r + 1) * NT]
            a = v(lambda e: e.tensor_copy(q(0), part(1)), t)
            a = v(lambda e: e.tensor_tensor(q(1), q(0), part(3), ALU.add), a)
            b_ = v(lambda e: e.tensor_copy(q(2), part(2)), a)
            b_ = v(lambda e: e.tensor_tensor(q(3), q(2), part(3), ALU.add), b_)
            a = v(lambda e: e.tensor_tensor(q(0), q(1), part(0), ALU.add), b_)
            a = v(lambda e: e.tensor_tensor(q(0), q(0), q(2), ALU.add), a)
            a = v(lambda e: e.tensor_scalar(q(1), q(1), 0.0, float(NB * S // 2), ALU.is_gt, ALU.mult), a)
            a = v(lambda e: e.tensor_tensor(q(1), q(1), q(0), ALU.add), a)
            a = v(lambda e: e.tensor_scalar(q(2), q(1), -1.0, 0.0, ALU.add, ALU.max), a)
            t_src = v(lambda e: e.tensor_copy(src_i[:, :], q(2)), a)
            a = v(lambda e: e.tensor_scalar(q(3), q(3), 0.0, float(NB * S), ALU.is_gt, ALU.mult), t_src)
            a = v(lambda e: e.tensor_tensor(q(3), q(3), q(2), ALU.add), a)
            a = v(lambda e: e.tensor_scalar(q(4), q(1), 0.0, 4.0 * NB * S, ALU.is_le, ALU.mult), a)
            a = v(lambda e: e.tensor_tensor(q(4), q(4), q(3), ALU.add), a)
            t_dst = v(lambda e: e.tensor_copy(dst_i[:, :], q(4)), a)
            E.join()
            r_scope.close()

            xg = sb("tile_x", [P, NX, C], scope=scope)
            xgT = sb("tile_xT", [P, NX, P], scope=scope)
            gS = sb("tile_g", [P, 2, I0], scope=scope)
            hS = sb("tile_h", [P, 2, I0], scope=scope)
            hT = sb("tile_hT", [P, 2, I0], scope=scope)
            yS = sb("tile_y", [P, NX, C], scope=scope)
            KC = I0 // P
            gate_f, up_f, down_f = [expert_w[:, i * n0:(i + 1) * n0] for i in range(3)]
            got, stored, yready = [None] * NT, [None] * NT, [None] * NT
            bfree = [None] * 8
            xT_ready, h_ready, hT_ready, xT_used, hT_used, xg_used, gS_used = [
                [None] * NT for _ in range(7)]
            at = {}

            def before(tokens, i):
                return tokens[i] if i >= 0 else None

            gather_sem = [E.sem(f"gathered{i}") for i in range(NX)]
            scatter_sem = [E.sem(f"scattered{i}") for i in range(NX)]

            def gather(j):
                i = j % NX
                E.queue["gpsimd"].append([
                    [w for w in (t_src, before(xg_used, j - NX), *(row_store if j == 0 else ())) if w],
                    lambda e: e.indirect_dma_start(
                        out=xg[:, i, :], out_offset=None, in_=rows_d,
                        in_offset=bass.IndirectOffsetOnAxis(ap=src_i[:, j:j + 1], axis=0)),
                    gather_sem[i], 16])
                got[j] = (gather_sem[i], 16 * (j // NX + 1))

            def tile_turn(j):
                i = j % NX
                xg_used[j] = t = do("tensor", lambda e: e.transpose(ps[:, 6, 0:P], xg[:, i, :], ident),
                                    got[j], bfree[6])
                bfree[6] = xT_ready[j] = do("scalar", lambda e: e.activation(
                    xgT[:, i, :], ps[:, 6, 0:P], ACT.Identity, scale=col("ln2_g"), bias=col("ln2_b")),
                    t, before(xT_used, j - NX))

            def tile_offset(j):
                def load(e):
                    at[j] = e.value_load(exp_i[0:1, j:j + 1], min_val=0, max_val=(NE0 - 1) * I0)
                E.queue["tensor"].append([[t_exp], load, None, 0])

            def tile_gate_up(j):
                bg, bu = (0, 1) if j % 2 == 0 else (2, 3)
                i = j % NX
                tg = do("tensor", lambda e: e.matmul(ps[:, bg, :], xgT[:, i, :], gate_f[:, bass.ds(at[j], I0)],
                                                     start=True, stop=True), xT_ready[j], bfree[bg])
                xT_used[j] = tu = do("tensor", lambda e: e.matmul(
                    ps[:, bu, :], xgT[:, i, :], up_f[:, bass.ds(at[j], I0)], start=True, stop=True), bfree[bu])
                bfree[bg] = t = do("scalar", lambda e: e.activation(gS[:, j % 2, :], ps[:, bg, :], ACT.Silu),
                                   tg, before(h_ready, j - 2))
                bfree[bu] = h_ready[j] = do("vector", lambda e: e.tensor_tensor(
                    hS[:, j % 2, :], gS[:, j % 2, :], ps[:, bu, :], ALU.mult), t, tu, before(hT_used, j - 2))

            def tile_turn_h(j):
                for k in range(KC):
                    t = do("tensor", lambda e, k=k: e.transpose(
                        ps[:, 4 + j % 2, k * P:(k + 1) * P], hS[:, j % 2, k * P:(k + 1) * P], ident),
                        h_ready[j], bfree[4 + j % 2], tell=k == KC - 1)
                hT_used[j] = t
                bfree[4 + j % 2] = hT_ready[j] = do("scalar", lambda e: e.copy(hT[:, j % 2, :], ps[:, 4 + j % 2, :]),
                                                    t, before(yready, j - 2))

            def tile_down(j):
                for k in range(KC):
                    t = do("tensor", lambda e, k=k: e.matmul(
                        ps[:, 7, 0:C], hT[:, j % 2, k * P:(k + 1) * P],
                        down_f[:, k * P:n0 - (KC - 1 - k) * P][:, bass.ds(at[j], C)],
                        start=k == 0, stop=k == KC - 1), hT_ready[j], bfree[7], tell=k == KC - 1)
                yready[j] = t
                i = j % NX
                bfree[7] = t2 = do("vector", lambda e: e.tensor_copy(yS[:, i, :], ps[:, 7, 0:C]), t,
                                   before(stored, j - NX))
                E.queue["gpsimd"].append([[t2, t_dst], lambda e: e.indirect_dma_start(
                    out=y_d, out_offset=bass.IndirectOffsetOnAxis(ap=dst_i[:, j:j + 1], axis=0),
                    in_=yS[:, i, :], in_offset=None, bounds_check=2 * NB * S - 1, oob_is_err=False),
                    scatter_sem[i], 16])
                stored[j] = (scatter_sem[i], 16 * (j // NX + 1))

            for l in l_moe0:
                E.wait("tensor", l)
            for j in range(3):
                gather(j)
            tile_turn(0)
            tile_offset(0)
            for j in range(NT + 2):
                if j < NT:
                    tile_gate_up(j)
                    if j + 1 < NT:
                        tile_offset(j + 1)
                if j + 1 < NT:
                    tile_turn(j + 1)
                if 1 <= j <= NT:
                    tile_turn_h(j - 1)
                if j >= 2:
                    tile_down(j - 2)
                if j + 3 < NT:
                    gather(j + 3)
            E.wait("sync", *stored[-NX:])

            y2 = sb("moe_y2", [P, 3, 2, GB, C], scope=scope)
            fin = [None] * NG
            for G in range(NG + 1):
                if G < NG:
                    s = G % 3
                    ly = [E.dma("sync", f"y{G}_{k}", y2[:, s, k, :, :],
                                y_d[k * NB * S + G * GN:k * NB * S + (G + 1) * GN, :].rearrange(
                                    "(b t) c -> t b c", b=GB), fin[G - 3] if G >= 3 else None) for k in range(2)]
                    for k in range(2):
                        for i in range(GB):
                            b = G * GB + i
                            t = do("vector", lambda e, k=k, i=i, b=b, s=s: e.scalar_tensor_tensor(
                                x_tok[:, b, :], y2[:, s, k, i, :], weight[:, k, b:b + 1], x_tok[:, b, :],
                                ALU.mult, ALU.add), ly[k], t_w, xh_done[G], t if k else None)
                    fin[G] = layer_stats(G, t)
                if G >= 1:
                    g = G - 1
                    x_done[g] = normalize(g, fin[g])
                    xT_done[g] = bfree[g % 2] = renew_xT(g, x_done[g], g % 2, bfree[g % 2])
            E.join()
            scope.close()

        def memory():
            scope = ExitStack()
            E.stage("memory")
            n1 = NE1 * I1
            w1 = expert_w[:, 0:n1].rearrange("p (e i) -> p e i", e=NE1)
            w3 = expert_w[:, n1:2 * n1].rearrange("p (e i) -> p e i", e=NE1)
            w2 = expert_w[:, 2 * n1:3 * n1].rearrange("p (e k c) -> p e k c", e=NE1, c=C)
            l_moe1 = [E.dma("sync", "w1_T", w1, D["w1_T"]), E.dma("sync", "w3_T", w3, D["w3_T"]),
                      E.dma("sync", "w2_T", w2, D["w2_T"])]
            wc = sb("mem_wc", [P, P], scope=scope)
            sm = sb("mem_scalars", [P, 6], scope=scope)
            mT = sb("mem_mask", [P, P], scope=scope)
            mT0 = sb("mem_exp", [P, P], scope=scope)
            vC = sb("mem_v", [P, 2, GB, C], scope=scope)
            sM = sb("mem_s", [P, 2, GB, S], scope=scope)
            a = do("scalar", lambda e: e.activation(sm[:, 0:1], col("decay"), ACT.Exp, scale=-1.0))
            b_ = do("scalar", lambda e: e.activation(sm[:, 4:5], col("log_alpha"), ACT.Exp))
            a = do("vector", lambda e: e.tensor_scalar(sm[:, 1:2], sm[:, 0:1], 1.0, None, ALU.add), a)
            a = do("vector", lambda e: e.reciprocal(sm[:, 2:3], sm[:, 1:2]), a)
            a = do("scalar", lambda e: e.activation(sm[:, 3:4], sm[:, 2:3], ACT.Ln), a)
            a = do("scalar", lambda e: e.activation(mT0[:, :], diffs, ACT.Exp, scale=sm[:, 3:4]), a)
            t_mask = do("vector", lambda e: e.tensor_tensor(mT[:, :], mT0[:, :], causal, ALU.mult), a)
            t = do("tensor", lambda e: e.matmul(ps[:, 7, 0:P], W("w_write"), W("w_read"), start=True, stop=True))
            t_wc = do("vector", lambda e: e.tensor_scalar(wc[:, :], ps[:, 7, 0:P], sm[:, 4:5], None, ALU.mult),
                      t, b_)
            free = [None] * 8
            s_used, pend = [None] * 2, [None] * NG
            s_ready, v_ready = [None] * NG, [None] * NG
            for G in range(NG + 2):
                if G < NG:
                    s = G % 2
                    for i in range(GB):
                        t = do("tensor", lambda e, i=i, G=G, s=s: e.matmul(
                            ps[:, s, i * C:(i + 1) * C], x_T[:, G * GB + i, :], wc[:, :], start=True, stop=True),
                            t_wc, free[s], tell=i == GB - 1)
                    v_ready[G] = free[s] = do("scalar", lambda e, s=s: e.copy(vC[:, s, :, :], bank4(s)), t, s_used[s])
                    for i in range(GB):
                        c0 = 8 + (G * GB + i) * S
                        t = do("tensor", lambda e, i=i, G=G, s=s, c0=c0: e.matmul(
                            ps[:, 2 + s, i * S:(i + 1) * S], x_Tp[:, c0 - 1:c0 - 1 + S],
                            x_T[:, G * GB + i, :], start=True, stop=True), free[2 + s], t_pad, tell=i == GB - 1)
                    mb = mT[:, :].unsqueeze(1).broadcast_to([P, GB, S])
                    s_ready[G] = free[2 + s] = do("vector", lambda e, s=s: e.tensor_tensor(
                        sM[:, s, :, :], bank4(2 + s), mb, ALU.mult), t, t_mask, s_used[s])
                if G >= 1 and G - 1 < NG:
                    g = G - 1
                    s = g % 2
                    for i in range(GB):
                        t = do("tensor", lambda e, i=i, s=s: e.matmul(
                            ps[:, 4 + s, i * C:(i + 1) * C], sM[:, s, i, :], vC[:, s, i, :], start=True, stop=True),
                            s_ready[g], v_ready[g], free[4 + s], tell=i == GB - 1)
                    s_used[s] = t
                    free[4 + s], pend[g] = residual(g, bank4(4 + s), t, 2.0)
                if G >= 2:
                    g = G - 2
                    x_done[g] = normalize(g, pend[g])
            for g in range(NG):
                xT_done[g] = free[6 + g % 2] = renew_xT(g, x_done[g], 6 + g % 2, free[6 + g % 2])
            E.join()
            scope.close()
            return w1, w3, w2, l_moe1

        def expert_choice(w1, w3, w2, l_moe1):
            scope = ExitStack()
            E.stage("choice")
            NS = NB * NE1
            K = 26
            scS = sb("ch_scores", [P, NE1, NB], scope=scope)
            wk = sb("ch_work", [P, 6, NE1, NB], scope=scope)
            sm = sb("ch_small", [P, 16, NE1], scope=scope)
            half = sb("ch_halves", [P, K + 1], scope=scope)
            wgt = sb("ch_weights", [P, NE1, NB], scope=scope)
            hS = sb("ch_h", [P, 4, GN], scope=scope)
            sG = sb("ch_s", [P, 3, GN], scope=scope)
            for b in range(NB):
                t = do("tensor", lambda e, b=b: e.matmul(ps[:, 0, b * 8:b * 8 + 8], x_T[:, b, :], gates[:, 1, :],
                                                         start=True, stop=True), tell=b == NB - 1)
            v = lambda f, *w: do("vector", f, *w)
            p = lambda f, *w: do("gpsimd", f, *w)
            a = v(lambda e: e.tensor_copy(scS[:, :, :].rearrange("p e b -> p b e"),
                                          ps[:, 0, 0:NS].rearrange("p (b e) -> p b e", b=NB)), t)
            S_ = scS[:, :, :]
            r_ = lambda i: sm[:, i, :]
            bc = lambda x: x.unsqueeze(2).broadcast_to([P, NE1, NB])
            a1 = v(lambda e: e.tensor_reduce(r_(0), S_, AX.X, ALU.max), a)
            a2 = v(lambda e: e.tensor_reduce(r_(1), S_, AX.X, ALU.max, apply_absolute_value=True), a)
            m1 = p(lambda e: e.partition_all_reduce(r_(2), r_(0), P, RMAX), a1)
            m2 = p(lambda e: e.partition_all_reduce(r_(3), r_(1), P, RMAX), a2)
            lo, hi, mid, mx, big = r_(4), r_(5), r_(6), r_(2), r_(3)
            a3 = v(lambda e: e.tensor_reduce(sm[:, 7, 0:1], big, AX.X, ALU.max), m2)
            a4 = v(lambda e: e.tensor_scalar(lo, big, 0.0, sm[:, 7, 0:1], ALU.mult, ALU.subtract), a3)
            a5 = v(lambda e: e.tensor_scalar(hi, lo, -1.001, 1e-30, ALU.mult, ALU.add), a4)
            a6 = v(lambda e: e.tensor_scalar(half[:, 0:1], sm[:, 7, 0:1], 1.0, None, ALU.mult), a5)
            for k in range(K):
                a6 = v(lambda e, k=k: e.tensor_scalar(half[:, k + 1:k + 2], half[:, k:k + 1], 0.5, None, ALU.mult), a6)
            cur = v(lambda e: e.tensor_scalar(mid, lo, half[:, 0:1], None, ALU.add), a6)
            hdone = None
            for k in range(K):
                g = v(lambda e: e.tensor_tensor(wk[:, 0, :, :], S_, bc(mid), ALU.is_ge), cur)
                g = v(lambda e: e.tensor_reduce(r_(8), wk[:, 0, :, :], AX.X, ALU.add), g)
                g = do("tensor", lambda e: e.matmul(ps[:, 1, 0:NE1], ones, r_(8), start=True, stop=True), g)
                g1 = v(lambda e: e.tensor_scalar(r_(9), ps[:, 1, 0:NE1], float(CAP), 1e30, ALU.is_ge, ALU.mult), g, hdone)
                g2 = v(lambda e, k=k: e.tensor_scalar(r_(10), ps[:, 1, 0:NE1], float(CAP), half[:, k:k + 1],
                                                      ALU.is_ge, ALU.mult), g)
                h1 = v(lambda e: e.tensor_tensor(r_(11), mid, r_(9), ALU.add), g1)
                g3 = v(lambda e: e.tensor_tensor(lo, lo, r_(10), ALU.add), g2)
                h2 = v(lambda e: e.tensor_tensor(hi, hi, r_(11), ALU.min), h1)
                cur = v(lambda e, k=k: e.tensor_scalar(mid, lo, half[:, k + 1:k + 2], None, ALU.add), g3, h1)
            a = h2
            sure, tied = wk[:, 1, :, :], wk[:, 2, :, :]
            a = v(lambda e: e.tensor_tensor(sure, S_, bc(hi), ALU.is_ge), a, cur)
            a = v(lambda e: e.tensor_tensor(tied, S_, bc(lo), ALU.is_ge), a)
            a = v(lambda e: e.tensor_tensor(tied, tied, sure, ALU.subtract), a)
            a = v(lambda e: e.tensor_reduce(r_(8), sure, AX.X, ALU.add), a)
            t1 = do("tensor", lambda e: e.matmul(ps[:, 2, 0:NE1], ones, r_(8), start=True, stop=True), a)
            t2 = do("tensor", lambda e: e.matmul(ps[:, 3, 0:NS], below, tied, start=True, stop=True), a)
            t3 = do("tensor", lambda e: e.matmul(ps[:, 4, 0:NS], ones, tied, start=True, stop=True), a)
            a = v(lambda e: e.tensor_scalar(r_(12), ps[:, 2, 0:NE1], -1.0, float(CAP), ALU.mult, ALU.add), t1)
            v3 = lambda ap: ap.rearrange("p (e b) -> p e b", e=NE1)
            z = v(lambda e: e.memset(wk[:, 3:5, :, :], 0.0), a)
            a = v(lambda e: e.tensor_copy(wk[:, 3, :, 1:NB], v3(ps[:, 4, 0:NS])[:, :, 0:NB - 1]), t3, z)
            src, dst, sh = 3, 4, 1
            while sh < NB:
                a = v(lambda e, s=src, d=dst, sh=sh: e.tensor_tensor(
                    wk[:, d, :, sh:NB], wk[:, s, :, sh:NB], wk[:, s, :, 0:NB - sh], ALU.add), a)
                a = v(lambda e, s=src, d=dst, sh=sh: e.tensor_copy(wk[:, d, :, 0:sh], wk[:, s, :, 0:sh]), a)
                src, dst, sh = dst, src, sh * 2
            a = v(lambda e, s=src: e.tensor_tensor(wk[:, 5, :, :], wk[:, s, :, :], v3(ps[:, 3, 0:NS]), ALU.add), a, t2)
            a = v(lambda e: e.tensor_tensor(wk[:, 0, :, :], wk[:, 5, :, :], bc(r_(12)), ALU.is_lt), a)
            a = v(lambda e: e.tensor_tensor(wk[:, 5, :, :], wk[:, 0, :, :], tied, ALU.mult), a)
            a = v(lambda e: e.tensor_tensor(wk[:, 1, :, :], wk[:, 5, :, :], sure, ALU.add), a)
            c = v(lambda e: e.tensor_tensor(wk[:, 0, :, :], S_, bc(mx), ALU.subtract), a, m1)
            c = do("scalar", lambda e: e.activation(wk[:, 2, :, :], wk[:, 0, :, :], ACT.Exp), c)
            c = v(lambda e: e.tensor_tensor(wk[:, 5, :, :], wk[:, 2, :, :], wk[:, 1, :, :], ALU.mult), c)
            c = v(lambda e: e.tensor_reduce(r_(8), wk[:, 5, :, :], AX.X, ALU.add), c)
            c = do("tensor", lambda e: e.matmul(ps[:, 5, 0:NE1], ones, r_(8), start=True, stop=True), c)
            c = v(lambda e: e.reciprocal(r_(9), ps[:, 5, 0:NE1]), c)
            c = v(lambda e: e.tensor_tensor(wgt[:, :, :], wk[:, 5, :, :], bc(r_(9)), ALU.mult), c)
            E.join()
            st = new_state()
            fin = [None] * NG
            for G in range(NG + 1):
                if G < NG:
                    st["acc"] = x_done[G]
                    for l in l_moe1:
                        E.wait("tensor", l)
                    experts("choice", G, x_T[:, group(G), :], None, w1, w3, w2, NE1, I1,
                            lambda b, ex: wgt[:, ex, b:b + 1], hS, sG, x_tok[:, group(G), :], x_done[G], c, st)
                    st["todo"].pop()()
                    fin[G] = layer_stats(G, st["acc"])
                if G >= 1:
                    g = G - 1
                    x_done[g] = normalize(g, fin[g])
            scope.close()

        if STOP >= 2:
            cross_attention("x0", False)
        if STOP >= 3:
            moe_top2()
        if STOP >= 4:
            got = memory()
        if STOP >= 5:
            cross_attention("x1", True)
        if STOP >= 6:
            expert_choice(*got)
        output()
        E.wait("sync", *stores)
        with nc.Block() as block:
            E.emit(block)


PROJ = ["ret_q", "ret_k", "ret_v", "ret_o", "x0_q", "x0_k", "x0_v", "x0_o", "attn_w",
        "w_write", "w_read", "x1_q", "x1_k", "x1_v", "x1_o"]
COLS = ["gn_w", "gn_b", "xq_b", "xk_b", "ln1_g", "ln1_b", "ln2_g", "ln2_b", "subln_w", "decay", "log_alpha"]


def constants(S, C):
    f = np.float32
    gam = (f(1.0) - np.exp(np.linspace(math.log(1 / 32), math.log(1 / 512), 8, dtype=f))).astype(np.float64)
    s, t = np.arange(S)[:, None], np.arange(S)[None, :]
    decay = np.stack([np.where(t >= s, g ** np.maximum(t - s, 0), 0.0) for g in gam], 1).astype(f)
    p = np.arange(P)
    headavg = (p[:, None] // 16 == p[None, :] // 16) / 16.0
    mats = np.stack([np.eye(P), headavg, np.maximum(t - 1 - s, 0), (t > s) & (s > 0), s < t, np.ones((P, P)),
                     (p[:, None] // 8 == p[None, :] // 8) / 8.0],
                    1).astype(f)
    picks = np.concatenate([(p[:, None] % 32) // 16 == np.arange(2), (p[:, None] % 32) // 8 == np.arange(4),
                            (p[:, None] % 32) // 4 == np.arange(8), np.broadcast_to(p, (P, P)),
                            p[:, None] + 1 + P * np.arange(16)],
                           1).astype(f)
    return decay, mats, picks


def kernel(**inputs):
    import concourse.bacc as bacc
    from concourse.bass_utils import run_bass_kernel_spmd

    i = {k: np.asarray(v) for k, v in inputs.items()}
    B, S, C = i["x"].shape
    order = np.array([(a * 16 + 4 * g + j) * 4 + d for g in range(4) for a in range(2) for j in range(4)
                      for d in range(4)])
    decay, mats, picks = constants(S, C)
    proj = [i["L0_attn_Wq"].T, i["L0_attn_Wk"].T, i["L0_attn_Wv"].T, i["L0_attn_Wo"].T,
            i["L0_xattn_wq_w"], i["L0_xattn_wk_w"], i["L0_xattn_wv_w"], i["L0_xattn_wo_w"],
            i["L0_ffn_attn_w"].T, i["L1_attn_W_write"], i["L1_attn_W_read"].T,
            i["L1_xattn_Wq"][order].T, i["L1_xattn_Wk"][order].T, i["L1_xattn_Wv"].T, i["L1_xattn_Wp"].T]
    rep = lambda v: np.broadcast_to(np.asarray(v).reshape(1, -1), (P, np.asarray(v).size))
    cols = [i["L0_attn_gn_weight"], i["L0_attn_gn_bias"], i["L0_xattn_wq_b"], i["L0_xattn_wk_b"],
            i["L0_ffn_ln1_g"], i["L0_ffn_ln1_b"], i["L0_ffn_ln2_g"], i["L0_ffn_ln2_b"],
            np.tile(i["L1_xattn_subln_w"], 16), rep(i["L1_attn_decay"])[:, 0], rep(i["L1_attn_log_alpha"])[:, 0]]
    chunked = lambda w: w.reshape(w.shape[0], C, -1, P).transpose(3, 0, 2, 1)
    data = {
        "x_tok": i["x"].transpose(1, 0, 2), "x_T": i["x"].transpose(2, 0, 1),
        "ctx_T": i["ctx_1024"].transpose(2, 0, 1), "mask": i["mask_Bx1xSxS2_ff1"][:, 0].transpose(1, 0, 2),
        "proj": np.stack(proj, 1), "cols": np.stack(cols, 1),
        "rows": np.stack([rep(i["L0_xattn_wv_b"]), rep(i["L0_xattn_wo_b"]), rep(i["L1_xattn_bp"])], 1),
        "gates": np.stack([i["L0_ffn_gate_w"].T, i["L1_ffn_Wg"].T], 1),
        "lams": np.stack([rep(i["L1_xattn_" + n]) for n in ("lq1", "lk1", "lq2", "lk2")], 1),
        "gate_T": i["L0_ffn_gate_proj"].transpose(2, 0, 1), "up_T": i["L0_ffn_up_proj"].transpose(2, 0, 1),
        "down_T": chunked(i["L0_ffn_down_proj"]),
        "w1_T": i["L1_ffn_W1"].transpose(2, 0, 1), "w3_T": i["L1_ffn_W3"].transpose(2, 0, 1),
        "w2_T": chunked(i["L1_ffn_W2"]),
        "decay": decay, "mats": mats, "picks": picks,
    }
    nc = bacc.Bacc("TRN2", target_bir_lowering=False, num_devices=1)
    arrays, D = {}, {}
    for name, a in data.items():
        a = np.ascontiguousarray(a)
        arrays[name] = a
        D[name] = nc.dram_tensor(name, a.shape, mybir.dt.from_np(a.dtype), kind="ExternalInput").ap()
    out = nc.dram_tensor("out", (S, B, C), F32, kind="ExternalOutput").ap()
    build(nc, D, out)
    r = run_bass_kernel_spmd(nc, [arrays], core_ids=[0])
    return np.ascontiguousarray(r.results[0]["out"].transpose(1, 0, 2))
```

```python
import math
from contextlib import ExitStack

import concourse.bass as bass
import numpy as np
from concourse import mybir

F32 = mybir.dt.float32
ALU = mybir.AluOpType
ACT = mybir.ActivationFunctionType
AX = mybir.AxisListType

P = 128


class Engines:

    ORDER = ("sync", "tensor", "vector", "scalar", "gpsimd")

    def __init__(self, nc, ctx):
        self.nc, self.ctx = nc, ctx
        self.queue = {e: [] for e in self.ORDER}
        self.progress, self.count, self.last = {}, {}, {}

    def sem(self, name):
        return self.ctx.enter_context(self.nc.semaphore(name))

    def stage(self, name):
        for e in self.ORDER[1:]:
            self.progress[e] = self.sem(f"{name}_{e}_done")
            self.count[e] = 0

    def do(self, engine, what, *waits, tell=True):
        step = [[w for w in waits if w is not None], what, None, 1]
        self.queue[engine].append(step)
        if not tell:
            return None
        self.count[engine] += 1
        step[2] = self.progress[engine]
        token = (self.progress[engine], self.count[engine])
        self.last[engine] = token
        return token

    def dma(self, engine, name, out, in_, *waits, **how):
        s = self.sem(f"{name}_landed")
        self.queue[engine].append([[w for w in waits if w is not None],
                                   lambda e: e.dma_start(out, in_, **how), s, 16])
        return (s, 16)

    def wait(self, engine, *waits):
        self.queue[engine].append([[w for w in waits if w is not None], None, None, 0])

    def join(self):
        ends = dict(self.last)
        for e in self.ORDER:
            self.wait(e, *[t for f, t in ends.items() if f != e])

    def emit(self, block):
        def body(name):
            def run(eng):
                seen = {}
                for waits, what, s, by in self.queue[name]:
                    for ws, value in waits:
                        if seen.get(id(ws), 0) < value:
                            eng.wait_ge(ws, value)
                            seen[id(ws)] = value
                    if what is not None:
                        ins = what(eng)
                        if s is not None:
                            ins.then_inc(s, by)
            return run
        for name in self.ORDER:
            blocks = {"sync": block.sync, "tensor": block.tensor, "vector": block.vector,
                            "scalar": block.scalar, "gpsimd": block.gpsimd}[name]
            blocks(body(name))


def build(nc, D, out):
    NB, S, C = D["x_tok"].shape[1], D["x_T"].shape[2], D["x_T"].shape[0]
    SK = D["ctx_T"].shape[2]
    GB = 4
    NG = NB // GB
    GN = GB * S
    EPS = 1e-5
    NE0, I0 = D["gate_T"].shape[1], D["gate_T"].shape[2]
    NE1, I1 = D["w1_T"].shape[1], D["w1_T"].shape[2]
    CAP = NB * S // NE1
    NEG = 1e9

    with ExitStack() as ctx:
        def sb(name, shape, dt=F32, scope=ctx):
            return scope.enter_context(nc.sbuf_tensor(name, shape, dt))

        E = Engines(nc, ctx)
        do = E.do
        ps = ctx.enter_context(nc.psum_tensor("ps", [P, 8, 512], F32))

        x_tok = sb("x_tok_sb", [P, NB, C])
        x_Tp = sb("x_T_sb", [P, NB * S + 8])
        x_T = x_Tp[:, 8:].rearrange("p (b t) -> p b t", b=NB)
        ctx_T = sb("ctx_T_sb", [P, NB, SK])
        n_proj = D["proj"].shape[1]
        proj = sb("proj_sb", [P, n_proj, P])
        n_cols = D["cols"].shape[1]
        cols = sb("cols_sb", [P, n_cols])
        rows = sb("rows_sb", [P, 2, P])
        gates = sb("gates_sb", [P, 2, 8])
        lams = sb("lams_sb", [P, 4, D["lams"].shape[2]])
        n_mats = D["mats"].shape[1]
        mats = sb("mats_sb", [P, n_mats, P])
        picks = sb("picks_sb", [P, D["picks"].shape[1]])
        stats = sb("stats", [P, NB, 6])
        mv = sb("mv", [P, NB, 2])
        veps = sb("veps", [P, NB])
        rstd = sb("rstd", [P, NB])
        minus_half = sb("minus_half", [P, P])
        EW = 3 * max(NE0 * I0, NE1 * I1)
        expert_w = sb("expert_w", [P, EW])

        PJ = {n: i for i, n in enumerate(PROJ)}
        CO = {n: i for i, n in enumerate(COLS)}
        W = lambda n: proj[:, PJ[n], :]
        col = lambda n: cols[:, CO[n]:CO[n] + 1]
        ident, headavg, diffs, causal, below, ones, mean8, same, before16 = [mats[:, i, :] for i in range(9)]

        E.stage("start")
        filler = sb("filler", [P, 512], mybir.dt.float16)
        t_filler = do("gpsimd", lambda e: e.memset(filler[:, :], 1.0))
        l_proj = E.dma("sync", "proj", proj[:, :, :], D["proj"])
        l_xT = [E.dma("sync", f"x_T{h}", x_T[:, h * 16:h * 16 + 16, :], D["x_T"][:, h * 16:h * 16 + 16, :])
                for h in range(2)]
        l_picks = E.dma("sync", "picks", picks[:, :], D["picks"])
        l_cols = E.dma("sync", "cols", cols[:, :], D["cols"])
        l_mats = E.dma("sync", "mats", mats[:, :, :], D["mats"])
        gate_pad = sb("gate_pad_sb", [P, D["gate_pad"].shape[1]])
        iota16 = sb("iota16", [P, P], mybir.dt.float16)
        a_scope = ExitStack()
        decay_T = sb("decay_T", [P, 8, S], scope=a_scope)
        l_decay = E.dma("sync", "decay", decay_T[:, :, :], D["decay"])
        l_xtok = E.dma("sync", "x_tok", x_tok[:, :, :], D["x_tok"])
        l_ctx = E.dma("sync", "ctx_T", ctx_T[:, :, :], D["ctx_T"])
        l_rows = E.dma("sync", "rows", rows[:, :, :], D["rows"])
        l_gate_pad = E.dma("sync", "gate_pad", gate_pad[:, :], D["gate_pad"])
        l_gates = E.dma("sync", "gates", gates[:, :, :], D["gates"])
        l_lams = E.dma("sync", "lams", lams[:, :, :], D["lams"])
        n0 = NE0 * I0
        gate_T = expert_w[:, 0:n0].rearrange("p (e i) -> p e i", e=NE0)
        up_T = expert_w[:, n0:2 * n0].rearrange("p (e i) -> p e i", e=NE0)
        down_T = expert_w[:, 2 * n0:3 * n0].rearrange("p (e k c) -> p e k c", e=NE0, c=C)
        l_moe0 = [E.dma("sync", "gate_T", gate_T, D["gate_T"]), E.dma("sync", "up_T", up_T, D["up_T"]),
                  E.dma("sync", "down_T", down_T, D["down_T"])]
        iotas = picks[:, 14:14 + P]
        tokens = picks[:, 14 + P:14 + P + NB // 2]
        expert_of = picks[:, 30 + P:38 + P]
        powers = picks[:, 38 + P:38 + P + 27]
        t_i16 = do("gpsimd", lambda e: e.tensor_copy(iota16[:, :], iotas), l_picks)
        t_half = do("gpsimd", lambda e: e.memset(minus_half[:, :], -0.5))
        t_pad = do("gpsimd", lambda e: e.memset(x_Tp[:, 0:8], 0.0))


        def keep_busy(bank, times, *waits, n=512):
            for _ in range(times):
                do("tensor", lambda e: e.matmul(ps[:, bank, 0:n], filler[:, 0:P], filler[:, 0:n],
                                                start=True, stop=True), t_filler, *waits, tell=False)

        def group(G):
            return slice(G * GB, (G + 1) * GB)

        def layer_stats(G, ready):
            t = ready
            for b in range(G * GB, (G + 1) * GB):
                t = do("vector", lambda e, b=b: e.bn_stats(stats[:, b, :], x_tok[:, b, :]), ready)
            for b in range(G * GB, (G + 1) * GB):
                t2 = do("vector", lambda e, b=b: e.bn_aggr(mv[:, b, :], stats[:, b, :]), t)
            g = group(G)
            t3 = do("gpsimd", lambda e: e.tensor_scalar(veps[:, g], mv[:, g, 1], EPS, None, ALU.add), t2)
            return do("gpsimd", lambda e: e.tensor_tensor(rstd[:, g], veps[:, g], minus_half[:, 0:GB], ALU.pow),
                      t3, t_half)

        def residual(G, summand, ready, times=1.0):
            g = group(G)
            t = do("vector", lambda e: e.scalar_tensor_tensor(x_tok[:, g, :], x_tok[:, g, :], times, summand,
                                                              ALU.mult, ALU.add), ready, l_xtok)
            return t, layer_stats(G, t)

        def normalize(G, ready, dst=None, *waits):
            dst = x_tok if dst is None else dst
            for i, b in enumerate(range(G * GB, (G + 1) * GB)):
                o = dst[:, b, :] if dst is x_tok else dst[:, i, :]
                t = do("vector", lambda e, b=b, o=o: e.tensor_scalar(
                    o, x_tok[:, b, :], mv[:, b, 0:1], rstd[:, b:b + 1], ALU.subtract, ALU.mult), ready, *waits)
            return t

        def turn(src, bank, *waits):
            for i in range(GB):
                t = do("tensor", lambda e, i=i, tile=src(i): e.transpose(ps[:, bank, i * S:(i + 1) * S], tile, ident),
                       *waits, l_mats, tell=i == GB - 1)
            return t

        def bank4(bank):
            return ps[:, bank, :].rearrange("p (b c) -> p b c", b=GB)

        def renew_xT(G, ready, bank, bank_free):
            t = turn(lambda i: x_tok[:, G * GB + i, :], bank, ready, bank_free)
            return do("scalar", lambda e: e.copy(x_T[:, group(G), :], bank4(bank)), t)

        def output():
            for G in range(NG):
                stores.append(E.dma("sync", f"out{G}", out[:, group(G), :], x_tok[:, group(G), :], x_done[G]))

        stores = []
        rows_d = nc.dram_tensor("choice_rows", (NB * S, C), F32, kind="Internal").ap()
        sums_d = nc.dram_tensor("choice_sums", (NB * S, C), F32, kind="Internal").ap()
        row_store, sum_store = [], []
        x_done = [l_xtok] * NG
        xT_done = [l_xT[G * GB // 16] for G in range(NG)]

        E.stage("retention")
        NH, HD = 8, C // 8
        kT = sb("ret_kT", [P, 2, GN], scope=a_scope)
        qB = sb("ret_qB", [P, 2, 2, GN], scope=a_scope)
        vB = sb("ret_v", [P, 2, GB, 4, 2, 32], scope=a_scope)
        t_zero = do("gpsimd", lambda e: e.memset(vB[:, :, :, :, :, :], 0.0))
        aT = sb("ret_aT", [P, 3, 2, 2, S], scope=a_scope)
        yT = sb("ret_yT", [P, NB, S], scope=a_scope)
        ystat = sb("ret_ystat", [P, NB, 6], scope=a_scope)
        ymv = sb("ret_ymv", [P, NB, 2], scope=a_scope)
        small = sb("ret_small", [P, 8, NB], scope=a_scope)

        free7 = None
        qkv_ready = [[None] * 3 for _ in range(NG)]
        qk_free = [None, None]
        y_free = [None, None]
        av_done = [None] * (2 * NB + 4)
        group_used = [None] * (NG + 1)

        def ret_project(G, which):
            nonlocal free7
            s = G % 2
            old = group_used[G - 2] if G >= 2 else None
            rhs = x_T[:, group(G), :]
            if which == 0:
                t = do("tensor", lambda e: e.matmul(ps[:, 7, :], W("ret_q"), rhs, start=True, stop=True),
                       free7, l_proj, xT_done[G])
                for j in range(2):
                    free7 = do("scalar", lambda e, j=j: e.activation(
                        qB[:, s, j, :], ps[:, 7, :], ACT.Copy, scale=picks[:, j:j + 1]), t, old, l_picks)
            elif which == 1:
                t = do("tensor", lambda e: e.matmul(ps[:, 7, :], W("ret_k"), rhs, start=True, stop=True), free7)
                free7 = do("scalar", lambda e: e.copy(kT[:, s, :], ps[:, 7, :]), t, old)
            else:
                for i in range(GB):
                    t = do("tensor", lambda e, i=i: e.matmul(ps[:, 7, i * S:(i + 1) * S], x_T[:, G * GB + i, :],
                                                             W("ret_v"), start=True, stop=True),
                           free7, tell=i == GB - 1)
                for i in range(GB):
                    flat = vB[:, s, i, :, :, :].rearrange("p g j c -> p g (j c)")
                    dst = bass.AP(tensor=flat.tensor, offset=flat.offset,
                                  ap=[list(flat.ap[0]), [64, 4], [48, 2], [1, HD]])
                    src = ps[:, 7, i * C:(i + 1) * C].rearrange("p (g j d) -> p g j d", g=4, d=HD)
                    free7 = do("scalar", lambda e, dst=dst, src=src: e.copy(dst, src), t, old, t_zero)
            qkv_ready[G][which] = free7

        def ret_scores(u):
            b, h = divmod(u, 2)
            G, i = divmod(b, GB)
            s = G % 2
            keep_busy(2 * h, 1, qk_free[h])
            for q in range(2):
                g = 2 * h + q
                t = do("tensor", lambda e, g=g: e.matmul(
                    ps[:, g, 0:2 * S].rearrange("p (j t) -> p j t", j=2),
                    kT[32 * g:32 * g + 32, s, i * S:(i + 1) * S],
                    qB[32 * g:32 * g + 32, s, :, i * S:(i + 1) * S], start=True, stop=True),
                    qk_free[h], *qkv_ready[G], tell=q == 1)
            a = aT[:, u % 3, :, :, :].rearrange("p g j t -> p g (j t)")
            m = decay_T[:, 4 * h:4 * h + 4, :].rearrange("p (g j) t -> p g (j t)", g=2)
            qk_free[h] = masked[u] = do("vector", lambda e: e.tensor_tensor(
                a, ps[:, 2 * h:2 * h + 2, 0:2 * S], m, ALU.mult), t, l_decay, av_done[u - 3] if u >= 3 else None)

        def ret_values(u):
            b, h = divmod(u, 2)
            G, i = divmod(b, GB)
            bank = 4 + G % 2
            for n in range(4):
                g, j = 2 * h + n // 2, n % 2
                t = do("tensor", lambda e, n=n, g=g, j=j: e.matmul(
                    ps[32 * g:32 * g + 32, bank, i * S:(i + 1) * S], vB[:, G % 2, i, g, j, :],
                    aT[:, u % 3, n // 2, j, :], start=j == 0, stop=j == 1),
                    masked[u], y_free[G % 2], tell=n == 3)
            av_done[u] = t
            if u % 8 == 7:
                group_used[G] = t
                y_free[G % 2] = y_copied[G] = do("scalar", lambda e: e.copy(yT[:, group(G), :], bank4(bank)), t)

        masked = [None] * (2 * NB)
        y_copied = [None] * NG

        def ret_turn(G):
            for b in range(G * GB, (G + 1) * GB):
                t3 = do("vector", lambda e, b=b: e.bn_stats(ystat[:, b, :], yT[:, b, :]), y_copied[G])
            return t3

        keep_busy(0, 20)
        for w in range(3):
            ret_project(0, w)
        n_u = 2 * NB
        for u in range(n_u + 2):
            if u < n_u:
                ret_scores(u)
            if u % 8 in (1, 2, 3) and u // 8 + 1 < NG:
                ret_project(u // 8 + 1, u % 8 - 1)
            if u >= 1 and u - 1 < n_u:
                ret_values(u - 1)
            if u % 8 == 4 and u >= 8:
                ret_turn(u // 8 - 1)
        t = ret_turn(NG - 1)
        for b in range(NB):
            t2 = do("vector", lambda e, b=b: e.bn_aggr(ymv[:, b, :], ystat[:, b, :]), t)
        mean_h, delta, dvar, v_h, y_scale, y_bias, tmp = [small[:, i, :] for i in range(7)]
        t3 = do("tensor", lambda e: e.matmul(ps[:, 6, 0:NB], headavg, ymv[:, :, 0], start=True, stop=True), t2)
        t4 = do("vector", lambda e: e.tensor_copy(mean_h, ps[:, 6, 0:NB]), t3)
        t5 = do("vector", lambda e: e.tensor_tensor(delta, ymv[:, :, 0], mean_h, ALU.subtract), t4)
        t6 = do("vector", lambda e: e.tensor_tensor(dvar, delta, delta, ALU.mult), t5)
        t7 = do("vector", lambda e: e.tensor_tensor(dvar, dvar, ymv[:, :, 1], ALU.add), t6)
        t8 = do("tensor", lambda e: e.matmul(ps[:, 6, 0:NB], headavg, dvar, start=True, stop=True), t7)
        t9 = do("vector", lambda e: e.tensor_scalar(v_h, ps[:, 6, 0:NB], EPS, None, ALU.add), t8)
        t10 = do("scalar", lambda e: e.activation(tmp, v_h, ACT.Sqrt), t9)
        t10 = do("vector", lambda e: e.reciprocal(tmp, tmp), t10)
        t11 = do("vector", lambda e: e.tensor_scalar(y_scale, tmp, col("gn_w"), None, ALU.mult), t10, l_cols)
        t12 = do("vector", lambda e: e.tensor_tensor(delta, mean_h, y_scale, ALU.mult), t11)
        t13 = do("vector", lambda e: e.tensor_scalar(y_bias, delta, -1.0, col("gn_b"), ALU.mult, ALU.add), t12)
        bank_free = [None] * 8
        pend = [None] * NG
        affine = [None] * NG

        def ret_affine(G):
            for b in range(G * GB, (G + 1) * GB):
                affine[G] = do("scalar", lambda e, b=b: e.activation(
                    yT[:, b, :], yT[:, b, :], ACT.Identity, scale=y_scale[:, b:b + 1],
                    bias=y_bias[:, b:b + 1]), t13)

        ret_affine(0)
        for G in range(NG + 2):
            if G + 1 < NG:
                ret_affine(G + 1)
            if G < NG:
                bank = G % 3
                for i in range(GB):
                    t2 = do("tensor", lambda e, i=i, G=G, bank=bank: e.matmul(
                        ps[:, bank, i * S:(i + 1) * S], yT[:, G * GB + i, :], W("ret_o"), start=True, stop=True),
                        affine[G], bank_free[bank], tell=i == GB - 1)
                bank_free[bank], pend[G] = residual(G, bank4(bank), t2)
            if 1 <= G <= NG:
                x_done[G - 1] = normalize(G - 1, pend[G - 1])
            if G >= 2:
                g = G - 2
                xT_done[g] = bank_free[4 + g % 2] = renew_xT(g, x_done[g], 4 + g % 2, bank_free[4 + g % 2])
        E.join()
        a_scope.close()

        def cross_attention(name, differential):
            scope = ExitStack()
            E.stage(name)
            NA = 2 if differential else 1
            NK = 4 * NA
            UH = 8
            VD = 8
            ND, NPB = 4, 6
            qT = sb(name + "_qT", [P, 2, GN], scope=scope)
            kB = sb(name + "_kB", [P, 2, NK, GB, SK], scope=scope)
            vX = sb(name + "_vX", [SK, 2, GB, 4, 4, 32], scope=scope)
            mS = sb(name + "_m", [P, ND, UH], scope=scope)
            dS = sb(name + "_d", [P, ND, UH, SK], scope=scope)
            pS = sb(name + "_p", [P, NPB, UH, SK], scope=scope)
            sums = sb(name + "_sums", [P, 2, NA, GB, 16], scope=scope)
            coef = sb(name + "_coef", [P, 4, UH], scope=scope)
            nS = sb(name + "_n", [P, 3, UH, SK], scope=scope)
            pT = sb(name + "_pT", [SK, 2, UH, S], scope=scope)
            cT = sb(name + "_cT", [P, 2, GN], scope=scope)
            if differential:
                cN = sb(name + "_cN", [P, 2, GN], scope=scope)
                sq = sb(name + "_sq", [P, 2, GN], scope=scope)
                rr = sb(name + "_rr", [P, 2, GN], scope=scope)
                lsq = sb(name + "_lsq", [P, 2, GB, C], scope=scope)
            else:
                tS = sb(name + "_t", [P, 2, UH, SK], scope=scope)
                rS = sb(name + "_r", [P, 3, UH, SK], scope=scope)
                mask = sb(name + "_mask", [P, NB, SK], scope=scope)
                l_mask = E.dma("sync", "mask", mask[:, :, :], D["mask"])
            t_zero = do("gpsimd", lambda e: e.memset(vX[:, :, :, :, :, :], 0.0))

            free7 = free6 = None
            ready = [[None] * 3 for _ in range(NG)]
            qk_free = [None, None]
            pt_free = None
            qk_last, av_last, c_done = [None] * NG, [None] * NG, [None] * NG
            NW = 2 * NB
            Q_FACTOR = 1.0 / (NEG * math.sqrt(8.0))
            FILL = 3 if differential else 4
            n_u = NA * NW
            scored, soft, exp_done, p_used = [[None] * n_u for _ in range(4)]
            n_done, turned, pt_ready, av_done = [[None] * NW for _ in range(4)]
            cT_used, cN_used = [None, None], [None, None]
            pend = [None] * NG

            def before(tokens, i):
                return tokens[i] if i >= 0 else None

            def project(G, which):
                nonlocal free7
                s = G % 2
                old = before(qk_last, G - 2)
                if which == 0:
                    t = do("tensor", lambda e: e.matmul(ps[:, 7, :], W(name + "_q"), x_T[:, group(G), :],
                                                        start=True, stop=True), free7)
                    if differential:
                        free7 = do("scalar", lambda e: e.mul(qT[:, s, :], ps[:, 7, :], 0.5), t, old)
                    else:
                        free7 = do("scalar", lambda e: e.activation(
                            qT[:, s, :], ps[:, 7, :], ACT.Identity, scale=Q_FACTOR, bias=qbias[:, 0:1]),
                            t, old, t_qbias)
                elif which == 1:
                    kin = ctx_T[:, group(G), :]
                    kp = ps[:, 7, 0:GB * SK]
                    t = do("tensor", lambda e: e.matmul(kp, W(name + "_k"), kin, start=True, stop=True),
                           free7, l_ctx)
                    src = kp.rearrange("p (b k) -> p b k", b=GB)
                    for j in range(NK):
                        dst = kB[:, s, j, :, :]
                        pick = picks[:, (6 if differential else 2) + j:(7 if differential else 3) + j]
                        if differential:
                            free7 = do("scalar", lambda e, dst=dst, pick=pick: e.activation(
                                dst, src, ACT.Copy, scale=pick), t, old)
                        else:
                            bias = kbias[:, j:j + 1]
                            free7 = do("scalar", lambda e, dst=dst, pick=pick, bias=bias: e.activation(
                                dst, src, ACT.Identity, scale=pick, bias=bias), t, old, t_kbias)
                else:
                    for i in range(GB):
                        t = do("tensor", lambda e, i=i: e.matmul(
                            ps[0:SK, 7, i * C:(i + 1) * C], ctx_T[:, G * GB + i, :], W(name + "_v"),
                            start=True, stop=True), free7, l_ctx, tell=i == GB - 1)
                    old = before(av_last, G - 2)
                    for i in range(GB):
                        flat = vX[:, s, i, :, :, :].rearrange("p g j c -> p g (j c)")
                        dst = bass.AP(tensor=flat.tensor, offset=flat.offset,
                                      ap=[list(flat.ap[0]), [128, 4], [40, 4], [1, VD]])
                        src = ps[0:SK, 7, i * C:(i + 1) * C].rearrange("p (g j d) -> p g j d", g=4, d=VD)
                        free7 = do("scalar", lambda e, dst=dst, src=src: e.copy(dst, src), t, old, t_zero)
                ready[G][which] = free7

            def score_products(u):
                w, att = divmod(u, NA)
                b, half = divmod(w, 2)
                G, i = divmod(b, GB)
                s = G % 2
                bp = 2 * (u % 2)
                keep_busy(bp, FILL, qk_free[u % 2])
                for q in range(2):
                    g = 2 * half + q
                    t = do("tensor", lambda e, g=g, q=q: e.matmul(
                        ps[:, bp + q, 0:4 * SK].rearrange("p (j k) -> p j k", j=4),
                        qT[32 * g:32 * g + 32, s, i * S:(i + 1) * S],
                        kB[32 * g:32 * g + 32, s, 4 * att:4 * att + 4, i, :], start=True, stop=True),
                        qk_free[u % 2], *ready[G][:2], tell=q == 1)
                scored[u] = t
                if half == 1 and i == GB - 1:
                    qk_last[G] = t

            def shifted_scores(u):
                b = u // NA // 2
                bp = 2 * (u % 2)
                t = scored[u]
                sc = ps[:, bp:bp + 2, 0:4 * SK].rearrange("p g (j k) -> p g j k", j=4)
                v = u % ND
                m = mS[:, v, :]
                if differential:
                    t2 = do("vector", lambda e: e.tensor_reduce(m, sc, AX.X, ALU.max), t)
                    mb = m.rearrange("p (g j k) -> p g j k", g=2, k=1).broadcast_to([P, 2, 4, SK])
                    soft[u] = qk_free[u % 2] = do("vector", lambda e: e.tensor_tensor(
                        dS[:, v, :, :].rearrange("p (g j) k -> p g j k", g=2), sc, mb, ALU.subtract),
                        t2, before(exp_done, u - ND))
                else:
                    mk = mask[:, b:b + 1, :].unsqueeze(1).broadcast_to([P, 2, 4, SK])
                    qk_free[u % 2] = t2 = do("vector", lambda e: e.tensor_tensor(
                        tS[:, u % 2, :, :].rearrange("p (g j) k -> p g j k", g=2), sc, mk, ALU.mult),
                        t, l_mask)
                    flat = tS[:, u % 2, :, :].rearrange("p h k -> p (h k)")
                    t3 = do("vector", lambda e: e.scalar_tensor_tensor(
                        rS[:, u % 3, :, :].rearrange("p h k -> p (h k)"), flat, 0.0, flat,
                        ALU.is_equal, ALU.subtract), t2, before(soft, u - 3))
                    t4 = do("vector", lambda e: e.tensor_reduce(m, rS[:, u % 3, :, :], AX.X, ALU.min), t3)
                    soft[u] = do("gpsimd", lambda e: e.tensor_tensor(
                        dS[:, v, :, :], rS[:, u % 3, :, :], m.unsqueeze(2).broadcast_to([P, UH, SK]),
                        ALU.subtract), t4, before(exp_done, u - ND))

            def exponentials(u):
                exp_done[u] = do("scalar", lambda e: e.activation(
                    pS[:, u % NPB, :, :], dS[:, u % ND, :, :], ACT.Exp, scale=1.0 if differential else -NEG),
                    soft[u], before(p_used, u - NPB))

            def normalizers(w):
                b, half = divmod(w, 2)
                G, i = divmod(b, GB)
                n = w % 3
                for att in range(NA):
                    u = w * NA + att
                    l = sums[:, G % 2, att, i, 8 * half:8 * half + 8]
                    ts = do("vector", lambda e, u=u, l=l: e.tensor_reduce(l, pS[:, u % NPB, :, :], AX.X, ALU.add),
                            exp_done[u], before(c_done, G - 2))
                c0, c1 = coef[:, w % 2, :], coef[:, 2 + w % 2, :]
                old = before(turned, w - 3)
                tr = do("vector", lambda e: e.reciprocal(c0, l), ts, before(n_done, w - 2))
                if not differential:
                    p0 = pS[:, w % NPB, :, :]
                    p_used[w] = n_done[w] = do("gpsimd", lambda e: e.tensor_tensor(
                        nS[:, n, :, :], p0, c0.unsqueeze(2).broadcast_to([P, UH, SK]), ALU.mult), tr, old)
                else:
                    p1, p2 = pS[:, (2 * w) % NPB, :, :], pS[:, (2 * w + 1) % NPB, :, :]
                    l1 = sums[:, G % 2, 0, i, 8 * half:8 * half + 8]
                    tc = do("vector", lambda e: e.scalar_tensor_tensor(c1, l1, neg_lam[:, 0:1], c0,
                                                                       ALU.mult, ALU.mult), tr, t_lam)
                    t = do("gpsimd", lambda e: e.tensor_tensor(
                        nS[:, n, :, :], p2, c1.unsqueeze(2).broadcast_to([P, UH, SK]), ALU.mult), tc, old)
                    t = do("gpsimd", lambda e: e.tensor_tensor(nS[:, n, :, :], nS[:, n, :, :], p1, ALU.add), t)
                    p_used[2 * w] = p_used[2 * w + 1] = n_done[w] = t

            def turn_p(w):
                nonlocal pt_free
                for h in range(UH):
                    t = do("tensor", lambda e, h=h: e.transpose(
                        ps[0:SK, 4 + h // 4, (h % 4) * S:(h % 4 + 1) * S], nS[:, w % 3, h, :], ident),
                        n_done[w], pt_free, tell=h == UH - 1)
                turned[w] = t
                pt_free = pt_ready[w] = do("scalar", lambda e: e.copy(
                    pT[:, w % 2, :, :].rearrange("p (g h) q -> p g (h q)", g=2), ps[0:SK, 4:6, :]),
                    t, before(av_done, w - 2))

            def values(w):
                nonlocal free6
                b, half = divmod(w, 2)
                G, i = divmod(b, GB)
                for n in range(UH):
                    g, j = 2 * half + n // 4, n % 4
                    t = do("tensor", lambda e, n=n, g=g, j=j: e.matmul(
                        ps[32 * g:32 * g + 32, 6, i * S:(i + 1) * S], vX[:, G % 2, i, g, j, :],
                        pT[:, w % 2, n, :], start=j == 0, stop=j == 3), pt_ready[w], ready[G][2], free6,
                        tell=n == UH - 1)
                av_done[w] = t
                if half == 1 and i == GB - 1:
                    av_last[G] = t
                    if not differential:
                        free6 = c_done[G] = do("scalar", lambda e: e.activation(
                            cT[:, G % 2, :], ps[:, 6, :], ACT.Identity, bias=col("xv_b")), t, cT_used[G % 2])
                        return
                    free6 = c_done[G] = do("scalar", lambda e: e.copy(cT[:, G % 2, :], ps[:, 6, :]),
                                           t, cT_used[G % 2])
                    s = G % 2
                    l1 = sums[:, s, 0, :, :].rearrange("p b h -> p (b h)").unsqueeze(2).broadcast_to(
                        [P, GB * 16, VD])
                    tl = do("vector", lambda e: e.scalar_tensor_tensor(
                        lsq[:, s, :, :].rearrange("p b (h d) -> p (b h) d", d=VD), l1, EPS, l1,
                        ALU.mult, ALU.mult), cN_used[s])
                    tq = do("scalar", lambda e: e.activation(sq[:, s, :], cT[:, s, :], ACT.Square),
                            c_done[G], cN_used[s])
                    c_done[G] = tq
                    lsq_done[G] = tl

            lsq_done = [None] * NG

            def rms(G):
                nonlocal free7
                s = G % 2
                t = do("tensor", lambda e: e.matmul(ps[:, 7, :], mean8, sq[:, s, :], start=True, stop=False),
                       c_done[G], free7, tell=False)
                for i in range(GB):
                    t = do("tensor", lambda e, i=i: e.matmul(
                        ps[:, 7, i * S:(i + 1) * S], lsq[:, s, i, :], ident, start=False, stop=i == GB - 1),
                        lsq_done[G], tell=i == GB - 1)
                free7 = t = do("scalar", lambda e: e.activation(rr[:, s, :], ps[:, 7, :], ACT.Ln), t, cN_used[s])
                rms_done[G] = do("scalar", lambda e: e.activation(rr[:, s, :], rr[:, s, :], ACT.Exp, scale=-0.5), t)

            rms_done = [None] * NG

            def scaled_context(G):
                s = G % 2
                c_done[G] = do("vector", lambda e: e.scalar_tensor_tensor(
                    cN[:, s, :], cT[:, s, :], sub_w[:, 0:1], rr[:, s, :], ALU.mult, ALU.mult), rms_done[G], t_sub, cN_used[s])

            def context_out(G):
                nonlocal free7
                s = G % 2
                src = cN if differential else cT
                for i in range(GB):
                    t = do("tensor", lambda e, i=i: e.matmul(
                        ps[:, 7, i * C:(i + 1) * C], src[:, s, i * S:(i + 1) * S], W(name + "_o"),
                        start=True, stop=True), c_done[G], free7, tell=i == GB - 1)
                cT_used[s] = cN_used[s] = out_done[G] = t

            def output_bias(G):
                b = rows[:, (1 if differential else 0):(2 if differential else 1), :].broadcast_to([P, GB, C])
                g = group(G)
                biased[G] = do("gpsimd", lambda e: e.tensor_tensor(x_tok[:, g, :], x_tok[:, g, :], b, ALU.add),
                               x_done[G], l_rows)

            def add_up(G):
                nonlocal free7
                E.wait("vector", biased[G])
                free7, pend[G] = residual(G, bank4(7), out_done[G])

            out_done, biased = [None] * NG, [None] * NG

            def finish(G):
                x_done[G] = normalize(G, pend[G])

            def renew(G):
                nonlocal free7
                free7 = xT_done[G] = renew_xT(G, x_done[G], 7, free7)
                if differential:
                    for what, to, done in (("rows", rows_d, row_store), ("sums", sums_d, sum_store)):
                        done.append(E.dma("sync", f"x1_{what}{G}", to[G * GN:(G + 1) * GN, :].rearrange(
                            "(b t) c -> t b c", b=GB), x_tok[:, group(G), :], x_done[G]))

            if differential:
                lam_init = 0.8 - 0.6 * math.exp(-0.3 * 4)
                lw = sb(name + "_lw", [P, 12], scope=scope)
                neg_lam = sb(name + "_neg_lam", [P, 1], scope=scope)
                sub_w = sb(name + "_sub_w", [P, 1], scope=scope)
                for a in range(2):
                    ta = do("vector", lambda e, a=a: e.tensor_tensor(
                        lw[:, 4 * a:4 * a + 4], lams[:, 2 * a, :], lams[:, 2 * a + 1, :], ALU.mult), l_lams)
                for a in range(2):
                    tb = do("vector", lambda e, a=a: e.tensor_reduce(
                        lw[:, 8 + a:9 + a], lw[:, 4 * a:4 * a + 4], AX.X, ALU.add), ta)
                tc = do("scalar", lambda e: e.activation(lw[:, 10:12], lw[:, 8:10], ACT.Exp), tb)
                td = do("vector", lambda e: e.tensor_scalar(lw[:, 8:9], lw[:, 10:11], lam_init, -1.0,
                                                            ALU.add, ALU.mult), tc)
                t_lam = do("vector", lambda e: e.tensor_tensor(neg_lam[:, :], lw[:, 8:9], lw[:, 11:12], ALU.add), td)
                t_sub = do("vector", lambda e: e.tensor_scalar(sub_w[:, :], col("subln_w"), 1.0 - lam_init, None,
                                                               ALU.mult))
            else:
                qbias = sb(name + "_qbias", [P, 1], scope=scope)
                t_qbias = do("vector", lambda e: e.tensor_scalar(qbias[:, :], col("xq_b"), Q_FACTOR, None, ALU.mult))
                kbias = sb(name + "_kbias", [P, 4], scope=scope)
                t_kbias = do("vector", lambda e: e.tensor_scalar(kbias[:, :], picks[:, 2:6], col("xk_b"), None,
                                                                 ALU.mult))

            for k in range(2):
                project(0, k)
            keep_busy(3, 16)
            score_products(0)
            project(0, 2)
            per = 2 * GB
            OUT = 7 if differential else 6
            LN, LT, LV = (1 if differential else 2), 3, 4
            for w in range(NW + per + 4):
                j, G = w % per, w // per
                if w < NW:
                    for u in range(w * NA, (w + 1) * NA):
                        shifted_scores(u)
                        exponentials(u)
                        if u + 1 < n_u:
                            score_products(u + 1)
                        if u % NA == 0 and LT <= w:
                            turn_p(w - LT)
                            if w >= LV:
                                values(w - LV)
                elif w < NW + LT:
                    turn_p(w - LT)
                if j in (1, 2) and G + 1 < NG and w < NW:
                    project(G + 1, j - 1)
                if LN <= w < NW + LN:
                    normalizers(w - LN)
                if NW <= w < NW + LV:
                    values(w - LV)
                if j == 4 and G + 1 < NG and w < NW:
                    project(G + 1, 2)
                if j == 3 and G < NG:
                    output_bias(G)
                for g in range(max(0, G - 2), min(G, NG)):
                    at = w - (g + 1) * per
                    if differential and at == 5:
                        rms(g)
                    if differential and at == 6:
                        scaled_context(g)
                    if at == OUT:
                        context_out(g)
                    if at == OUT + 1:
                        add_up(g)
                    if at == OUT + 2:
                        finish(g)
                    if at == per + 3:
                        renew(g)
            E.join()
            scope.close()

        def moe_top2():
            scope = ExitStack()
            E.stage("moe")
            NT = 2 * NB + NE0
            NX = 4
            rows_d = nc.dram_tensor("moe_rows", (NB * S, C), F32, kind="Internal").ap()
            y_d = nc.dram_tensor("moe_y", (2 * NB * S, C), F32, kind="Internal").ap()
            hB = sb("moe_hB", [P, 3, GB, C], scope=scope)
            n1 = sb("moe_n", [P, 2, GB, C], scope=scope)
            n2 = sb("moe_n2", [P, 3, GB, C], scope=scope)
            nT = sb("moe_nT", [P, 2, GB, S], scope=scope)
            tT = sb("moe_tT", [P, 2, GN], scope=scope)
            lg = sb("moe_logits", [P, NB, NE0], scope=scope)
            free = [None] * 8
            xh_done, row_store = [None] * NG, [None] * NG
            l1_done, l2_done, n1_used, nT_used = [None] * NG, [None] * NG, [None] * 2, [None] * 2
            h_done, tT_used, n2_used = [None] * NG, [None] * 2, [None] * 3

            def stats_of(src, G, ready, *waits):
                for i in range(GB):
                    t = do("vector", lambda e, i=i, tile=src(i): e.bn_stats(stats[:, G * GB + i, :], tile), ready, *waits)
                for i in range(GB):
                    t2 = do("vector", lambda e, i=i: e.bn_aggr(mv[:, G * GB + i, :], stats[:, G * GB + i, :]), t)
                g = group(G)
                t3 = do("gpsimd", lambda e: e.tensor_scalar(veps[:, g], mv[:, g, 1], EPS, None, ALU.add), t2)
                return do("gpsimd", lambda e: e.tensor_tensor(rstd[:, g], veps[:, g], minus_half[:, 0:GB],
                                                              ALU.pow), t3, t_half)

            def normal(dst, src, G, ready, *waits):
                for i in range(GB):
                    b = G * GB + i
                    t = do("vector", lambda e, b=b, to=dst(i), tile=src(i): e.tensor_scalar(
                        to, tile, mv[:, b, 0:1], rstd[:, b:b + 1], ALU.subtract, ALU.mult), ready, *waits)
                return t

            turned1, turned2, n_done = [None] * NG, [None] * NG, [None] * NG

            def norm1(G):
                s = G % 2
                n_done[G] = normal(lambda i: n1[:, s, i, :], lambda i: x_tok[:, G * GB + i, :], G, l1_done[G],
                                   n1_used[s])

            def turn1(G):
                s = G % 2
                n1_used[s] = t = turn(lambda i: n1[:, s, i, :], s, n_done[G], free[s])
                free[s] = turned1[G] = do("scalar", lambda e: e.activation(
                    nT[:, s, :, :], bank4(s), ACT.Identity, scale=col("ln1_g"), bias=col("ln1_b")), t, nT_used[s])

            def product1(G):
                s = G % 2
                for i in range(GB):
                    t4 = do("tensor", lambda e, i=i: e.matmul(ps[:, 2 + s, i * C:(i + 1) * C], nT[:, s, i, :],
                                                              W("attn_w"), start=True, stop=True),
                            turned1[G], free[2 + s], tell=i == GB - 1)
                nT_used[s] = t4

            def sum1(G):
                s = G % 2
                g = group(G)
                t4 = nT_used[s]
                h_done[G] = t5 = do("vector", lambda e: e.tensor_tensor(
                    hB[:, G % 3, :, :], bank4(2 + s), x_tok[:, g, :], ALU.add), t4)
                free[2 + s] = xh_done[G] = do("vector", lambda e: e.scalar_tensor_tensor(
                    x_tok[:, g, :], x_tok[:, g, :], 2.0, bank4(2 + s), ALU.mult, ALU.add), t5)
                l2_done[G] = stats_of(lambda i: hB[:, G % 3, i, :], G, h_done[G])

            def norm2(G):
                n_done[G] = t = normal(lambda i: n2[:, G % 3, i, :], lambda i: hB[:, G % 3, i, :], G, l2_done[G],
                                       row_store[G - 3] if G >= 3 else None, turned2[G - 3] if G >= 3 else None)
                row_store[G] = E.dma("sync", f"rows{G}", rows_d[G * GN:(G + 1) * GN, :].rearrange(
                    "(b t) c -> t b c", b=GB), n2[:, G % 3, :, :], t)

            def turn2(G):
                s = G % 2
                t = turned2[G] = turn(lambda i: n2[:, G % 3, i, :], 4 + s, n_done[G], free[4 + s])
                free[4 + s] = tT_ready[s] = do("scalar", lambda e: e.activation(
                    tT[:, s, :], ps[:, 4 + s, :], ACT.Identity, scale=col("ln2_g"), bias=col("ln2_b")), t, tT_used[s])

            def logits_of(G):
                s = G % 2
                for i in range(GB):
                    t = do("tensor", lambda e, i=i: e.matmul(
                        ps[:, 6, (G * GB + i) * 8:(G * GB + i) * 8 + 8], tT[:, s, i * S:(i + 1) * S],
                        gates[:, 0, :], start=True, stop=True), tT_ready[s], l_gates, tell=i == GB - 1)
                tT_used[s] = t
                return t

            tT_ready = [None] * 2
            l1_done[0] = stats_of(lambda i: x_tok[:, i, :], 0, x_done[0])
            for k in range(NG + 2):
                if k < NG:
                    norm1(k)
                    turn1(k)
                if k >= 2:
                    norm2(k - 2)
                    turn2(k - 2)
                if k < NG:
                    product1(k)
                if k >= 2:
                    t_logits = logits_of(k - 2)
                if k + 1 < NG:
                    l1_done[k + 1] = stats_of(lambda i: x_tok[:, (k + 1) * GB + i, :], k + 1, x_done[k + 1])
                if 1 <= k <= NG:
                    sum1(k - 1)

            weight = sb("rt_weight", [P, 2, NB], scope=scope)
            exp_i = sb("rt_exp_i", [1, NT], mybir.dt.int32, scope=scope)
            src_i = sb("rt_src", [P, NT], mybir.dt.int32, scope=scope)
            dst_i = sb("rt_dst", [P, NT], mybir.dt.int32, scope=scope)
            r_scope = ExitStack()
            wk = sb("rt_work", [P, 8, NB, NE0], scope=r_scope)
            sc = sb("rt_scalars", [P, 2, NB], scope=r_scope)
            slot = sb("rt_slot", [P, 2, NB], scope=r_scope)
            slot_i = sb("rt_slot_i", [P, 2, NB], mybir.dt.int32, scope=r_scope)
            hi = sb("rt_hi", [P, 2, NB], scope=r_scope)
            lo = sb("rt_lo", [P, 2, NB], scope=r_scope)
            tl = sb("rt_tiles", [P, 6, NE0], scope=r_scope)
            cmp32 = sb("rt_cmp", [P, NE0, NB], scope=r_scope)
            cmpT = sb("rt_cmpT", [1, NT, NE0], scope=r_scope)
            exp_f = sb("rt_exp_f", [1, NT], scope=r_scope)
            hotL = sb("rt_hotL", [P, 8, P], mybir.dt.float16, scope=r_scope)
            hotH = sb("rt_hotH", [P, 8, NT], mybir.dt.float16, scope=r_scope)
            inv = sb("rt_inv", [P, 6, NT], scope=r_scope)
            v = lambda f, *w: do("vector", f, *w)
            B3 = [P, NB, NE0]
            restart = sb("rt_restart", [P, NB * NE0], scope=r_scope)
            t_restart = do("gpsimd", lambda e: e.memset(restart[:, :], 1.0))
            t_restart = do("gpsimd", lambda e: e.memset(restart[:, :].rearrange("p (e b) -> p e b", e=NE0)[:, :, 0:1],
                                                        0.0), t_restart)
            eio = iotas[:, 0:NE0].unsqueeze(1).broadcast_to(B3)
            over_e = lambda x: x.unsqueeze(2).broadcast_to(B3)
            over_b = lambda x: x.unsqueeze(1).broadcast_to(B3)
            flat = lambda x: x.rearrange("p b e -> p (b e)")
            logits, oh1, oh2, rest = lg[:, :, :], wk[:, 0, :, :], wk[:, 1, :, :], wk[:, 2, :, :]
            tmp0, tmp1, scanA, scanB = wk[:, 3, :, :], wk[:, 4, :, :], wk[:, 5, :, :], wk[:, 6, :, :]
            a = v(lambda e: e.tensor_copy(lg[:, :, :], ps[:, 6, 0:NB * 8].rearrange("p (b e) -> p b e", b=NB)), t_logits)

            def first_max(src, onehot, top, a):
                a = v(lambda e: e.tensor_reduce(top, src, AX.X, ALU.max), a)
                a = v(lambda e: e.tensor_tensor(tmp0, src, over_e(top), ALU.is_lt), a)
                a = v(lambda e: e.scalar_tensor_tensor(tmp1, tmp0, 100.0, eio, ALU.mult, ALU.add), a, l_picks)
                a = v(lambda e: e.tensor_reduce(hi[:, 0, :], tmp1, AX.X, ALU.min), a)
                return v(lambda e: e.tensor_tensor(onehot, eio, over_e(hi[:, 0, :]), ALU.is_equal), a)
            a = first_max(logits, oh1, sc[:, 0, :], a)
            a = v(lambda e: e.scalar_tensor_tensor(flat(rest), flat(oh1), -3.0e38, flat(logits), ALU.mult, ALU.add), a)
            a = first_max(rest, oh2, sc[:, 1, :], a)
            a = v(lambda e: e.tensor_tensor(tmp0, oh1, oh2, ALU.add), a)
            tb = do("tensor", lambda e: e.matmul(ps[:, 0, 0:NB * 8], below, flat(tmp0), start=True, stop=True), a)
            tt = do("tensor", lambda e: e.matmul(ps[:, 1, 0:NB * 8], ones, flat(tmp0), start=True, stop=True), a)
            totals = ps[:, 1, 0:NB * 8].rearrange("p (b e) -> p b e", b=NB)
            within = ps[:, 0, 0:NB * 8].rearrange("p (b e) -> p b e", b=NB)
            a = v(lambda e: e.tensor_tensor(lo[:, 0, :], sc[:, 1, :], sc[:, 0, :], ALU.subtract), a)
            ex = do("scalar", lambda e: e.activation(lo[:, 1, :], lo[:, 0, :], ACT.Exp), a)
            by_e = lambda i: wk[:, i, :, :].rearrange("p b e -> p (b e)")
            a = v(lambda e: e.tensor_copy(by_e(5).rearrange("p (e b) -> p e b", e=NE0),
                                          totals.rearrange("p b e -> p e b")), tt)
            a = v(lambda e: e.tensor_tensor_scan(by_e(6), restart[:, :], by_e(5), 0.0, ALU.mult, ALU.add), a, t_restart)
            incl = by_e(6).rearrange("p (e b) -> p b e", e=NE0)
            count, ntile, base, base2 = [tl[:, i, :] for i in range(4)]
            a = v(lambda e: e.tensor_scalar(count, incl[:, NB - 1, :], 1.0 / P, None, ALU.mult), a)
            a = v(lambda e: e.tensor_tensor(cmp32[:, :, :], iotas[:, 0:NB].unsqueeze(1).broadcast_to([P, NE0, NB]),
                                            count.unsqueeze(2).broadcast_to([P, NE0, NB]), ALU.is_lt), a)
            a = v(lambda e: e.tensor_reduce(ntile, cmp32[:, :, :], AX.X, ALU.add), a)
            z = ntile
            bufs, sh = [base, base2], 1
            while sh < NE0:
                d = bufs[0]
                v(lambda e, z=z, d=d, sh=sh: e.tensor_copy(d[:, 0:sh], z[:, 0:sh]), a)
                a = v(lambda e, z=z, d=d, sh=sh: e.tensor_tensor(d[:, sh:NE0], z[:, sh:NE0], z[:, 0:NE0 - sh],
                                                                 ALU.add), a)
                z, bufs, sh = d, bufs[::-1], 2 * sh
            end = z
            a = v(lambda e: e.tensor_tensor(
                cmpT[:, :, :], iotas[0:1, 0:NT].unsqueeze(2).broadcast_to([1, NT, NE0]),
                end[0:1, :].unsqueeze(1).broadcast_to([1, NT, NE0]), ALU.is_ge), a)
            a = v(lambda e: e.tensor_reduce(exp_f[:, :], cmpT[:, :, :], AX.X, ALU.add), a)
            a = v(lambda e: e.tensor_scalar(exp_f[:, :], exp_f[:, :], float(NE0 - 1), float(I0), ALU.min, ALU.mult), a)
            t_exp = v(lambda e: e.tensor_copy(exp_i[:, :], exp_f[:, :]), a)
            start = tl[:, 4, :]
            a = v(lambda e: e.tensor_tensor(tl[:, 5, :], end, ntile, ALU.subtract), t_exp)
            a = v(lambda e: e.tensor_scalar(start, tl[:, 5, :], float(P), None, ALU.mult), a)
            a = v(lambda e: e.tensor_tensor(tmp0, incl, totals, ALU.subtract), a)
            a = v(lambda e: e.tensor_tensor(tmp1, tmp0, within, ALU.add), a, tb)
            a = v(lambda e: e.tensor_tensor(tmp0, tmp1, over_b(start), ALU.add), a)
            a1 = v(lambda e: e.tensor_tensor(tmp1, tmp0, oh1, ALU.mult), a)
            a2 = v(lambda e: e.tensor_tensor(rest, tmp0, oh2, ALU.mult), a)
            a = v(lambda e: e.tensor_reduce(slot[:, 0, :], tmp1, AX.X, ALU.add), a1)
            a = v(lambda e: e.tensor_reduce(slot[:, 1, :], rest, AX.X, ALU.add), a2, a)
            a = v(lambda e: e.tensor_copy(slot_i[:, :, :], slot[:, :, :]), a)
            a = v(lambda e: e.tensor_single_scalar(slot_i[:, :, :], slot_i[:, :, :], 7, ALU.arith_shift_right), a)
            a = v(lambda e: e.tensor_scalar(weight[:, 0, :], lo[:, 1, :], 1.0, None, ALU.add), a, ex)
            a = v(lambda e: e.reciprocal(weight[:, 0, :], weight[:, 0, :]), a)
            t_w = v(lambda e: e.tensor_tensor(weight[:, 1, :], weight[:, 0, :], lo[:, 1, :], ALU.mult), a)
            a = v(lambda e: e.tensor_copy(hi[:, :, :], slot_i[:, :, :]), t_w)
            a = v(lambda e: e.scalar_tensor_tensor(
                lo[:, :, :].rearrange("p k b -> p (k b)"), hi[:, :, :].rearrange("p k b -> p (k b)"), -float(P),
                slot[:, :, :].rearrange("p k b -> p (k b)"), ALU.mult, ALU.add), a)
            HB = NB // 2
            hot_used = [None] * 8
            n = 0
            for k in range(2):
                for b in range(NB):
                    i = n % 8
                    tl_ = v(lambda e, i=i, k=k, b=b: e.tensor_scalar(
                        hotL[:, i, :], iota16[:, 0:P], lo[:, k, b:b + 1], None, ALU.is_equal), a, hot_used[i], t_i16)
                    th_ = do("gpsimd" if n % 4 == 3 else "vector", lambda e, i=i, k=k, b=b: e.tensor_scalar(
                        hotH[:, i, :], iota16[:, 0:NT], hi[:, k, b:b + 1], tokens[:, b % HB:b % HB + 1],
                        ALU.is_equal, ALU.mult), a, hot_used[i])
                    r = 2 * k + b // HB
                    hot_used[i] = t = do("tensor", lambda e, i=i, r=r, b=b: e.matmul(
                        ps[:, 2, r * NT:(r + 1) * NT], hotL[:, i, :], hotH[:, i, :],
                        start=b % HB == 0, stop=b % HB == HB - 1), th_, tl_)
                    n += 1
            q = lambda i: inv[:, i, :]
            part = lambda r: ps[:, 2, r * NT:(r + 1) * NT]
            a = v(lambda e: e.tensor_copy(q(0), part(1)), t)
            a = v(lambda e: e.tensor_tensor(q(1), q(0), part(3), ALU.add), a)
            b_ = v(lambda e: e.tensor_copy(q(2), part(2)), a)
            b_ = v(lambda e: e.tensor_tensor(q(3), q(2), part(3), ALU.add), b_)
            a = v(lambda e: e.tensor_tensor(q(0), q(1), part(0), ALU.add), b_)
            a = v(lambda e: e.tensor_tensor(q(0), q(0), q(2), ALU.add), a)
            a = v(lambda e: e.tensor_scalar(q(1), q(1), 0.0, float(NB * S // 2), ALU.is_gt, ALU.mult), a)
            a = v(lambda e: e.tensor_tensor(q(1), q(1), q(0), ALU.add), a)
            a = v(lambda e: e.tensor_scalar(q(2), q(1), -1.0, 0.0, ALU.add, ALU.max), a)
            t_src = v(lambda e: e.tensor_copy(src_i[:, :], q(2)), a)
            a = v(lambda e: e.tensor_scalar(q(3), q(3), 0.0, float(NB * S), ALU.is_gt, ALU.mult), t_src)
            a = v(lambda e: e.tensor_tensor(q(3), q(3), q(2), ALU.add), a)
            a = v(lambda e: e.tensor_scalar(q(4), q(1), 0.0, 4.0 * NB * S, ALU.is_le, ALU.mult), a)
            a = v(lambda e: e.tensor_tensor(q(4), q(4), q(3), ALU.add), a)
            t_dst = v(lambda e: e.tensor_copy(dst_i[:, :], q(4)), a)
            E.join()
            r_scope.close()

            xg = sb("tile_x", [P, NX, C], scope=scope)
            xgT = sb("tile_xT", [P, NX, P], scope=scope)
            gS = sb("tile_g", [P, 2, I0], scope=scope)
            hS = sb("tile_h", [P, 2, I0], scope=scope)
            hT = sb("tile_hT", [P, 2, I0], scope=scope)
            yS = sb("tile_y", [P, NX, C], scope=scope)
            KC = I0 // P
            gate_f, up_f, down_f = [expert_w[:, i * n0:(i + 1) * n0] for i in range(3)]
            got, stored, yready = [None] * NT, [None] * NT, [None] * NT
            bfree = [None] * 8
            xT_ready, h_ready, hT_ready, xT_used, hT_used, xg_used, gS_used = [
                [None] * NT for _ in range(7)]
            at = {}

            def before(tokens, i):
                return tokens[i] if i >= 0 else None

            gather_sem = [E.sem(f"gathered{i}") for i in range(NX)]
            scatter_sem = [E.sem(f"scattered{i}") for i in range(NX)]

            def gather(j):
                i = j % NX
                E.queue["gpsimd"].append([
                    [w for w in (t_src, before(xg_used, j - NX), *(row_store if j == 0 else ())) if w],
                    lambda e: e.indirect_dma_start(
                        out=xg[:, i, :], out_offset=None, in_=rows_d,
                        in_offset=bass.IndirectOffsetOnAxis(ap=src_i[:, j:j + 1], axis=0)),
                    gather_sem[i], 16])
                got[j] = (gather_sem[i], 16 * (j // NX + 1))

            def tile_turn(j):
                i = j % NX
                xg_used[j] = t = do("tensor", lambda e: e.transpose(ps[:, 6, 0:P], xg[:, i, :], ident),
                                    got[j], bfree[6])
                bfree[6] = xT_ready[j] = do("scalar", lambda e: e.activation(
                    xgT[:, i, :], ps[:, 6, 0:P], ACT.Identity, scale=col("ln2_g"), bias=col("ln2_b")),
                    t, before(xT_used, j - NX))

            def tile_offset(j):
                def load(e):
                    at[j] = e.value_load(exp_i[0:1, j:j + 1], min_val=0, max_val=(NE0 - 1) * I0)
                E.queue["tensor"].append([[t_exp], load, None, 0])

            def tile_gate_up(j):
                bg, bu = (0, 1) if j % 2 == 0 else (2, 3)
                i = j % NX
                tg = do("tensor", lambda e: e.matmul(ps[:, bg, :], xgT[:, i, :], gate_f[:, bass.ds(at[j], I0)],
                                                     start=True, stop=True), xT_ready[j], bfree[bg])
                xT_used[j] = tu = do("tensor", lambda e: e.matmul(
                    ps[:, bu, :], xgT[:, i, :], up_f[:, bass.ds(at[j], I0)], start=True, stop=True), bfree[bu])
                bfree[bg] = t = do("scalar", lambda e: e.activation(gS[:, j % 2, :], ps[:, bg, :], ACT.Silu),
                                   tg, before(h_ready, j - 2))
                bfree[bu] = h_ready[j] = do("vector", lambda e: e.tensor_tensor(
                    hS[:, j % 2, :], gS[:, j % 2, :], ps[:, bu, :], ALU.mult), t, tu, before(hT_used, j - 2))

            def tile_turn_h(j):
                for k in range(KC):
                    t = do("tensor", lambda e, k=k: e.transpose(
                        ps[:, 4 + j % 2, k * P:(k + 1) * P], hS[:, j % 2, k * P:(k + 1) * P], ident),
                        h_ready[j], bfree[4 + j % 2], tell=k == KC - 1)
                hT_used[j] = t
                bfree[4 + j % 2] = hT_ready[j] = do("scalar", lambda e: e.copy(hT[:, j % 2, :], ps[:, 4 + j % 2, :]),
                                                    t, before(yready, j - 2))

            def tile_down(j):
                for k in range(KC):
                    t = do("tensor", lambda e, k=k: e.matmul(
                        ps[:, 7, 0:C], hT[:, j % 2, k * P:(k + 1) * P],
                        down_f[:, k * P:n0 - (KC - 1 - k) * P][:, bass.ds(at[j], C)],
                        start=k == 0, stop=k == KC - 1), hT_ready[j], bfree[7], tell=k == KC - 1)
                yready[j] = t
                i = j % NX
                bfree[7] = t2 = do("vector", lambda e: e.tensor_copy(yS[:, i, :], ps[:, 7, 0:C]), t,
                                   before(stored, j - NX))
                E.queue["gpsimd"].append([[t2, t_dst], lambda e: e.indirect_dma_start(
                    out=y_d, out_offset=bass.IndirectOffsetOnAxis(ap=dst_i[:, j:j + 1], axis=0),
                    in_=yS[:, i, :], in_offset=None, bounds_check=2 * NB * S - 1, oob_is_err=False),
                    scatter_sem[i], 16])
                stored[j] = (scatter_sem[i], 16 * (j // NX + 1))

            for l in l_moe0:
                E.wait("tensor", l)
            for j in range(3):
                gather(j)
            tile_turn(0)
            tile_offset(0)
            for j in range(NT + 2):
                if j < NT:
                    tile_gate_up(j)
                    if j + 1 < NT:
                        tile_offset(j + 1)
                if j + 1 < NT:
                    tile_turn(j + 1)
                if 1 <= j <= NT:
                    tile_turn_h(j - 1)
                if j >= 2:
                    tile_down(j - 2)
                if j + 3 < NT:
                    gather(j + 3)
            E.wait("sync", *stored[-NX:])

            y2 = sb("moe_y2", [P, 3, 2, GB, C], scope=scope)
            fin = [None] * NG
            for G in range(NG + 2):
                if G < NG:
                    s = G % 3
                    ly = [E.dma("sync", f"y{G}_{k}", y2[:, s, k, :, :],
                                y_d[k * NB * S + G * GN:k * NB * S + (G + 1) * GN, :].rearrange(
                                    "(b t) c -> t b c", b=GB), fin[G - 3] if G >= 3 else None) for k in range(2)]
                    for k in range(2):
                        for i in range(GB):
                            b = G * GB + i
                            t = do("vector", lambda e, k=k, i=i, b=b, s=s: e.scalar_tensor_tensor(
                                x_tok[:, b, :], y2[:, s, k, i, :], weight[:, k, b:b + 1], x_tok[:, b, :],
                                ALU.mult, ALU.add), ly[k], t_w, xh_done[G], t if k else None)
                    fin[G] = layer_stats(G, t)
                if 1 <= G <= NG:
                    x_done[G - 1] = normalize(G - 1, fin[G - 1])
                if G >= 2:
                    g = G - 2
                    xT_done[g] = bfree[g % 2] = renew_xT(g, x_done[g], g % 2, bfree[g % 2])
            E.join()
            scope.close()

        def memory():
            scope = ExitStack()
            E.stage("memory")
            n1 = NE1 * I1
            w1 = expert_w[:, 0:n1].rearrange("p (e i) -> p e i", e=NE1)
            w3 = expert_w[:, n1:2 * n1].rearrange("p (e i) -> p e i", e=NE1)
            w2 = expert_w[:, 2 * n1:3 * n1].rearrange("p (e k c) -> p e k c", e=NE1, c=C)
            l_moe1 = [E.dma("sync", "w1_T", w1, D["w1_T"]), E.dma("sync", "w3_T", w3, D["w3_T"]),
                      E.dma("sync", "w2_T", w2, D["w2_T"])]
            wc = sb("mem_wc", [P, P], scope=scope)
            sm = sb("mem_scalars", [P, 6], scope=scope)
            mT = sb("mem_mask", [P, P], scope=scope)
            mT0 = sb("mem_exp", [P, P], scope=scope)
            vC = sb("mem_v", [P, 2, GB, C], scope=scope)
            sM = sb("mem_s", [P, 2, GB, S], scope=scope)
            a = do("scalar", lambda e: e.activation(sm[:, 0:1], col("decay"), ACT.Exp, scale=-1.0))
            b_ = do("scalar", lambda e: e.activation(sm[:, 4:5], col("log_alpha"), ACT.Exp))
            a = do("vector", lambda e: e.tensor_scalar(sm[:, 1:2], sm[:, 0:1], 1.0, None, ALU.add), a)
            a = do("vector", lambda e: e.reciprocal(sm[:, 2:3], sm[:, 1:2]), a)
            a = do("scalar", lambda e: e.activation(sm[:, 3:4], sm[:, 2:3], ACT.Ln), a)
            a = do("scalar", lambda e: e.activation(mT0[:, :], diffs, ACT.Exp, scale=sm[:, 3:4]), a)
            t_mask = do("vector", lambda e: e.tensor_tensor(mT[:, :], mT0[:, :], causal, ALU.mult), a)
            t = do("tensor", lambda e: e.matmul(ps[:, 7, 0:P], W("w_write"), W("w_read"), start=True, stop=True))
            t_wc = do("vector", lambda e: e.tensor_scalar(wc[:, :], ps[:, 7, 0:P], sm[:, 4:5], None, ALU.mult),
                      t, b_)
            free = [None] * 8
            s_used, pend = [None] * 2, [None] * NG
            s_ready, v_ready = [None] * NG, [None] * NG
            for G in range(NG + 2):
                if G < NG:
                    s = G % 2
                    for i in range(GB):
                        t = do("tensor", lambda e, i=i, G=G, s=s: e.matmul(
                            ps[:, s, i * C:(i + 1) * C], x_T[:, G * GB + i, :], wc[:, :], start=True, stop=True),
                            t_wc, free[s], tell=i == GB - 1)
                    v_ready[G] = free[s] = do("scalar", lambda e, s=s: e.copy(vC[:, s, :, :], bank4(s)), t, s_used[s])
                    for i in range(GB):
                        c0 = 8 + (G * GB + i) * S
                        t = do("tensor", lambda e, i=i, G=G, s=s, c0=c0: e.matmul(
                            ps[:, 2 + s, i * S:(i + 1) * S], x_Tp[:, c0 - 1:c0 - 1 + S],
                            x_T[:, G * GB + i, :], start=True, stop=True), free[2 + s], t_pad, tell=i == GB - 1)
                    mb = mT[:, :].unsqueeze(1).broadcast_to([P, GB, S])
                    s_ready[G] = free[2 + s] = do("vector", lambda e, s=s: e.tensor_tensor(
                        sM[:, s, :, :], bank4(2 + s), mb, ALU.mult), t, t_mask, s_used[s])
                if G >= 1 and G - 1 < NG:
                    g = G - 1
                    s = g % 2
                    for i in range(GB):
                        t = do("tensor", lambda e, i=i, s=s: e.matmul(
                            ps[:, 4 + s, i * C:(i + 1) * C], sM[:, s, i, :], vC[:, s, i, :], start=True, stop=True),
                            s_ready[g], v_ready[g], free[4 + s], tell=i == GB - 1)
                    s_used[s] = t
                    free[4 + s], pend[g] = residual(g, bank4(4 + s), t, 2.0)
                if G >= 2:
                    g = G - 2
                    x_done[g] = normalize(g, pend[g])
            for g in range(NG):
                xT_done[g] = free[6 + g % 2] = renew_xT(g, x_done[g], 6 + g % 2, free[6 + g % 2])
            E.join()
            scope.close()
            return w1, w3, w2, l_moe1

        def expert_choice(w1, w3, w2, l_moe1):
            scope = ExitStack()
            E.stage("choice")
            JR = P // NE1
            TW = NB * S // JR
            BJ = TW // S
            K = 26
            TILES = CAP // P
            LO, HI = 32, CAP // 32
            FAR = 3.0e38
            F16 = mybir.dt.float16
            v = lambda f, *w: do("vector", f, *w)
            pe = lambda f, *w: do("tensor", f, *w)
            r_scope = ExitStack()
            idx_i = sb("ch_token", [P, NE1 * TILES], mybir.dt.int32, scope=scope)
            edge = sb("ch_edge", [P, NE1 + 2], scope=scope)
            rsum = sb("ch_rsum", [P, NE1], scope=scope)
            sA = sb("ch_scores", [P, TW], scope=r_scope)
            fl = sb("ch_flags", [P, 6, TW], scope=r_scope)
            eS = sb("ch_exp", [P, TW], scope=r_scope)
            one = sb("ch_ones", [P, TW], scope=r_scope)
            junk = sb("ch_junk", [P, TW], F16, scope=r_scope)
            same16 = sb("ch_same", [P, P], F16, scope=r_scope)
            cnt = sb("ch_count", [P, 1], F16, scope=r_scope)
            mids = sb("ch_mids", [P, K + 1], scope=r_scope)
            half = sb("ch_halves", [P, K + 1], scope=r_scope)
            nhalf = sb("ch_minus_halves", [P, K + 1], scope=r_scope)
            step = sb("ch_step", [P, 2], scope=r_scope)
            rm = sb("ch_row_max", [P, 2], scope=r_scope)
            row = sb("ch_rows", [1, P + NE1 + 2], scope=r_scope)
            side = sb("ch_side", [P, 2, K], scope=r_scope)
            sm = sb("ch_small", [P, 12], scope=r_scope)
            per_e = sb("ch_per_expert", [P, NE1], scope=r_scope)
            rk_i = sb("ch_rank_i", [P, 2, NB, NE1], mybir.dt.int32, scope=r_scope)
            rk = sb("ch_rank", [P, 2, NB * NE1], F16, scope=r_scope)
            tok16 = sb("ch_tok16", [P, NB // 2], F16, scope=r_scope)
            hotL = sb("ch_hotL", [P, NB * NE1, LO], F16, scope=r_scope)
            hotH = sb("ch_hotH", [P, NB * NE1, HI], F16, scope=r_scope)
            inv = sb("ch_inv", [P, 4, 2, HI], scope=r_scope)

            for j in range(JR):
                t = pe(lambda e, j=j: e.matmul(ps[:, 0, 0:TW], gate_pad[:, JR - 1 - j:JR - 1 - j + P],
                                               x_T[:, BJ * j:BJ * (j + 1), :], start=j == 0, stop=j == JR - 1),
                       l_gate_pad)
            t_one = do("gpsimd", lambda e: e.memset(one[:, :], 1.0))
            t_same = do("gpsimd", lambda e: e.tensor_copy(same16[:, :], same))
            t_tok = do("gpsimd", lambda e: e.tensor_copy(tok16[:, :], tokens))
            a = v(lambda e: e.tensor_copy(sA[:, :], ps[:, 0, 0:TW]), t)
            a = v(lambda e: e.tensor_reduce(rm[:, 0:1], sA[:, :], AX.X, ALU.max), a)
            a = v(lambda e: e.tensor_reduce(rm[:, 1:2], sA[:, :], AX.X, ALU.max, apply_absolute_value=True), a)
            for i in range(2):
                t = pe(lambda e, i=i: e.transpose(ps[0:1, 1, i * P:(i + 1) * P], rm[:, i:i + 1], ident), a)
            a = v(lambda e: e.tensor_reduce(row[:, P + NE1 + 1:P + NE1 + 2],
                                            ps[0:1, 1, 0:P].rearrange("p (e j) -> p e j", e=NE1)[:, 0, :],
                                            AX.X, ALU.max), t)
            a = v(lambda e: e.tensor_reduce(row[:, P:P + NE1], ps[0:1, 1, 0:P].rearrange("p (e j) -> p e j", e=NE1),
                                            AX.X, ALU.max), a)
            a = v(lambda e: e.tensor_scalar(row[:, P:P + NE1], row[:, P:P + NE1], -1.0, None, ALU.mult), a)
            a = v(lambda e: e.tensor_reduce(row[:, P + NE1:P + NE1 + 1], ps[0:1, 1, P:2 * P], AX.X, ALU.max), a)
            a = v(lambda e: e.tensor_copy(row[:, 0:P].rearrange("p (e j) -> p e j", e=NE1),
                                          row[:, P:P + NE1].unsqueeze(2).broadcast_to([1, NE1, JR])), a)
            t = pe(lambda e: e.matmul(ps[:, 2, 0:NE1 + 1], ones[0:1, :], row[0:1, P:P + NE1 + 1],
                                      start=True, stop=True), a)
            t = pe(lambda e: e.matmul(ps[:, 2, NE1 + 1:NE1 + 2], row[0:1, 0:P], ones[0:1, 0:1],
                                      start=True, stop=True), a)
            a = t_edge = v(lambda e: e.tensor_copy(edge[:, :], ps[:, 2, 0:NE1 + 2]), t)
            big = edge[:, NE1:NE1 + 1]
            t_exp = do("scalar", lambda e: e.activation(eS[:, :], sA[:, :], ACT.Exp, bias=edge[:, NE1 + 1:NE1 + 2]), a)
            v(lambda e: e.memset(mids[:, 0:1], 0.0))
            v(lambda e: e.tensor_scalar(half[:, :], powers, big, None, ALU.mult), a)
            a = v(lambda e: e.tensor_scalar(nhalf[:, :], powers, big, -1.0, ALU.mult, ALU.mult), a)
            for k in range(K):
                g = v(lambda e, k=k: e.tensor_scalar(junk[:, :], sA[:, :], mids[:, k:k + 1], 0.0, ALU.is_ge, ALU.add,
                                                     accum_out=cnt[:, :]), a)
                g = pe(lambda e, k=k: e.matmul(ps[:, 3, k:k + 1], same16[:, :], cnt[:, :], start=True, stop=True),
                       g, t_same)
                g = v(lambda e, k=k: e.tensor_scalar(step[:, 0:1], ps[:, 3, k:k + 1], float(CAP), half[:, k:k + 1],
                                                     ALU.is_ge, ALU.mult), g)
                a = v(lambda e, k=k: e.scalar_tensor_tensor(mids[:, k + 1:k + 2], step[:, 0:1], mids[:, k:k + 1],
                                                            nhalf[:, k + 1:k + 2], ALU.add, ALU.add), g)
            lo, hi = sm[:, 0:1], sm[:, 1:2]
            g = v(lambda e: e.tensor_scalar(side[:, 0, :], ps[:, 3, 0:K], float(CAP), -FAR, ALU.is_lt, ALU.mult), a)
            g1 = v(lambda e: e.tensor_scalar(side[:, 1, :], ps[:, 3, 0:K], float(CAP), FAR, ALU.is_ge, ALU.mult), a)
            g = v(lambda e: e.tensor_tensor(side[:, 0, :], side[:, 0, :], mids[:, 0:K], ALU.add), g)
            g1 = v(lambda e: e.tensor_tensor(side[:, 1, :], side[:, 1, :], mids[:, 0:K], ALU.add), g1)
            g = v(lambda e: e.tensor_reduce(lo, side[:, 0, :], AX.X, ALU.max), g)
            a = v(lambda e: e.tensor_reduce(hi, side[:, 1, :], AX.X, ALU.min), g1)
            sure, tied, upto, sel, rank = [fl[:, i, :] for i in range(5)]
            a = v(lambda e: e.tensor_scalar(sure, sA[:, :], hi, 0.0, ALU.is_ge, ALU.add, accum_out=sm[:, 2:3]), a)
            a = v(lambda e: e.scalar_tensor_tensor(tied, sA[:, :], lo, sure, ALU.is_ge, ALU.subtract), a, g)
            a = v(lambda e: e.tensor_tensor_scan(upto, one[:, :], tied, 0.0, ALU.mult, ALU.add), a, t_one)
            t = pe(lambda e: e.matmul(ps[:, 4, 0:1], same, sm[:, 2:3], start=True, stop=False), a)
            t = pe(lambda e: e.matmul(ps[:, 4, 0:1], before16, upto[:, TW - 1:TW], start=False, stop=True), a)
            a = v(lambda e: e.tensor_scalar(sm[:, 3:4], ps[:, 4, 0:1], -1.0, float(CAP), ALU.mult, ALU.add), t)
            a = v(lambda e: e.scalar_tensor_tensor(upto, upto, sm[:, 3:4], tied, ALU.is_le, ALU.mult), a)
            a = t_sel = v(lambda e: e.tensor_tensor(sel, upto, sure, ALU.add), a)
            a = v(lambda e: e.tensor_tensor_scan(rank, one[:, :], sel, 0.0, ALU.mult, ALU.add), a)
            t = pe(lambda e: e.matmul(ps[:, 4, 1:2], before16, rank[:, TW - 1:TW], start=True, stop=True), a)
            a = v(lambda e: e.tensor_copy(sm[:, 4:5], ps[:, 4, 1:2]), t)
            a = v(lambda e: e.scalar_tensor_tensor(rank, rank, sm[:, 4:5], sel, ALU.add, ALU.mult), a)
            for h in range(BJ):
                t = pe(lambda e, h=h: e.transpose(ps[:, 5, h * P:(h + 1) * P], rank[:, h * S:(h + 1) * S], ident), a)
            rank_T = ps[:, 5, 0:BJ * P].rearrange("p (h e j) -> p j h e", h=BJ, j=JR)
            r0, r1 = rk_i[:, 0, :, :], rk_i[:, 1, :, :]
            fl0, fl1 = [rk_i[:, i, :, :].rearrange("p b e -> p (b e)") for i in range(2)]
            for h in range(BJ):
                a = v(lambda e, h=h: e.tensor_scalar(
                    r0.rearrange("p (j h) e -> p j h e", h=BJ)[:, :, h, :], rank_T[:, :, h, :], -1.0, None, ALU.add), t)
            g = v(lambda e: e.tensor_single_scalar(fl1, fl0, 5, ALU.arith_shift_right), a)
            g1 = v(lambda e: e.tensor_single_scalar(fl0, fl0, LO - 1, ALU.bitwise_and), g)
            g = v(lambda e: e.tensor_copy(rk[:, 1, :], fl1), g)
            g1 = v(lambda e: e.tensor_copy(rk[:, 0, :], fl0), g1)
            HB = NB // 2
            EH = 4
            for hf in range(2):
                w = slice(hf * HB * NE1, (hf + 1) * HB * NE1)
                n = HB * NE1
                gh = v(lambda e, w=w: e.tensor_tensor(
                    hotH[:, w, :], iota16[:, 0:HI].unsqueeze(1).broadcast_to([P, n, HI]),
                    rk[:, 1, w].unsqueeze(2).broadcast_to([P, n, HI]), ALU.is_equal), g)
                gl = v(lambda e, w=w: e.tensor_tensor(
                    hotL[:, w, :], iota16[:, 0:LO].unsqueeze(1).broadcast_to([P, n, LO]),
                    rk[:, 0, w].unsqueeze(2).broadcast_to([P, n, LO]), ALU.is_equal), g1)
                hv = hotH[:, w, :].rearrange("p (b e) i -> p b (e i)", b=HB)
                gh = do("gpsimd", lambda e, hv=hv: e.tensor_tensor(
                    hv, hv, tok16[:, :].unsqueeze(2).broadcast_to([P, HB, NE1 * HI]), ALU.mult), gh, t_tok)
                for q in range(NE1 // EH):
                    c0 = (q * 2 + hf) * EH * HI
                    for b in range(HB):
                        r = (hf * HB + b) * NE1 + q * EH
                        t = pe(lambda e, b=b, c0=c0, r=r: e.matmul(
                            ps[:, 6, c0:c0 + EH * HI], hotL[:, r:r + EH, :].rearrange("p e i -> p (e i)"),
                            hotH[:, r:r + EH, :].rearrange("p e i -> p (e i)"), start=b == 0, stop=b == HB - 1),
                            gh, gl)
            part = ps[:, 6, 0:4 * EH * HI].rearrange("p (q f e i) -> p f q e i", q=2, f=2, e=EH)
            for x in range(EH):
                a = v(lambda e, x=x: e.tensor_copy(inv[32 * x:32 * x + 32, 0:2, :, :],
                                                   part[32 * x:32 * x + 32, :, :, x, :]), t)
            A, B_, C_, D_ = [inv[:, i, :, :].rearrange("p q i -> p (q i)") for i in range(4)]
            a = v(lambda e: e.tensor_scalar(C_, B_, 0.0, float(HB * S), ALU.is_gt, ALU.mult), a)
            a = v(lambda e: e.tensor_tensor(A, A, B_, ALU.add), a)
            a = v(lambda e: e.scalar_tensor_tensor(D_, C_, -1.0, A, ALU.add, ALU.add), a)
            where = inv[:, 3, :, :].rearrange("p q (t u) -> p q u t", u=P // LO)
            for x in range(EH):
                for u in range(P // LO):
                    dst = ps[LO * u:LO * u + LO, 7, 0:NE1 * TILES].rearrange("p (q x t) -> p q x t", q=2, x=EH)
                    t = pe(lambda e, x=x, u=u, dst=dst: e.matmul(
                        dst[:, :, x, :], ident[:, LO * x:LO * x + LO], where[:, :, u, :], start=True, stop=True), a)
            t_idx = a = v(lambda e: e.tensor_copy(idx_i[:, :], ps[:, 7, 0:NE1 * TILES]), t)
            a = v(lambda e: e.scalar_tensor_tensor(fl[:, 5, :], eS[:, :], 1.0, sel, ALU.mult, ALU.mult,
                                                   accum_out=sm[:, 5:6]), a, t_exp)
            a = v(lambda e: e.tensor_scalar(per_e[:, :], expert_of, sm[:, 5:6], None, ALU.mult), a)
            t = pe(lambda e: e.matmul(ps[:, 4, 8:8 + NE1], ones, per_e[:, :], start=True, stop=True), a)
            t_rsum = v(lambda e: e.reciprocal(rsum[:, :], ps[:, 4, 8:8 + NE1]), t)
            E.join()
            r_scope.close()

            NC = I1 // P
            NXG, NY = 4, 2
            xg = sb("ch_x", [P, NXG, TILES, C], scope=scope)
            xgT = sb("ch_xT", [P, NE1, CAP], scope=scope)
            gS = sb("ch_g", [P, 2, NC, CAP], scope=scope)
            hS = sb("ch_h", [P, 2, NC, CAP], scope=scope)
            yS = sb("ch_y", [P, NY, TILES, C], scope=scope)
            wS = sb("ch_w", [P, NE1, TILES], scope=scope)
            bfree = [None] * 8
            got, xT_ready, xT_read, h_ready, h_used, g_used = [[None] * NE1 for _ in range(6)]
            weighted = [None] * NE1
            gather_sem = [E.sem(f"choice_gathered{i}") for i in range(NXG)]
            scatter_sem = E.sem("choice_scattered")
            all_tiles = 16 * TILES

            def before(tokens, i):
                return tokens[i] if i >= 0 else None

            def gather(x):
                for i in range(TILES):
                    n = x * TILES + i
                    E.queue["gpsimd"].append([
                        [w for w in (t_idx, before(xT_read, x - NXG), *(row_store if x == 0 else ())) if w],
                        lambda e, n=n, i=i: e.indirect_dma_start(
                            out=xg[:, x % NXG, i, :], out_offset=None, in_=rows_d,
                            in_offset=bass.IndirectOffsetOnAxis(ap=idx_i[:, n:n + 1], axis=0)),
                        gather_sem[x % NXG], 16])
                got[x] = (gather_sem[x % NXG], all_tiles * (x // NXG + 1))

            def turn_x(x):
                for i in range(TILES):
                    t = pe(lambda e, i=i: e.transpose(ps[:, 4, i * P:(i + 1) * P], xg[:, x % NXG, i, :], ident),
                           got[x], bfree[4])
                xT_read[x] = t
                bfree[4] = xT_ready[x] = do("scalar", lambda e: e.copy(xgT[:, x, :], ps[:, 4, :]), t)

            def slot_scores(x):
                for i in range(TILES):
                    n = (x * TILES + i) * NE1
                    t = pe(lambda e, i=i, n=n: e.matmul(ps[:, 5, n:n + NE1], xgT[:, x, i * P:(i + 1) * P],
                                                        gates[:, 1, :], start=True, stop=True), xT_ready[x], bfree[5])
                src = ps[:, 5, x * TILES * NE1:(x + 1) * TILES * NE1].rearrange("p (i e) -> p i e", e=NE1)
                bfree[5] = weighted[x] = do("scalar", lambda e: e.activation(
                    wS[:, x, :], src[:, :, x], ACT.Exp, bias=edge[:, x:x + 1]), t)

            def gate_up(x):
                for c in range(NC):
                    bg, bu = 2 * c, 2 * c + 1
                    tg = pe(lambda e, c=c, bg=bg: e.matmul(ps[:, bg, :], w1[:, x, c * P:(c + 1) * P], xgT[:, x, :],
                                                           start=True, stop=True), xT_ready[x], bfree[bg])
                    tu = pe(lambda e, c=c, bu=bu: e.matmul(ps[:, bu, :], w3[:, x, c * P:(c + 1) * P], xgT[:, x, :],
                                                           start=True, stop=True), bfree[bu])
                    bfree[bg] = ts = do("scalar", lambda e, c=c, bg=bg: e.activation(
                        gS[:, x % 2, c, :], ps[:, bg, :], ACT.Silu), tg, before(h_ready, x - 2))
                    bfree[bu] = th = v(lambda e, c=c, bu=bu: e.tensor_tensor(
                        hS[:, x % 2, c, :], gS[:, x % 2, c, :], ps[:, bu, :], ALU.mult),
                        ts, tu, before(h_used, x - 2))
                h_ready[x] = th

            def down(x):
                bank = 6 + x % 2
                for i in range(TILES):
                    for c in range(NC):
                        t = pe(lambda e, i=i, c=c: e.matmul(
                            ps[:, bank, i * C:(i + 1) * C], hS[:, x % 2, c, i * P:(i + 1) * P], w2[:, x, c, :],
                            start=c == 0, stop=c == NC - 1), h_ready[x], bfree[bank])
                h_used[x] = t
                for i in range(TILES):
                    t2 = v(lambda e, i=i: e.tensor_scalar(
                        yS[:, x % NY, i, :], ps[:, bank, i * C:(i + 1) * C], wS[:, x, i:i + 1], rsum[:, x:x + 1],
                        ALU.mult, ALU.mult), t, weighted[x], (scatter_sem, all_tiles * (x - NY + 1)) if x >= NY else None)
                    n = x * TILES + i
                    E.queue["gpsimd"].append([
                        [t2, *([(scatter_sem, all_tiles * x)] if x else sum_store)],
                        lambda e, n=n, i=i: e.indirect_dma_start(
                            out=sums_d, out_offset=bass.IndirectOffsetOnAxis(ap=idx_i[:, n:n + 1], axis=0),
                            in_=yS[:, x % NY, i, :], in_offset=None, compute_op=ALU.add),
                        scatter_sem, 16])
                bfree[bank] = t2

            for l in l_moe1:
                E.wait("tensor", l)
            for x in range(NXG - 1):
                gather(x)
            for x in range(NE1 + 1):
                if x < NE1:
                    turn_x(x)
                    slot_scores(x)
                    gate_up(x)
                if x >= 1:
                    down(x - 1)
                if x + NXG - 1 < NE1:
                    gather(x + NXG - 1)
            fin = [None] * NG
            done = [(scatter_sem, all_tiles * NE1)]
            for G in range(NG + 1):
                if G < NG:
                    l = E.dma("sync", f"sum{G}", x_tok[:, group(G), :],
                              sums_d[G * GN:(G + 1) * GN, :].rearrange("(b t) c -> t b c", b=GB), *done)
                    fin[G] = layer_stats(G, l)
                if G >= 1:
                    g = G - 1
                    x_done[g] = normalize(g, fin[g])
            scope.close()

        cross_attention("x0", False)
        moe_top2()
        got = memory()
        cross_attention("x1", True)
        expert_choice(*got)
        output()
        E.wait("sync", *stores)
        with nc.Block() as block:
            E.emit(block)


PROJ = ["ret_q", "ret_k", "ret_v", "ret_o", "x0_q", "x0_k", "x0_v", "x0_o", "attn_w",
        "w_write", "w_read", "x1_q", "x1_k", "x1_v", "x1_o"]
COLS = ["gn_w", "gn_b", "xq_b", "xk_b", "ln1_g", "ln1_b", "ln2_g", "ln2_b", "subln_w", "decay", "log_alpha", "xv_b"]


def constants(S, C):
    f = np.float32
    gam = (f(1.0) - np.exp(np.linspace(math.log(1 / 32), math.log(1 / 512), 8, dtype=f))).astype(np.float64)
    s, t = np.arange(S)[:, None], np.arange(S)[None, :]
    decay = np.stack([np.where(t >= s, g ** np.maximum(t - s, 0), 0.0) for g in gam], 1).astype(f)
    p = np.arange(P)
    headavg = (p[:, None] // 16 == p[None, :] // 16) / 16.0
    mats = np.stack([np.eye(P), headavg, np.maximum(t - 1 - s, 0), (t > s) & (s > 0), s < t, np.ones((P, P)),
                     (p[:, None] // 8 == p[None, :] // 8) / 8.0, p[:, None] // 16 == p[None, :] // 16,
                     (p[:, None] // 16 == p[None, :] // 16) & (p[:, None] < p[None, :])],
                    1).astype(f)
    picks = np.concatenate([(p[:, None] % 32) // 16 == np.arange(2), (p[:, None] % 32) // 8 == np.arange(4),
                            (p[:, None] % 32) // 4 == np.arange(8), np.broadcast_to(p, (P, P)),
                            p[:, None] + 1 + P * np.arange(16), p[:, None] // 16 == np.arange(8),
                            np.broadcast_to(0.5 ** np.arange(27), (P, 27))],
                           1).astype(f)
    return decay, mats, picks


def kernel(**inputs):
    import concourse.bacc as bacc
    from concourse.bass_utils import run_bass_kernel_spmd

    i = {k: np.asarray(v) for k, v in inputs.items()}
    B, S, C = i["x"].shape
    order = np.array([(a * 16 + 4 * g + j) * 4 + d for g in range(4) for a in range(2) for j in range(4)
                      for d in range(4)])
    decay, mats, picks = constants(S, C)
    gate_pad = np.zeros((C, 15 + P), i["L1_ffn_Wg"].dtype)
    gate_pad[:, 15::16] = i["L1_ffn_Wg"].T
    proj = [i["L0_attn_Wq"].T, i["L0_attn_Wk"].T, i["L0_attn_Wv"].T, i["L0_attn_Wo"].T,
            i["L0_xattn_wq_w"], i["L0_xattn_wk_w"], i["L0_xattn_wv_w"], i["L0_xattn_wo_w"],
            i["L0_ffn_attn_w"].T, i["L1_attn_W_write"], i["L1_attn_W_read"].T,
            i["L1_xattn_Wq"][order].T, i["L1_xattn_Wk"][order].T, i["L1_xattn_Wv"].T, i["L1_xattn_Wp"].T]
    rep = lambda v: np.broadcast_to(np.asarray(v).reshape(1, -1), (P, np.asarray(v).size))
    cols = [i["L0_attn_gn_weight"], i["L0_attn_gn_bias"], i["L0_xattn_wq_b"], i["L0_xattn_wk_b"],
            i["L0_ffn_ln1_g"], i["L0_ffn_ln1_b"], i["L0_ffn_ln2_g"], i["L0_ffn_ln2_b"],
            np.tile(i["L1_xattn_subln_w"], 16), rep(i["L1_attn_decay"])[:, 0], rep(i["L1_attn_log_alpha"])[:, 0],
            i["L0_xattn_wv_b"]]
    chunked = lambda w: w.reshape(w.shape[0], C, -1, P).transpose(3, 0, 2, 1)
    data = {
        "x_tok": i["x"].transpose(1, 0, 2), "x_T": i["x"].transpose(2, 0, 1),
        "ctx_T": i["ctx_1024"].transpose(2, 0, 1), "mask": i["mask_Bx1xSxS2_ff1"][:, 0].transpose(1, 0, 2),
        "proj": np.stack(proj, 1), "cols": np.stack(cols, 1),
        "rows": np.stack([rep(i["L0_xattn_wo_b"]), rep(i["L1_xattn_bp"])], 1),
        "gates": np.stack([i["L0_ffn_gate_w"].T, i["L1_ffn_Wg"].T], 1),
        "lams": np.stack([rep(i["L1_xattn_" + n]) for n in ("lq1", "lk1", "lq2", "lk2")], 1),
        "gate_T": i["L0_ffn_gate_proj"].transpose(2, 0, 1), "up_T": i["L0_ffn_up_proj"].transpose(2, 0, 1),
        "down_T": chunked(i["L0_ffn_down_proj"]),
        "w1_T": i["L1_ffn_W1"].transpose(2, 0, 1), "w3_T": i["L1_ffn_W3"].transpose(2, 0, 1),
        "w2_T": chunked(i["L1_ffn_W2"]),
        "gate_pad": gate_pad, "decay": decay, "mats": mats, "picks": picks,
    }
    nc = bacc.Bacc("TRN2", target_bir_lowering=False, num_devices=1)
    arrays, D = {}, {}
    for name, a in data.items():
        a = np.ascontiguousarray(a)
        arrays[name] = a
        D[name] = nc.dram_tensor(name, a.shape, mybir.dt.from_np(a.dtype), kind="ExternalInput").ap()
    out = nc.dram_tensor("out", (S, B, C), F32, kind="ExternalOutput").ap()
    build(nc, D, out)
    r = run_bass_kernel_spmd(nc, [arrays], core_ids=[0])
    return np.ascontiguousarray(r.results[0]["out"].transpose(1, 0, 2))
```
